# Optimizing a Trainium2 kernel written in Bass

```python
import numpy as np
import jax
import jax.numpy as jnp

def _softmax(x, axis=-1):
    return jax.nn.softmax(x, axis=axis)

def _gelu(x):
    return jax.nn.gelu(x, approximate=True)

def _silu(x):
    return jax.nn.silu(x)

def _sigmoid(x):
    return jax.nn.sigmoid(x)

def _layernorm(x, axis=-1, eps=1e-05):
    m = jnp.mean(x, axis=axis, keepdims=True)
    v = jnp.var(x, axis=axis, keepdims=True)
    return (x - m) / jnp.sqrt(v + eps)

def _scatter_add(tgt, idx, src, axis=0):
    return tgt.at[idx].add(src)

def _segment_sum(src, seg, n):
    return jax.ops.segment_sum(src, seg, n)
kernel_name = 'mk_flamingo_gated_d1_seqx_r4_cf932b'

def setup_inputs(seed: int=0):
    np.random.seed(seed)
    _w = jnp.asarray

    def _rec_inputs():
        import jax
        import jax.numpy as jnp
        _rk = jax.random.key(seed)
        x = -0.0003929 + 0.9999 * jax.random.normal(jax.random.fold_in(_rk, 1), (4, 512, 256), jnp.float32)
        _lenS = 512 - jax.random.randint(jax.random.fold_in(_rk, 7), (4,), 0, max(1, 512 // 4) + 1, jnp.int32)
        _lenS2 = 512 - jax.random.randint(jax.random.fold_in(_rk, 8), (4,), 0, max(1, 512 // 4) + 1, jnp.int32)
        _ctx_1024P = jax.random.normal(jax.random.fold_in(_rk, 11), (4, 16, 256), jnp.float32)
        _ctx_1024c = jax.random.dirichlet(jax.random.fold_in(_rk, 511), 0.3 * jnp.ones((16,), jnp.float32), (4, 512))
        _ctx_1024t = jnp.einsum('bsk,bkd->bsd', _ctx_1024c, _ctx_1024P)
        _ctx_1024t = _ctx_1024t * jax.lax.rsqrt(jnp.mean(jnp.square(_ctx_1024t)) + 1e-12) * 0.953939
        ctx_1024 = 2.81802e-05 + 1.00001 * (_ctx_1024t + 0.3 * jax.random.normal(jax.random.fold_in(_rk, 611), (4, 512, 256), jnp.float32))
        _g = jax.random.normal(jax.random.fold_in(_rk, 9001), (2, 1), jnp.float32)
        _g = jnp.sign(_g) * jnp.maximum(jnp.abs(_g), 1.0) + (_g == 0) * 1.0
        g_xattn = _g[0]
        g_ffn = _g[1]
        return (x, ctx_1024, g_xattn, g_ffn)
    x, ctx_1024, g_xattn, g_ffn = _rec_inputs()

    def _L0_xattn_setup():
        import jax, jax.numpy as jnp
        import numpy as np
        D_MODEL = 256
        NUM_HEADS = 16
        HEAD_DIM = D_MODEL // NUM_HEADS
        FEATURE_DIM = 64
        EPS = 1e-08
        key = jax.random.key(seed)
        ks = jax.random.split(key, 16)
        B, S = (4, 1024)
        s = 1.0 / np.sqrt(D_MODEL)
        sf = 1.0 / np.sqrt(HEAD_DIM)
        return {'query': jax.random.normal(ks[0], (B, S, D_MODEL), jnp.float32), 'key': jax.random.normal(ks[1], (B, S, D_MODEL), jnp.float32), 'value': jax.random.normal(ks[2], (B, S, D_MODEL), jnp.float32), 'Wq': jax.random.normal(ks[3], (D_MODEL, D_MODEL), jnp.float32) * s, 'bq': jnp.zeros((D_MODEL,), jnp.float32), 'Wk': jax.random.normal(ks[4], (D_MODEL, D_MODEL), jnp.float32) * s, 'bk': jnp.zeros((D_MODEL,), jnp.float32), 'Wv': jax.random.normal(ks[5], (D_MODEL, D_MODEL), jnp.float32) * s, 'bv': jnp.zeros((D_MODEL,), jnp.float32), 'Wf': jax.random.normal(ks[6], (HEAD_DIM, FEATURE_DIM), jnp.float32) * sf, 'bf': jnp.zeros((FEATURE_DIM,), jnp.float32), 'Wo': jax.random.normal(ks[7], (D_MODEL, D_MODEL), jnp.float32) * s, 'bo': jnp.zeros((D_MODEL,), jnp.float32)}
    _L0_xattn_all = _L0_xattn_setup()
    _L0_xattn_in = {k: v for k, v in _L0_xattn_all.items() if k in ('Wq', 'bq', 'Wk', 'bk', 'Wv', 'bv', 'Wf', 'bf', 'Wo', 'bo')}
    del _L0_xattn_all

    def _L0_ffn_setup():
        import jax, jax.numpy as jnp
        import numpy as np
        EPS = 1e-05

        def _ln(x, g, b):
            mu = jnp.mean(x, axis=-1, keepdims=True)
            var = jnp.mean(jnp.square(x - mu), axis=-1, keepdims=True)
            return (x - mu) * jax.lax.rsqrt(var + EPS) * g + b

        def _forward(x, index_b, index_t, sw1, sb1, sw2, sb2, sw3, sb3, s_ln_g, s_ln_b, sg_w, sg_b, eg_w, eg_b, exp_bias, ew1, eb1, ew2, eb2, ew3, eb3, sel_ln_g, sel_ln_b):
            x1 = jnp.einsum('btd,hd->bth', x, sw1) + sb1
            x2 = jnp.einsum('btd,hd->bth', x, sw2) + sb2
            sh = _ln(jax.nn.silu(x1) * x2, s_ln_g, s_ln_b)
            shared_out = jnp.einsum('bth,dh->btd', sh, sw3) + sb3
            x_moe = x[index_b, index_t]
            shared_scores = jax.nn.sigmoid(x_moe @ sg_w.T + sg_b)
            expert_scores = jax.nn.sigmoid(x_moe @ eg_w.T + eg_b)
            top1_idx = jnp.argmax(expert_scores + exp_bias, axis=-1)
            top1_score = jnp.take_along_axis(expert_scores, top1_idx[:, None], axis=-1)
            weights = jax.nn.softmax(jnp.concatenate([shared_scores, top1_score], axis=-1), axis=-1)
            shared_w, expert_w = (weights[:, 0], weights[:, 1])
            shared_moe_out = shared_out[index_b, index_t] * shared_w[:, None]
            h1 = jnp.einsum('md,ehd->meh', x_moe, ew1) + eb1
            h2 = jnp.einsum('md,ehd->meh', x_moe, ew2) + eb2
            z = _ln(jax.nn.silu(h1) * h2, sel_ln_g, sel_ln_b)
            out_all = jnp.einsum('meh,edh->med', z, ew3) + eb3
            expert_out = jnp.take_along_axis(out_all, top1_idx[:, None, None], axis=1)[:, 0]
            expert_moe_out = expert_out * expert_w[:, None]
            final_out = shared_out.at[index_b, index_t].set(shared_moe_out + expert_moe_out)
            return final_out
        B, T, D, E, H, M = (2, 512, 256, 8, 128, 512)
        key = jax.random.key(seed)
        ks = jax.random.split(key, 24)
        s = 0.02
        inp = {}
        inp['x'] = jax.random.normal(ks[0], (B, T, D), jnp.float32)
        flat = jnp.arange(M, dtype=jnp.int32) * 2
        inp['index_b'] = flat // T
        inp['index_t'] = flat % T
        inp['sw1'] = jax.random.normal(ks[1], (H, D), jnp.float32) * s
        inp['sb1'] = jnp.zeros((H,), jnp.float32)
        inp['sw2'] = jax.random.normal(ks[2], (H, D), jnp.float32) * s
        inp['sb2'] = jnp.zeros((H,), jnp.float32)
        inp['sw3'] = jax.random.normal(ks[3], (D, H), jnp.float32) * s
        inp['sb3'] = jnp.zeros((D,), jnp.float32)
        inp['s_ln_g'] = jnp.ones((H,), jnp.float32)
        inp['s_ln_b'] = jnp.zeros((H,), jnp.float32)
        inp['sg_w'] = jax.random.normal(ks[4], (1, D), jnp.float32) * s
        inp['sg_b'] = jnp.zeros((1,), jnp.float32)
        inp['eg_w'] = jax.random.normal(ks[5], (E, D), jnp.float32) * s
        inp['eg_b'] = jnp.zeros((E,), jnp.float32)
        inp['exp_bias'] = jnp.zeros((E,), jnp.float32)
        inp['ew1'] = jax.random.normal(ks[6], (E, H, D), jnp.float32) * s
        inp['eb1'] = jnp.zeros((E, H), jnp.float32)
        inp['ew2'] = jax.random.normal(ks[7], (E, H, D), jnp.float32) * s
        inp['eb2'] = jnp.zeros((E, H), jnp.float32)
        inp['ew3'] = jax.random.normal(ks[8], (E, D, H), jnp.float32) * s
        inp['eb3'] = jnp.zeros((E, D), jnp.float32)
        inp['sel_ln_g'] = jnp.ones((H,), jnp.float32)
        inp['sel_ln_b'] = jnp.zeros((H,), jnp.float32)
        return inp
    _L0_ffn_all = _L0_ffn_setup()
    _L0_ffn_in = {k: v for k, v in _L0_ffn_all.items() if k in ('index_b', 'index_t', 'sw1', 'sb1', 'sw2', 'sb2', 'sw3', 'sb3', 's_ln_g', 's_ln_b', 'sg_w', 'sg_b', 'eg_w', 'eg_b', 'exp_bias', 'ew1', 'eb1', 'ew2', 'eb2', 'ew3', 'eb3', 'sel_ln_g', 'sel_ln_b')}
    del _L0_ffn_all
    return {'x': x, 'ctx_1024': ctx_1024, 'g_xattn': g_xattn, 'g_ffn': g_ffn, 'L0_xattn_Wq': _L0_xattn_in['Wq'], 'L0_xattn_bq': _L0_xattn_in['bq'], 'L0_xattn_Wk': _L0_xattn_in['Wk'], 'L0_xattn_bk': _L0_xattn_in['bk'], 'L0_xattn_Wv': _L0_xattn_in['Wv'], 'L0_xattn_bv': _L0_xattn_in['bv'], 'L0_xattn_Wf': _L0_xattn_in['Wf'], 'L0_xattn_bf': _L0_xattn_in['bf'], 'L0_xattn_Wo': _L0_xattn_in['Wo'], 'L0_xattn_bo': _L0_xattn_in['bo'], 'L0_ffn_index_b': _L0_ffn_in['index_b'], 'L0_ffn_index_t': _L0_ffn_in['index_t'], 'L0_ffn_sw1': _L0_ffn_in['sw1'], 'L0_ffn_sb1': _L0_ffn_in['sb1'], 'L0_ffn_sw2': _L0_ffn_in['sw2'], 'L0_ffn_sb2': _L0_ffn_in['sb2'], 'L0_ffn_sw3': _L0_ffn_in['sw3'], 'L0_ffn_sb3': _L0_ffn_in['sb3'], 'L0_ffn_s_ln_g': _L0_ffn_in['s_ln_g'], 'L0_ffn_s_ln_b': _L0_ffn_in['s_ln_b'], 'L0_ffn_sg_w': _L0_ffn_in['sg_w'], 'L0_ffn_sg_b': _L0_ffn_in['sg_b'], 'L0_ffn_eg_w': _L0_ffn_in['eg_w'], 'L0_ffn_eg_b': _L0_ffn_in['eg_b'], 'L0_ffn_exp_bias': _L0_ffn_in['exp_bias'], 'L0_ffn_ew1': _L0_ffn_in['ew1'], 'L0_ffn_eb1': _L0_ffn_in['eb1'], 'L0_ffn_ew2': _L0_ffn_in['ew2'], 'L0_ffn_eb2': _L0_ffn_in['eb2'], 'L0_ffn_ew3': _L0_ffn_in['ew3'], 'L0_ffn_eb3': _L0_ffn_in['eb3'], 'L0_ffn_sel_ln_g': _L0_ffn_in['sel_ln_g'], 'L0_ffn_sel_ln_b': _L0_ffn_in['sel_ln_b']}

def reference(x, ctx_1024, g_xattn, g_ffn, L0_xattn_Wq, L0_xattn_bq, L0_xattn_Wk, L0_xattn_bk, L0_xattn_Wv, L0_xattn_bv, L0_xattn_Wf, L0_xattn_bf, L0_xattn_Wo, L0_xattn_bo, L0_ffn_index_b, L0_ffn_index_t, L0_ffn_sw1, L0_ffn_sb1, L0_ffn_sw2, L0_ffn_sb2, L0_ffn_sw3, L0_ffn_sb3, L0_ffn_s_ln_g, L0_ffn_s_ln_b, L0_ffn_sg_w, L0_ffn_sg_b, L0_ffn_eg_w, L0_ffn_eg_b, L0_ffn_exp_bias, L0_ffn_ew1, L0_ffn_eb1, L0_ffn_ew2, L0_ffn_eb2, L0_ffn_ew3, L0_ffn_eb3, L0_ffn_sel_ln_g, L0_ffn_sel_ln_b):
    import jax
    import jax.numpy as jnp

    def _L0_xattn_ref(query, key, value, Wq, bq, Wk, bk, Wv, bv, Wf, bf, Wo, bo):
        import jax, jax.numpy as jnp
        import numpy as np
        D_MODEL = 256
        NUM_HEADS = 16
        HEAD_DIM = D_MODEL // NUM_HEADS
        FEATURE_DIM = 64
        EPS = 1e-08
        B, S, D = query.shape
        H, hd = (NUM_HEADS, HEAD_DIM)
        q = (query @ Wq + bq).reshape(B, S, H, hd)
        k = (key @ Wk + bk).reshape(B, S, H, hd)
        v = (value @ Wv + bv).reshape(B, S, H, hd)
        qf = jax.nn.relu(q @ Wf + bf)
        kf = jax.nn.relu(k @ Wf + bf)
        kv = jnp.einsum('bshf,bshd->bhfd', kf, v)
        out = jnp.einsum('bshf,bhfd->bshd', qf, kv)
        k_sum = jnp.sum(kf, axis=1)
        q_k_sum = jnp.einsum('bshf,bhf->bsh', qf, k_sum)
        out = out / (q_k_sum[..., None] + EPS)
        out = out.reshape(B, S, D)
        return out @ Wo + bo

    def _L0_ffn_ref(x, index_b, index_t, sw1, sb1, sw2, sb2, sw3, sb3, s_ln_g, s_ln_b, sg_w, sg_b, eg_w, eg_b, exp_bias, ew1, eb1, ew2, eb2, ew3, eb3, sel_ln_g, sel_ln_b):
        import jax, jax.numpy as jnp
        import numpy as np
        EPS = 1e-05

        def _ln(x, g, b):
            mu = jnp.mean(x, axis=-1, keepdims=True)
            var = jnp.mean(jnp.square(x - mu), axis=-1, keepdims=True)
            return (x - mu) * jax.lax.rsqrt(var + EPS) * g + b

        def _forward(x, index_b, index_t, sw1, sb1, sw2, sb2, sw3, sb3, s_ln_g, s_ln_b, sg_w, sg_b, eg_w, eg_b, exp_bias, ew1, eb1, ew2, eb2, ew3, eb3, sel_ln_g, sel_ln_b):
            x1 = jnp.einsum('btd,hd->bth', x, sw1) + sb1
            x2 = jnp.einsum('btd,hd->bth', x, sw2) + sb2
            sh = _ln(jax.nn.silu(x1) * x2, s_ln_g, s_ln_b)
            shared_out = jnp.einsum('bth,dh->btd', sh, sw3) + sb3
            x_moe = x[index_b, index_t]
            shared_scores = jax.nn.sigmoid(x_moe @ sg_w.T + sg_b)
            expert_scores = jax.nn.sigmoid(x_moe @ eg_w.T + eg_b)
            top1_idx = jnp.argmax(expert_scores + exp_bias, axis=-1)
            top1_score = jnp.take_along_axis(expert_scores, top1_idx[:, None], axis=-1)
            weights = jax.nn.softmax(jnp.concatenate([shared_scores, top1_score], axis=-1), axis=-1)
            shared_w, expert_w = (weights[:, 0], weights[:, 1])
            shared_moe_out = shared_out[index_b, index_t] * shared_w[:, None]
            h1 = jnp.einsum('md,ehd->meh', x_moe, ew1) + eb1
            h2 = jnp.einsum('md,ehd->meh', x_moe, ew2) + eb2
            z = _ln(jax.nn.silu(h1) * h2, sel_ln_g, sel_ln_b)
            out_all = jnp.einsum('meh,edh->med', z, ew3) + eb3
            expert_out = jnp.take_along_axis(out_all, top1_idx[:, None, None], axis=1)[:, 0]
            expert_moe_out = expert_out * expert_w[:, None]
            final_out = shared_out.at[index_b, index_t].set(shared_moe_out + expert_moe_out)
            return final_out
        return _forward(x, index_b, index_t, sw1, sb1, sw2, sb2, sw3, sb3, s_ln_g, s_ln_b, sg_w, sg_b, eg_w, eg_b, exp_bias, ew1, eb1, ew2, eb2, ew3, eb3, sel_ln_g, sel_ln_b)
    x = x + jnp.tanh(g_xattn[0]) * _L0_xattn_ref(_layernorm(x, axis=-1), ctx_1024, ctx_1024, L0_xattn_Wq, L0_xattn_bq, L0_xattn_Wk, L0_xattn_bk, L0_xattn_Wv, L0_xattn_bv, L0_xattn_Wf, L0_xattn_bf, L0_xattn_Wo, L0_xattn_bo)
    x = x + jnp.tanh(g_ffn[0]) * _L0_ffn_ref(_layernorm(x, axis=-1), L0_ffn_index_b, L0_ffn_index_t, L0_ffn_sw1, L0_ffn_sb1, L0_ffn_sw2, L0_ffn_sb2, L0_ffn_sw3, L0_ffn_sb3, L0_ffn_s_ln_g, L0_ffn_s_ln_b, L0_ffn_sg_w, L0_ffn_sg_b, L0_ffn_eg_w, L0_ffn_eg_b, L0_ffn_exp_bias, L0_ffn_ew1, L0_ffn_eb1, L0_ffn_ew2, L0_ffn_eb2, L0_ffn_ew3, L0_ffn_eb3, L0_ffn_sel_ln_g, L0_ffn_sel_ln_b)
    return x

_drawn_inputs = setup_inputs


def setup_inputs(seed=0):
    import zlib

    import numpy as np

    out = dict(_drawn_inputs(seed))
    spreads = {'L0_xattn_bq': (0.0, 0.8),
     'L0_xattn_bk': (0.0, 0.8),
     'L0_xattn_bv': (0.0, 0.1),
     'L0_xattn_bf': (0.0, 0.8),
     'L0_xattn_bo': (0.0, 0.1),
     'L0_ffn_sb1': (0.0, 0.1),
     'L0_ffn_sb2': (0.0, 0.1),
     'L0_ffn_sb3': (0.0, 0.1),
     'L0_ffn_s_ln_g': (1.0, 0.2),
     'L0_ffn_s_ln_b': (0.0, 0.429),
     'L0_ffn_eg_b': (0.0, 0.375),
     'L0_ffn_exp_bias': (0.0, 0.1),
     'L0_ffn_eb1': (0.0, 0.453),
     'L0_ffn_eb2': (0.0, 0.468),
     'L0_ffn_eb3': (0.0, 0.362),
     'L0_ffn_sel_ln_g': (1.0, 0.6),
     'L0_ffn_sel_ln_b': (0.0, 0.8)}
    factors = {'L0_ffn_sg_w': 8.0}
    for name, (base, spread) in spreads.items():
        noise = np.random.default_rng([zlib.crc32(name.encode()), seed]).standard_normal(out[name].shape)
        drawn = base * np.exp(spread * noise) if base else spread * noise
        out[name] = jnp.asarray(drawn.astype(out[name].dtype))
    for name, factor in factors.items():
        out[name] = (out[name] * factor).astype(out[name].dtype)
    return out
```

```python
from contextlib import ExitStack

import concourse.bass as bass
from concourse import mybir

P = 128
F32 = mybir.dt.float32
BF16 = mybir.dt.bfloat16
I32 = mybir.dt.int32
U32 = mybir.dt.uint32
ALU = mybir.AluOpType
ACT = mybir.ActivationFunctionType
AX_X = mybir.AxisListType.X
LN_EPS = 1e-5
ATT_EPS = 1e-8


def flamingo_block(nc, x, ctx_t, w_q, w_k, w_v, w_o, w_f_diag, rows, cols, sw12, sw3, w_gate, ew12, ew3,
                   eb12, eb3, index, ident, out):
    NB, S, D = 4, 512, x.shape[1]
    N = NB * S
    T = S // P
    KD = D // P
    HD, FD = 16, w_f_diag.shape[1] // 8
    PAIRS = D // (2 * HD)
    PG = PAIRS // KD
    H = sw3.shape[0]
    E = ew3.shape[1]
    M = index.shape[0] * index.shape[2]
    MT = M // P
    assert 2 * FD == P and H == P and PG == 4 and T == 4 and MT == 4 and KD == 2

    R_BV, R_BF, R_BO = 0, D, D + 8 * FD
    R_SB12 = R_BO + D
    R_SB3 = R_SB12 + 2 * H
    R_GB = R_SB3 + D
    R_XB = R_GB + E + 1
    R_GX = R_XB + E
    R_GF = R_GX + 1
    C_BQ, C_BK, C_BF, C_SG, C_SB, C_EG, C_EB = 0, 2, 4, 5, 6, 7, 8

    scratch_x1 = nc.dram_tensor("scratch_x1", (N, D), F32).ap()
    scratch_sh = nc.dram_tensor("scratch_sh", (N, D), F32).ap()

    def by_tile(a):
        return a.rearrange("(g p) d -> p g d", p=P)

    with ExitStack() as ctx:
        def sb(name, shape, dt=F32):
            return ctx.enter_context(nc.sbuf_tensor(name, shape, dt))

        def sem(name):
            return ctx.enter_context(nc.semaphore(name))

        wq_sb, wk_sb, wv_sb, wo_sb = (sb(n, [P, KD, D]) for n in ("wq_sb", "wk_sb", "wv_sb", "wo_sb"))
        wf_sb = sb("wf_sb", [P, 8 * FD])
        rows_sb = sb("rows_sb", [P, rows.shape[1]])
        cols_sb = sb("cols_sb", [P, cols.shape[1]])
        sw12_sb = sb("sw12_sb", [P, KD, 2 * H])
        sw3_sb = sb("sw3_sb", [P, D])
        wg_sb = sb("wg_sb", [P, KD, E + 1])
        ew12_sb = sb("ew12_sb", [P, E, KD, 2 * H])
        ew3_sb = sb("ew3_sb", [P, E, D])
        eb12_sb = sb("eb12_sb", [E, 2 * H])
        eb3_sb = sb("eb3_sb", [E, D])
        ident_sb = sb("ident_sb", [P, P])
        ident_bf = sb("ident_bf", [P, P], BF16)
        ones_sb = sb("ones_sb", [P, 2 * HD])
        neg_half = sb("neg_half", [P, 16])
        tanh_g = sb("tanh_g", [P, 2])
        tbo = sb("tbo", [P, D])
        xs = sb("xs", [P, NB * T, D])
        x1 = sb("x1", [P, NB * T, D])
        ctx_sb = sb("ctx_sb", [P, KD, S])
        kT = sb("kT", [P, KD, S])
        vv = sb("vv", [P, T, D])
        x_cur = sb("x_cur", [P, T, D])
        nm_cur = sb("nm_cur", [P, T])
        rs_cur = sb("rs_cur", [P, T])
        xn = sb("xn", [P, T, D])
        xnT = sb("xnT", [P, KD, S])
        qT = sb("qT", [P, KD, S])
        kf = sb("kf", [P, T, PAIRS * P])
        kf_sum = sb("kf_sum", [P, PAIRS * P])
        qf = sb("qf", [P, PAIRS, S])
        kvs = sb("kvs", [P, 2 * KD, P])
        kvd = sb("kvd", [P, 2 * KD, PG, 2 * HD])
        rden = sb("rden", [P, S])
        deps = sb("deps", [P, S])
        aT = sb("aT", [P, KD, S])
        st1 = sb("st1", [P, NB * T, 6])
        mv1 = sb("mv1", [P, NB * T, 2])
        ve1 = sb("ve1", [P, NB * T])
        nm1 = sb("nm1", [P, NB * T])
        st2 = sb("st2", [P, T, 6])
        mv2 = sb("mv2", [P, T, 2])
        ve2 = sb("ve2", [P, NB * T])
        nm2 = sb("nm2", [P, NB * T])
        xn2, xn2T = xn, xnT
        hb = sb("hb", [P, T, 2 * H])
        sg = sb("sg", [P, T, H])
        hu = sb("hu", [P, T, H])
        hz = sb("hz", [P, T, H])
        st3 = sb("st3", [P, T, 6])
        mv3 = sb("mv3", [P, T, 2])
        ve3 = sb("ve3", [P, T])
        nm3 = sb("nm3", [P, T])
        rs3 = sb("rs3", [P, T])
        zn = sb("zn", [P, T, H])
        zT = sb("zT", [P, S])
        sh = sb("sh", [P, T, D])
        yo = sb("yo", [P, T, D])
        idx_i = sb("idx_i", [P, 2, MT], I32)
        idf = sb("idf", [P, 8, MT])
        gidx = sb("gidx", [P, MT], U32)
        sidx = sb("sidx", [P, MT], U32)
        xg, shg, fin, fin2 = (qf[:, 2 * n:2 * n + 2, :].rearrange("p a n -> p (a n)").rearrange("p (t d) -> p t d", t=MT)
                              for n in range(4))
        stg = sb("stg", [P, MT, 6])
        mvg = sb("mvg", [P, MT, 2])
        veg = sb("veg", [P, MT])
        nmg = sb("nmg", [P, MT])
        rsg = sb("rsg", [P, MT])
        xgn = sb("xgn", [P, MT, D])
        xgT = sb("xgT", [P, KD, M])
        lg = sb("lg", [P, MT, E + 1])
        sc = sb("sc", [P, MT, E + 1])
        sx = sb("sx", [P, MT, E])
        rank_w = sb("rank_w", [P, MT, E])
        eq = sb("eq", [P, MT, E])
        mx = sb("mx", [P, MT])
        m2 = sb("m2", [P, MT])
        oh = sb("oh", [P, MT, E])
        mask, ohb = (xs[:, 8 * n:8 * n + 8, :].bitcast(BF16).rearrange("p a n -> p (a n)")
                     .rearrange("p (t e q) -> p t e q", t=MT, e=E) for n in range(2))
        top = sb("top", [P, MT])
        dif = sb("dif", [P, MT])
        swt = sb("swt", [P, 2, MT])
        cw = sb("cw", [P, 2, MT])
        ohT = sb("ohT", [E, MT, P])
        xe = kf[:].rearrange("p t n -> p (t n)").rearrange("p (i e k n) -> p i e k n", i=2, e=E, k=KD)
        sgm = sb("sgm", [P, 2, H])
        hum = sb("hum", [P, 2, H])
        hzm = sb("hzm", [P, 2, H])
        stm = sb("stm", [P, MT, 6])
        mvm = sb("mvm", [P, MT, 2])
        vem = sb("vem", [P, MT])
        nmm = sb("nmm", [P, MT])
        rsm = sb("rsm", [P, MT])
        znm = sb("znm", [P, 2, H])
        zTm = sb("zTm", [P, 2, P])
        ze = sb("ze", [P, 2, E, P])

        bank = [ctx.enter_context(nc.psum_tensor(f"bank{i}", [P, 512], F32)) for i in range(8)]

        def halves(b):
            return b[:].rearrange("p (t d) -> p t d", t=2)

        def quarters(b):
            return b[:].rearrange("p (t d) -> p t d", t=4)

        in_wk, in_ctx, in_wv, in_x0, in_x, in_const, in_wq, in_wf, in_wo, in_ffn, in_moe, in_idx = (
            sem(n) for n in ("in_wk", "in_ctx", "in_wv", "in_x0", "in_x", "in_const", "in_wq", "in_wf", "in_wo",
                             "in_ffn", "in_moe", "in_idx"))
        x1_stored, sh_stored, out_stored, xg_in, shg_in, scattered = (
            sem(n) for n in ("x1_stored", "sh_stored", "out_stored", "xg_in", "shg_in", "scattered"))
        consts_ready, tanh_ready, tbo_ready = sem("consts_ready"), sem("tanh_ready"), sem("tbo_ready")
        st1_ready, mv1_ready, ve1_ready = (sem(n) for n in ("st1_ready", "mv1_ready", "ve1_ready"))
        x_cur_in, cur_ready, held, pool_held = sem("x_cur_in"), sem("cur_ready"), sem("held"), sem("pool_held")
        pe_k, pe_v, pe_xt, pe_q, pe_kf, pe_qf, pe_kv, pe_kvt, pe_nd, pe_wo = (
            sem(n) for n in ("pe_k", "pe_v", "pe_xt", "pe_q", "pe_kf", "pe_qf", "pe_kv", "pe_kvt", "pe_nd", "pe_wo"))
        (xn_ready, xb_ready, kT_ready, v_ready, xnT_ready, qT_ready, kf_added, kf_ready, kfs_part, kfs_ready, qf_even,
         qf_odd, kvs_ready, kvd_zero, kvd_ready, den_eps, rden_ready, aT_ready, x1_ready) = (
            sem(n) for n in ("xn_ready", "xb_ready", "kT_ready", "v_ready", "xnT_ready", "qT_ready", "kf_added",
                             "kf_ready", "kfs_part", "kfs_ready", "qf_even", "qf_odd", "kvs_ready", "kvd_zero", "kvd_ready",
                             "den_eps", "rden_ready", "aT_ready", "x1_ready"))
        st2_ready, mv2_ready, ve2_ready = (sem(n) for n in ("st2_ready", "mv2_ready", "ve2_ready"))
        pe_x2t, pe_h, pe_zt, pe_y = (sem(n) for n in ("pe_x2t", "pe_h", "pe_zt", "pe_y"))
        (xn2_ready, xn2T_ready, hb_ready, sg_ready, hu_ready, hz_ready, st3_ready, mv3_ready, ve3_ready, rs3_ready,
         zn_ready, zT_ready, sh_ready, yo_ready) = (
            sem(n) for n in ("xn2_ready", "xn2T_ready", "hb_ready", "sg_ready", "hu_ready", "hz_ready", "st3_ready",
                             "mv3_ready", "ve3_ready", "rs3_ready", "zn_ready", "zT_ready", "sh_ready", "yo_ready"))
        idx_step, idx_ready, dve_g, rsg_ready, xgn_ready, pe_xgt, xgT_ready, pe_gate, gate_added, sc_ready = (
            sem(n) for n in ("idx_step", "idx_ready", "dve_g", "rsg_ready", "xgn_ready", "pe_xgt", "xgT_ready", "pe_gate",
                             "gate_added", "sc_ready"))
        rank_ready, route_step, dif_ready, swt_ready, oh_ready, ohb_ready, pe_oht, ohT_ready, pe_mask, mask_ready = (
            sem(n) for n in ("rank_ready", "route_step", "dif_ready", "swt_ready", "oh_ready", "ohb_ready", "pe_oht",
                             "ohT_ready", "pe_mask", "mask_ready"))
        (xe_ready, pe_hm, sgm_ready, hum_ready, hzm_ready, dve_m, ve_m_ready, rsm_ready, znm_ready, pe_ztm, zTm_ready,
         ze_ready, pe_ym, fin_part, fin_ready) = (
            sem(n) for n in ("xe_ready", "pe_hm", "sgm_ready", "hum_ready", "hzm_ready", "dve_m", "ve_m_ready", "rsm_ready",
                             "znm_ready", "pe_ztm", "zTm_ready", "ze_ready", "pe_ym", "fin_part", "fin_ready"))

        block = ctx.enter_context(nc.Block())

        def row(at, n):
            return rows_sb[:, at:at + n]

        def col(at):
            return cols_sb[:, at:at + 1]

        def bc(a, n, dim=1):
            return a.unsqueeze(1).to_broadcast([P, n, a.shape[1]])

        def bcl(a, n):
            return a.unsqueeze(2).to_broadcast([P, a.shape[1], n])

        @block.sync
        def _(sp):
            sp.dma_start(wk_sb[:], w_k.rearrange("(k p) n -> p k n", p=P)).then_inc(in_wk, 16)
            ctx_v = ctx_t.rearrange("(k p) n -> p k n", p=P)
            sp.dma_start(ctx_sb[:], ctx_v[:, :, 0:S]).then_inc(in_ctx, 16)
            sp.dma_start(cols_sb[:], cols).then_inc(in_const, 16)
            xv = by_tile(x)
            sp.dma_start(xs[:, 0:T, :], xv[:, 0:T, :]).then_inc(in_x0, 16)
            sp.wait_ge(in_x0, 16)
            sp.dma_start(x_cur[:], xs[:, 0:T, :]).then_inc(x_cur_in, 16)
            sp.dma_start(wv_sb[:], w_v.rearrange("(k p) n -> p k n", p=P)).then_inc(in_wv, 16)
            sp.dma_start(rows_sb[:], rows.partition_broadcast(P)).then_inc(in_const, 16)
            sp.dma_start(ident_sb[:], ident).then_inc(in_const, 16)
            sp.dma_start(wq_sb[:], w_q.rearrange("(k p) n -> p k n", p=P)).then_inc(in_wq, 16)
            sp.dma_start(wf_sb[:], w_f_diag).then_inc(in_wf, 16)
            sp.dma_start(xs[:, T:NB * T, :], xv[:, T:NB * T, :]).then_inc(in_x, 16)
            sp.dma_start(wo_sb[:], w_o.rearrange("(k p) n -> p k n", p=P)).then_inc(in_wo, 16)
            sp.wait_ge(in_x, 16)
            with sp.Fori(1, NB) as b:
                sp.wait_ge(xn_ready, 4 * b)
                sp.dma_start(x_cur[:], xs[:, bass.ds(b * T, T), :]).then_inc(x_cur_in, 16)
                sp.wait_ge(pe_v, 2 * b)
                sp.dma_start(ctx_sb[:], ctx_v[:, :, bass.ds(b * S, S)]).then_inc(in_ctx, 16)
            sp.dma_start(idx_i[:], index).then_inc(in_idx, 16)
            sp.dma_start(sw12_sb[:], sw12.rearrange("(k p) n -> p k n", p=P)).then_inc(in_ffn, 16)
            sp.dma_start(sw3_sb[:], sw3).then_inc(in_ffn, 16)
            sp.dma_start(wg_sb[:], w_gate.rearrange("(k p) n -> p k n", p=P)).then_inc(in_moe, 16)
            sp.dma_start(ew12_sb[:], ew12).then_inc(in_moe, 16)
            sp.dma_start(ew3_sb[:], ew3).then_inc(in_moe, 16)
            sp.dma_start(eb12_sb[:], eb12).then_inc(in_moe, 16)
            sp.dma_start(eb3_sb[:], eb3).then_inc(in_moe, 16)
            s1, s2, o = by_tile(scratch_x1), by_tile(scratch_sh), by_tile(out)
            with sp.Fori(0, NB) as b:
                sp.wait_ge(x1_ready, 2 * b + 2)
                sp.dma_start(s1[:, bass.ds(b * T, T), :], x1[:, bass.ds(b * T, T), :]).then_inc(x1_stored, 16)

            def load_x1(b, first):
                if first:
                    sp.wait_ge(xn_ready, 4 * NB)
                else:
                    sp.wait_ge(xn2_ready, 4 * b)
                sp.dma_start(x_cur[:], x1[:, bass.ds(b * T, T), :]).then_inc(x_cur_in, 16)

            def store_ffn(b):
                sp.wait_ge(sh_ready, 2 * b + 2)
                sp.dma_start(s2[:, bass.ds(b * T, T), :], sh[:]).then_inc(sh_stored, 16)
                sp.wait_ge(yo_ready, 2 * b + 2)
                sp.dma_start(o[:, bass.ds(b * T, T), :], yo[:]).then_inc(out_stored, 16)

            load_x1(0, True)
            load_x1(1, False)
            with sp.Fori(2, NB) as b:
                load_x1(b, False)
                store_ffn(b - 2)
            with sp.Fori(NB - 2, NB) as b:
                store_ffn(b)
            sp.wait_ge(scattered, 16 * MT)

        @block.tensor
        def _(pe):
            def proj_t(b, w, src, banks, done):
                for m in range(KD):
                    for k in range(KD):
                        last = pe.matmul(banks[m][:], w[:, k, m * P:(m + 1) * P], src[:, k, :],
                                         start=(k == 0), stop=(k == KD - 1))
                    last.then_inc(done, 1)
                    yield m

            def transposes(src, dst, k, done):
                for t in range(T):
                    last = pe.transpose(dst[:, t * P:(t + 1) * P], src[:, t, k * P:(k + 1) * P], ident_sb[:])
                last.then_inc(done, 1)

            def out_proj(b):
                pe.wait_ge(aT_ready, 2 * b + 2)
                for n, dst in enumerate((bank[7], bank[6])):
                    for t in (2 * n, 2 * n + 1):
                        for k in range(KD):
                            last = pe.matmul(halves(dst)[:, t % 2, :], aT[:, k, t * P:(t + 1) * P], wo_sb[:, k, :],
                                             start=(k == 0), stop=(k == KD - 1))
                    last.then_inc(pe_wo, 1)

            def key_features(j):
                t, c = j // 2, j % 2
                pe.matmul(bank[2 + j % 4][:], kT[:, c, t * P:(t + 1) * P], wf_sb[:], start=True, stop=True)\
                  .then_inc(pe_kf, 1)

            def query_features(b, p):
                if p < 4:
                    pe.wait_ge(kf_added, 8 * b + p + 5)
                elif p % 2 == 0:
                    pe.wait_ge(qf_even, 4 * b + p // 2 - 1)
                else:
                    pe.wait_ge(qf_odd, 4 * b + p // 2 - 1)
                pe.matmul(bank[2 + p % 4][:], wf_sb[:, (p % PG) * P:(p % PG + 1) * P], qT[:, p // PG, :],
                          start=True, stop=True).then_inc(pe_qf, 1)

            def attention(b, first):
                pe.wait_ge(in_ctx, 16 * b + 16)
                if first:
                    pe.wait_ge(in_wk, 16)
                for m in range(KD):
                    if not first:
                        pe.wait_ge(qT_ready, 2 * b - 1 + m)
                    for k in range(KD):
                        last = pe.matmul(bank[m][:], wk_sb[:, k, m * P:(m + 1) * P], ctx_sb[:, k, :],
                                         start=(k == 0), stop=(k == KD - 1))
                    last.then_inc(pe_k, 1)
                if first:
                    pe.wait_ge(in_wv, 16)
                for n in range(2):
                    pe.wait_ge(kT_ready, 2 * b + 1 + n)
                    for t in (2 * n, 2 * n + 1):
                        for k in range(KD):
                            last = pe.matmul(halves(bank[n])[:, t % 2, :], ctx_sb[:, k, t * P:(t + 1) * P],
                                             wv_sb[:, k, :], start=(k == 0), stop=(k == KD - 1))
                    last.then_inc(pe_v, 1)
                if first:
                    pe.wait_ge(in_const, 48)
                pe.wait_ge(xn_ready, 4 * b + 4)
                for k in range(KD):
                    pe.wait_ge(v_ready, 2 * b + 1 + k)
                    transposes(xn, bank[k], k, pe_xt)
                if first:
                    pe.wait_ge(in_wq, 16)
                pe.wait_ge(xnT_ready, 2 * b + 2)
                for m in range(KD):
                    for k in range(KD):
                        last = pe.matmul(bank[m][:], wq_sb[:, k, m * P:(m + 1) * P], xnT[:, k, :],
                                         start=(k == 0), stop=(k == KD - 1))
                    last.then_inc(pe_q, 1)
                if first:
                    pe.wait_ge(in_wf, 16)
                else:
                    out_proj(b - 1)
                for j in range(2 * T):
                    if j >= 4:
                        pe.wait_ge(kf_added, 8 * b + j - 3)
                    elif not first and j % 2 == 0:
                        pe.wait_ge(aT_ready, 2 * b - 1 + j // 2)
                    key_features(j)
                pe.wait_ge(qT_ready, 2 * b + 2)
                query_features(b, 0)
                query_features(b, 1)
                pe.wait_ge(kf_ready, 8 * b + 8)
                pe.wait_ge(v_ready, 2 * b + 2)
                if not first:
                    pe.wait_ge(x1_ready, 2 * b)
                for c in range(KD):
                    for t in range(T):
                        for g in range(PG):
                            p = PG * c + g
                            pe.matmul(quarters(bank[6])[32 * g:32 * g + 32, c, :], vv[:, t, 32 * p:32 * p + 32],
                                      kf[:, t, P * p:P * (p + 1)], start=(t == 0), stop=(t == T - 1))
                query_features(b, 2)
                query_features(b, 3)
                pe.wait_ge(kfs_ready, b + 1)
                for c in range(KD):
                    for g in range(PG):
                        p = PG * c + g
                        last = pe.matmul(quarters(bank[6])[32 * g:32 * g + 32, KD + c, :], ones_sb[:],
                                         kf_sum[:, P * p:P * (p + 1)], start=True, stop=True)
                last.then_inc(pe_kv, 1)
                query_features(b, 4)
                query_features(b, 5)
                pe.wait_ge(kvs_ready, b + 1)
                for n in range(2 * KD):
                    last = pe.transpose(quarters(bank[6])[:, n, :], kvs[:, n, :], ident_sb[:])
                last.then_inc(pe_kvt, 1)
                query_features(b, 6)
                query_features(b, 7)
                pe.wait_ge(kvd_ready, 2 * b + 2)
                for c in range(KD):
                    pe.wait_ge(qf_even, 4 * b + 2 * c + 2)
                    pe.wait_ge(qf_odd, 4 * b + 2 * c + 2)
                    if c == 0:
                        pe.wait_ge(qf_even, 4 * b + 3)
                        pe.wait_ge(qf_odd, 4 * b + 3)
                    for n in range(2):
                        for g in range(PG):
                            last = pe.matmul(bank[2 + 2 * c + n][32 * g:32 * g + 32, :], kvd[:, KD * n + c, g, :],
                                             qf[:, PG * c + g, :], start=True, stop=True)
                    last.then_inc(pe_nd, 1)

            attention(0, True)
            pe.wait_ge(in_wo, 16)
            with pe.Fori(1, NB) as b:
                attention(b, False)
            out_proj(NB - 1)

            def ffn_up(b, first):
                pe.wait_ge(xn2_ready, 4 * b + 4)
                for k in range(KD):
                    if not first:
                        pe.wait_ge(xn2T_ready, 2 * b - 1 + k)
                    transposes(xn2, bank[k], k, pe_x2t)
                pe.wait_ge(xn2T_ready, 2 * b + 2)
                for n in range(2):
                    if not first:
                        pe.wait_ge(hb_ready, 2 * b - 1 + n)
                    for t in (2 * n, 2 * n + 1):
                        for k in range(KD):
                            last = pe.matmul(halves(bank[2 + n])[:, t % 2, :], xn2T[:, k, t * P:(t + 1) * P],
                                             sw12_sb[:, k, :], start=(k == 0), stop=(k == KD - 1))
                    last.then_inc(pe_h, 1)

            def ffn_down(b, first):
                pe.wait_ge(zn_ready, 4 * b + 4)
                if not first:
                    pe.wait_ge(zT_ready, b)
                for t in range(T):
                    last = pe.transpose(bank[4][:, t * P:(t + 1) * P], zn[:, t, :], ident_sb[:])
                last.then_inc(pe_zt, 1)
                pe.wait_ge(zT_ready, b + 1)
                for n in range(2):
                    if first:
                        pe.wait_ge(x1_ready, 2 * NB)
                    else:
                        pe.wait_ge(sh_ready, 2 * b - 1 + n)
                    for t in (2 * n, 2 * n + 1):
                        last = pe.matmul(halves(bank[5 + n])[:, t % 2, :], zT[:, t * P:(t + 1) * P], sw3_sb[:],
                                         start=True, stop=True)
                    last.then_inc(pe_y, 1)

            pe.wait_ge(in_ffn, 32)
            pe.wait_ge(aT_ready, 2 * NB)
            ffn_up(0, True)
            ffn_up(1, False)
            ffn_down(0, True)
            with pe.Fori(2, NB) as b:
                ffn_up(b, False)
                ffn_down(b - 1, False)
            pe.wait_ge(xgn_ready, 1)
            for k in range(KD):
                if k:
                    pe.wait_ge(xgT_ready, k)
                transposes(xgn, bank[7], k, pe_xgt)
            pe.wait_ge(xgT_ready, KD)
            pe.wait_ge(in_moe, 80)
            for t in range(MT):
                for k in range(KD):
                    last = pe.matmul(bank[7][:, t * (E + 1):(t + 1) * (E + 1)], xgT[:, k, t * P:(t + 1) * P],
                                     wg_sb[:, k, :], start=(k == 0), stop=(k == KD - 1))
            last.then_inc(pe_gate, 1)
            ffn_down(NB - 1, False)

            pe.wait_ge(oh_ready, 1)
            for t in range(MT):
                last = pe.transpose(bank[7][0:E, t * P:(t + 1) * P], oh[:, t, :], ident_sb[:])
            last.then_inc(pe_oht, 1)
            for t in range(MT):
                pe.wait_ge(ohb_ready, t + 1)
                if t:
                    pe.wait_ge(mask_ready, 2 * t)
                for e in range(E):
                    last = pe.matmul(quarters(bank[e // 4])[:, e % 4, :], ohb[:, t, e, :], ident_bf[:],
                                     start=True, stop=True)
                    if e % 4 == 3:
                        last.then_inc(pe_mask, 1)
            pe.wait_ge(ohT_ready, 1)

            def expert_up(t):
                pe.wait_ge(xe_ready, t + 1)
                if t >= 2:
                    pe.wait_ge(hzm_ready, t - 1)
                dst = bank[2 + t % 2][:, 0:2 * H]
                for e in range(E):
                    for k in range(KD):
                        pe.matmul(dst, xe[:, t % 2, e, k, :], ew12_sb[:, e, k, :], start=(e + k == 0), stop=False)
                pe.matmul(dst, ohT[:, t, :], eb12_sb[:], start=False, stop=True).then_inc(pe_hm, 1)

            def expert_down(t):
                pe.wait_ge(znm_ready, t + 1)
                if t:
                    pe.wait_ge(zTm_ready, t)
                pe.transpose(bank[4][:, 0:P], znm[:, t % 2, :], ident_sb[:]).then_inc(pe_ztm, 1)
                pe.wait_ge(ze_ready, t + 1)
                if t < 2:
                    pe.wait_ge(sh_ready, 2 * NB)
                else:
                    pe.wait_ge(fin_part, t - 1)
                dst = bank[5 + t % 2][:, 0:D]
                for e in range(E):
                    pe.matmul(dst, ze[:, t % 2, e, :], ew3_sb[:, e, :], start=(e == 0), stop=False)
                pe.matmul(dst, ohT[:, t, :], eb3_sb[:], start=False, stop=True).then_inc(pe_ym, 1)

            expert_up(0)
            for t in range(1, MT):
                expert_up(t)
                expert_down(t - 1)
            expert_down(MT - 1)

        @block.scalar
        def _(act):
            act.wait_ge(in_const, 48)
            act.activation(tanh_g[:], row(R_GX, 2), ACT.Tanh).then_inc(tanh_ready, 1)

            def query_evac(b, p):
                act.wait_ge(pe_qf, 8 * b + p + 1)
                act.activation(qf[:, p, :], bank[2 + p % 4][:], ACT.Relu, bias=col(C_BF)).then_inc(qf_even, 1)

            def attention(b):
                for m in range(KD):
                    act.wait_ge(pe_k, 2 * b + 1 + m)
                    act.activation(kT[:, m, :], bank[m][:], ACT.Identity, bias=col(C_BK + m)).then_inc(kT_ready, 1)
                for k in range(KD):
                    act.wait_ge(pe_xt, 2 * b + 1 + k)
                    act.activation(xnT[:, k, :], bank[k][:], ACT.Copy).then_inc(xnT_ready, 1)
                for m in range(KD):
                    act.wait_ge(pe_q, 2 * b + 1 + m)
                    act.activation(qT[:, m, :], bank[m][:], ACT.Identity, bias=col(C_BQ + m)).then_inc(qT_ready, 1)
                for j in range(2 * T):
                    act.wait_ge(kf_added, 8 * b + j + 1)
                    part = kf[:, j // 2, (j % 2) * 512:(j % 2) * 512 + 512]
                    act.activation(part, part, ACT.Relu).then_inc(kf_ready, 1)
                query_evac(b, 0)
                query_evac(b, 2)
                act.wait_ge(pe_kv, b + 1)
                act.activation(kvs[:], quarters(bank[6]), ACT.Copy).then_inc(kvs_ready, 1)
                query_evac(b, 4)
                query_evac(b, 6)

            with act.Fori(0, NB) as b:
                attention(b)

            def ffn_up(b):
                for k in range(KD):
                    act.wait_ge(pe_x2t, 2 * b + 1 + k)
                    act.activation(xn2T[:, k, :], bank[k][:], ACT.Copy).then_inc(xn2T_ready, 1)
                act.wait_ge(hb_ready, 2 * b + 2)
                act.activation(sg[:], hb[:, :, 0:H], ACT.Sigmoid).then_inc(sg_ready, 1)

            def ffn_down(b):
                act.wait_ge(pe_zt, b + 1)
                act.activation(zT[:], bank[4][:], ACT.Identity, bias=col(C_SB), scale=col(C_SG)).then_inc(zT_ready, 1)

            ffn_up(0)
            with act.Fori(1, NB) as b:
                ffn_up(b)
                ffn_down(b - 1)
            for k in range(KD):
                act.wait_ge(pe_xgt, k + 1)
                act.activation(xgT[:, k, :], bank[7][:], ACT.Copy).then_inc(xgT_ready, 1)
            act.wait_ge(gate_added, 1)
            act.activation(sc[:], lg[:], ACT.Sigmoid).then_inc(sc_ready, 1)
            ffn_down(NB - 1)
            act.wait_ge(dif_ready, 1)
            act.activation(swt[:, 0, :], dif[:], ACT.Sigmoid).then_inc(swt_ready, 1)
            act.activation(swt[:, 1, :], dif[:], ACT.Sigmoid, scale=-1.0).then_inc(swt_ready, 1)
            act.wait_ge(pe_oht, 1)
            act.activation(ohT[:], quarters(bank[7])[0:E], ACT.Copy).then_inc(ohT_ready, 1)
            for t in range(MT):
                for n in range(2):
                    act.wait_ge(pe_mask, 2 * t + n + 1)
                    act.activation(mask[:, t, 4 * n:4 * n + 4, :], quarters(bank[n]), ACT.Copy).then_inc(mask_ready, 1)
            for t in range(MT):
                act.wait_ge(pe_hm, t + 1)
                act.activation(sgm[:, t % 2, :], bank[2 + t % 2][:, 0:H], ACT.Sigmoid).then_inc(sgm_ready, 1)
                act.wait_ge(pe_ztm, t + 1)
                act.activation(zTm[:, t % 2, :], bank[4][:, 0:P], ACT.Identity, bias=col(C_EB), scale=col(C_EG))\
                   .then_inc(zTm_ready, 1)

        @block.vector
        def _(dve):
            def stats(src, st, mv, g0, n, st_sem, mv_sem, st_total, mv_total, own_wait):
                for t in range(n):
                    last = dve.bn_stats(st[:, t, :], src(t))
                last.then_inc(st_sem, 1)
                dve.wait_ge(st_sem, st_total)
                if own_wait:
                    dve.sem_inc(held, 1)
                for t in range(n):
                    last = dve.bn_aggr(mv[:, t, :], st[:, t, :])
                last.then_inc(mv_sem, 1)
                dve.wait_ge(mv_sem, mv_total)

            dve.memset(neg_half[:], -0.5).then_inc(consts_ready, 1)
            dve.memset(ones_sb[:], 1.0).then_inc(consts_ready, 1)
            dve.memset(kvd[:], 0.0).then_inc(kvd_zero, 1)
            for b in range(NB):
                if b == 0:
                    dve.wait_ge(in_x0, 16)
                if b == 1:
                    dve.wait_ge(in_x, 16)
                stats(lambda t: xs[:, T * b + t, :], st1[:, T * b:T * b + T, :], mv1[:, T * b:T * b + T, :], 0, T,
                      st1_ready, mv1_ready, b + 1, b + 1, False)
                dve.tensor_scalar(ve1[:, T * b:T * b + T], mv1[:, T * b:T * b + T, 1], LN_EPS, None, ALU.add)\
                   .then_inc(ve1_ready, 1)
                dve.tensor_scalar(nm1[:, T * b:T * b + T], mv1[:, T * b:T * b + T, 0], -1.0, None, ALU.mult)\
                   .then_inc(ve1_ready, 1)
                if b == 0:
                    dve.wait_ge(in_const, 48)
                    dve.tensor_copy(ident_bf[:], ident_sb[:]).then_inc(consts_ready, 1)
                    dve.wait_ge(tanh_ready, 1)
                    dve.tensor_scalar(tbo[:], row(R_BO, D), tanh_g[:, 0:1], None, ALU.mult).then_inc(tbo_ready, 1)
            dve.wait_ge(kvd_zero, 1)

            def residual(b):
                for n, src in enumerate((bank[7], bank[6])):
                    dve.wait_ge(xb_ready, b + 1)
                    dve.wait_ge(pe_wo, 2 * b + 1 + n)
                    at = bass.ds(b * T + 2 * n, 2)
                    dve.scalar_tensor_tensor(x1[:, at, :], halves(src), tanh_g[:, 0:1], xs[:, at, :], ALU.mult, ALU.add)\
                       .then_inc(x1_ready, 1)
                dve.wait_ge(x1_ready, 2 * b + 2)
                dve.sem_inc(held, 1)
                stats(lambda t: x1[:, b * T + t, :], st2, mv2, 0, T, st2_ready, mv2_ready, b + 1, b + 1, True)
                dve.tensor_scalar(ve2[:, bass.ds(b * T, T)], mv2[:, :, 1], LN_EPS, None, ALU.add).then_inc(ve2_ready, 1)
                dve.tensor_scalar(nm2[:, bass.ds(b * T, T)], mv2[:, :, 0], -1.0, None, ALU.mult).then_inc(ve2_ready, 1)
                dve.wait_ge(ve2_ready, 2 * b + 2)

            def query_evac(b, p):
                dve.wait_ge(pe_qf, 8 * b + p + 1)
                dve.tensor_scalar(qf[:, p, :], bank[2 + p % 4][:], col(C_BF), 0.0, ALU.add, ALU.max)\
                   .then_inc(qf_odd, 1)

            def attention(b, first):
                for n in range(2):
                    dve.wait_ge(pe_v, 2 * b + 1 + n)
                    dve.tensor_tensor(vv[:, 2 * n:2 * n + 2, :], halves(bank[n]), bc(row(R_BV, D), 2), ALU.add)\
                       .then_inc(v_ready, 1)
                if not first:
                    residual(b - 1)
                for j in range(2 * T):
                    dve.wait_ge(pe_kf, 8 * b + j + 1)
                    dve.tensor_tensor(kf[:, j // 2, (j % 2) * 512:(j % 2) * 512 + 512], bank[2 + j % 4][:],
                                      row(R_BF, 8 * FD), ALU.add).then_inc(kf_added, 1)
                for p in (1, 3, 5):
                    query_evac(b, p)
                dve.wait_ge(pe_kvt, b + 1)
                src = bank[6][:].rearrange("p (n g d) -> p (n g) d", n=2 * KD, g=PG)
                dst = kvd[:].rearrange("p n g d -> p (n g) d")
                for a in range(2):
                    dve.tensor_copy(dst[64 * a:64 * a + 64, :, HD * a:HD * a + HD],
                                    src[64 * a:64 * a + 64, :, HD * a:HD * a + HD]).then_inc(kvd_ready, 1)
                query_evac(b, 7)
                for c in range(KD):
                    dve.wait_ge(pe_nd, 2 * b + c + 1)
                    if not first or c:
                        dve.wait_ge(aT_ready, 2 * b + c)
                    dve.tensor_scalar(deps[:], bank[3 + 2 * c][:], ATT_EPS, None, ALU.add).then_inc(den_eps, 1)
                    dve.wait_ge(den_eps, 2 * b + c + 1)
                    dve.reciprocal(rden[:], deps[:]).then_inc(rden_ready, 1)
                    dve.wait_ge(rden_ready, 2 * b + c + 1)
                    dve.tensor_tensor(aT[:, c, :], bank[2 + 2 * c][:], rden[:], ALU.mult).then_inc(aT_ready, 1)

            attention(0, True)
            with dve.Fori(1, NB) as b:
                attention(b, False)
            residual(NB - 1)

            step = [0]

            def link(sem_, ins):
                step[0] += 1
                ins.then_inc(sem_, 1)
                dve.wait_ge(sem_, step[0])

            dve.wait_ge(in_idx, 16)
            for n, size in ((0, NB), (1, S)):
                v, neg = idf[:, n, :], idf[:, 2 + n, :]
                link(idx_step, dve.tensor_copy(v, idx_i[:, n, :]))
                link(idx_step, dve.tensor_scalar(neg, v, 0.0, float(size), ALU.is_lt, ALU.mult))
                link(idx_step, dve.tensor_tensor(v, v, neg, ALU.add))
                link(idx_step, dve.tensor_scalar(neg, v, 0.0, None, ALU.is_ge))
                link(idx_step, dve.scalar_tensor_tensor(idf[:, 4 + n, :], v, float(size - 1), neg, ALU.is_le, ALU.mult))
                link(idx_step, dve.tensor_scalar(v, v, 0.0, float(size - 1), ALU.max, ALU.min))
            link(idx_step, dve.scalar_tensor_tensor(idf[:, 6, :], idf[:, 0, :], float(S), idf[:, 1, :], ALU.mult, ALU.add))
            link(idx_step, dve.tensor_copy(gidx[:], idf[:, 6, :]))
            link(idx_step, dve.tensor_tensor(idf[:, 7, :], idf[:, 4, :], idf[:, 5, :], ALU.mult))
            link(idx_step, dve.tensor_scalar(idf[:, 7, :], idf[:, 7, :], -float(N), float(N), ALU.mult, ALU.add))
            link(idx_step, dve.tensor_tensor(idf[:, 6, :], idf[:, 6, :], idf[:, 7, :], ALU.add))
            dve.tensor_copy(sidx[:], idf[:, 6, :]).then_inc(idx_ready, 1)
            for e in range(E):
                dve.memset(rank_w[:, :, e], float(E - e)).then_inc(rank_ready, 1)

            def ffn_up(b, first):
                for n in range(2):
                    dve.wait_ge(pe_h, 2 * b + 1 + n)
                    dve.tensor_tensor(hb[:, 2 * n:2 * n + 2, :], halves(bank[2 + n]), bc(row(R_SB12, 2 * H), 2), ALU.add)\
                       .then_inc(hb_ready, 1)
                dve.wait_ge(hu_ready, b + 1)
                dve.tensor_tensor(hz[:], hu[:], hb[:, :, H:2 * H], ALU.mult).then_inc(hz_ready, 1)
                dve.wait_ge(hz_ready, b + 1)
                if not first:
                    dve.sem_inc(held, 1)
                stats(lambda t: hz[:, t, :], st3, mv3, 0, T, st3_ready, mv3_ready, b + 1, b + 1, not first)
                dve.tensor_scalar(ve3[:], mv3[:, :, 1], LN_EPS, None, ALU.add).then_inc(ve3_ready, 1)
                dve.tensor_scalar(nm3[:], mv3[:, :, 0], -1.0, None, ALU.mult).then_inc(ve3_ready, 1)
                dve.wait_ge(rs3_ready, b + 1)
                dve.wait_ge(ve3_ready, 2 * b + 2)
                if not first:
                    dve.wait_ge(pe_zt, b)
                for t in range(T):
                    dve.tensor_scalar(zn[:, t, :], hz[:, t, :], nm3[:, t:t + 1], rs3[:, t:t + 1], ALU.add, ALU.mult)\
                       .then_inc(zn_ready, 1)

            def ffn_down(b, first):
                for n in range(2):
                    dve.wait_ge(pe_y, 2 * b + 1 + n)
                    if not first:
                        dve.wait_ge(sh_stored, 16 * b)
                    dve.tensor_tensor(sh[:, 2 * n:2 * n + 2, :], halves(bank[5 + n]), bc(row(R_SB3, D), 2), ALU.add)\
                       .then_inc(sh_ready, 1)
                for n in range(2):
                    dve.wait_ge(sh_ready, 2 * b + 1 + n)
                    if not first:
                        dve.wait_ge(out_stored, 16 * b)
                    dve.scalar_tensor_tensor(yo[:, 2 * n:2 * n + 2, :], sh[:, 2 * n:2 * n + 2, :], tanh_g[:, 1:2],
                                             x1[:, bass.ds(b * T + 2 * n, 2), :], ALU.mult, ALU.add).then_inc(yo_ready, 1)

            ffn_up(0, True)
            ffn_up(1, False)
            ffn_down(0, True)
            with dve.Fori(2, NB) as b:
                ffn_up(b, False)
                ffn_down(b - 1, False)
            step[0] = 0
            dve.wait_ge(xg_in, 16 * MT)
            for t in range(MT):
                last = dve.bn_stats(stg[:, t, :], xg[:, t, :])
            link(dve_g, last)
            for t in range(MT):
                last = dve.bn_aggr(mvg[:, t, :], stg[:, t, :])
            link(dve_g, last)
            link(dve_g, dve.tensor_scalar(veg[:], mvg[:, :, 1], LN_EPS, None, ALU.add))
            link(dve_g, dve.tensor_scalar(nmg[:], mvg[:, :, 0], -1.0, None, ALU.mult))
            dve.wait_ge(rsg_ready, 1)
            for t in range(MT):
                last = dve.tensor_scalar(xgn[:, t, :], xg[:, t, :], nmg[:, t:t + 1], rsg[:, t:t + 1], ALU.add, ALU.mult)
            last.then_inc(xgn_ready, 1)
            dve.wait_ge(pe_gate, 1)
            dve.tensor_tensor(lg[:], bank[7][:, 0:MT * (E + 1)].rearrange("p (t e) -> p t e", t=MT),
                              bc(row(R_GB, E + 1), MT), ALU.add).then_inc(gate_added, 1)
            step[0] = 0
            dve.wait_ge(sc_ready, 1)
            dve.wait_ge(rank_ready, E)
            link(route_step, dve.tensor_tensor(sx[:], sc[:, :, 0:E], bc(row(R_XB, E), MT), ALU.add))
            link(route_step, dve.reduce_max(mx[:], sx[:], AX_X))
            link(route_step, dve.tensor_tensor(eq[:], sx[:], bcl(mx[:], E), ALU.is_equal))
            link(route_step, dve.tensor_tensor(eq[:], eq[:], rank_w[:], ALU.mult))
            link(route_step, dve.reduce_max(m2[:], eq[:], AX_X))
            dve.tensor_tensor(oh[:], eq[:], bcl(m2[:], E), ALU.is_equal).then_inc(oh_ready, 1)
            dve.wait_ge(oh_ready, 1)
            for t in range(MT):
                dve.tensor_copy(ohb[:, t, :, :], bcl(oh[:, t, :], P)).then_inc(ohb_ready, 1)
            link(route_step, dve.tensor_tensor(sx[:], sc[:, :, 0:E], oh[:], ALU.mult))
            link(route_step, dve.reduce_sum(top[:], sx[:], AX_X))
            dve.tensor_tensor(dif[:], top[:], sc[:, :, E], ALU.subtract).then_inc(dif_ready, 1)
            ffn_down(NB - 1, False)
            dve.wait_ge(swt_ready, 2)
            link(route_step, dve.tensor_scalar(cw[:], swt[:], tanh_g[:, 1:2], None, ALU.mult))

            def masked_inputs(t):
                dve.wait_ge(mask_ready, 2 * t + 2)
                if t >= 2:
                    dve.wait_ge(pe_hm, t - 1)
                for k in range(KD):
                    last = dve.tensor_tensor(xe[:, t % 2, :, k, :], bc(xgT[:, k, t * P:(t + 1) * P], E), mask[:, t, :, :],
                                             ALU.mult)
                last.then_inc(xe_ready, 1)

            dve.wait_ge(xgT_ready, KD)
            mstep = [0]

            def mlink(ins):
                mstep[0] += 1
                ins.then_inc(dve_m, 1)
                dve.wait_ge(dve_m, mstep[0])

            def expert_hidden(t):
                i, src = t % 2, bank[2 + t % 2]
                dve.wait_ge(sgm_ready, t + 1)
                mlink(dve.tensor_tensor(hum[:, i, :], src[:, 0:H], sgm[:, i, :], ALU.mult))
                dve.tensor_tensor(hzm[:, i, :], src[:, H:2 * H], hum[:, i, :], ALU.mult).then_inc(hzm_ready, 1)
                dve.wait_ge(hzm_ready, t + 1)
                mlink(dve.bn_stats(stm[:, t, :], hzm[:, i, :]))
                mlink(dve.bn_aggr(mvm[:, t, :], stm[:, t, :]))
                dve.tensor_scalar(vem[:, t:t + 1], mvm[:, t, 1:2], LN_EPS, None, ALU.add).then_inc(ve_m_ready, 1)
                mlink(dve.tensor_scalar(nmm[:, t:t + 1], mvm[:, t, 0:1], -1.0, None, ALU.mult))
                dve.wait_ge(rsm_ready, t + 1)
                if t >= 2:
                    dve.wait_ge(pe_ztm, t - 1)
                dve.tensor_scalar(znm[:, i, :], hzm[:, i, :], nmm[:, t:t + 1], rsm[:, t:t + 1], ALU.add, ALU.mult)\
                   .then_inc(znm_ready, 1)
                dve.wait_ge(zTm_ready, t + 1)
                if t >= 2:
                    dve.wait_ge(pe_ym, t - 1)
                dve.tensor_tensor(ze[:, i, :, :], bc(zTm[:, i, :], E), mask[:, t, :, :], ALU.mult).then_inc(ze_ready, 1)

            def combine(t):
                dve.wait_ge(pe_ym, t + 1)
                dve.scalar_tensor_tensor(fin2[:, t, :], bank[5 + t % 2][:, 0:D], cw[:, 0, t:t + 1], xg[:, t, :],
                                         ALU.mult, ALU.add).then_inc(fin_part, 1)
                dve.wait_ge(fin_part, t + 1)
                if t == 0:
                    dve.wait_ge(shg_in, 16 * MT)
                dve.scalar_tensor_tensor(fin[:, t, :], shg[:, t, :], cw[:, 1, t:t + 1], fin2[:, t, :],
                                         ALU.mult, ALU.add).then_inc(fin_ready, 1)

            masked_inputs(0)
            masked_inputs(1)
            for t in range(MT):
                expert_hidden(t)
                if t + 2 < MT:
                    masked_inputs(t + 2)
                if t:
                    combine(t - 1)
            combine(MT - 1)

        @block.gpsimd
        def _(pool):
            def norm_rows(b, ve, nm, ve_sem, dst, done, loads, free, free_total):
                pool.wait_ge(ve_sem, 2 * b + 2)
                pool.sem_inc(pool_held, 1)
                at = bass.ds(b * T, T)
                pool.tensor_tensor(rs_cur[:], ve[:, at], neg_half[:, 0:T], ALU.pow).then_inc(cur_ready, 1)
                pool.tensor_tensor(nm_cur[:], nm[:, at], ones_sb[:, 0:T], ALU.mult).then_inc(cur_ready, 1)
                pool.wait_ge(x_cur_in, 16 * loads)
                pool.wait_ge(cur_ready, 2 * loads)
                if free is not None:
                    pool.wait_ge(free, free_total)
                pool.sem_inc(pool_held, 1)
                for t in range(T):
                    pool.tensor_scalar(dst[:, t, :], x_cur[:, t, :], nm_cur[:, t:t + 1], rs_cur[:, t:t + 1],
                                       ALU.add, ALU.mult).then_inc(done, 1)
                pool.wait_ge(done, 4 * b + 4)

            def attention(b, first):
                if first:
                    pool.wait_ge(consts_ready, 2)
                norm_rows(b, ve1, nm1, ve1_ready, xn, xn_ready, b + 1, None if first else pe_xt, 2 * b)
                if first:
                    pool.wait_ge(tbo_ready, 1)
                pool.sem_inc(pool_held, 1)
                at = bass.ds(b * T, T)
                pool.tensor_tensor(xs[:, at, :], xs[:, at, :], bc(tbo[:], T), ALU.add).then_inc(xb_ready, 1)
                if not first:
                    pool.wait_ge(pe_kv, b)
                pool.wait_ge(kf_ready, 8 * b + 4)
                pool.tensor_tensor(kf_sum[:], kf[:, 0, :], kf[:, 1, :], ALU.add).then_inc(kfs_part, 1)
                pool.wait_ge(kfs_part, 2 * b + 1)
                pool.wait_ge(kf_ready, 8 * b + 6)
                pool.tensor_tensor(kf_sum[:], kf_sum[:], kf[:, 2, :], ALU.add).then_inc(kfs_part, 1)
                pool.wait_ge(kfs_part, 2 * b + 2)
                pool.wait_ge(kf_ready, 8 * b + 8)
                pool.tensor_tensor(kf_sum[:], kf_sum[:], kf[:, 3, :], ALU.add).then_inc(kfs_ready, 1)

            attention(0, True)
            with pool.Fori(1, NB) as b:
                attention(b, False)

            def ffn(b, first):
                norm_rows(b, ve2, nm2, ve2_ready, xn2, xn2_ready, NB + b + 1,
                          pe_xt if first else pe_x2t, 2 * NB if first else 2 * b)
                pool.wait_ge(sg_ready, b + 1)
                pool.tensor_tensor(hu[:], sg[:], hb[:, :, 0:H], ALU.mult).then_inc(hu_ready, 1)
                pool.wait_ge(ve3_ready, 2 * b + 2)
                pool.tensor_tensor(rs3[:], ve3[:], neg_half[:, 0:T], ALU.pow).then_inc(rs3_ready, 1)

            ffn(0, True)
            pool.wait_ge(idx_ready, 1)
            pool.wait_ge(x1_stored, 16 * NB)
            for t in range(MT):
                pool.indirect_dma_start(xg[:, t, :], None, scratch_x1, bass.IndirectOffsetOnAxis(ap=gidx[:, t:t + 1], axis=0))\
                    .then_inc(xg_in, 16)
            with pool.Fori(1, NB) as b:
                ffn(b, False)
            pool.wait_ge(dve_g, 3)
            pool.tensor_tensor(rsg[:], veg[:], neg_half[:, 0:MT], ALU.pow).then_inc(rsg_ready, 1)
            pool.wait_ge(sh_stored, 16 * NB)
            for t in range(MT):
                pool.indirect_dma_start(shg[:, t, :], None, scratch_sh, bass.IndirectOffsetOnAxis(ap=gidx[:, t:t + 1], axis=0))\
                    .then_inc(shg_in, 16)
            for t in range(MT):
                pool.wait_ge(ve_m_ready, t + 1)
                pool.tensor_tensor(rsm[:, t:t + 1], vem[:, t:t + 1], neg_half[:, 0:1], ALU.pow).then_inc(rsm_ready, 1)
            pool.wait_ge(out_stored, 16 * NB)
            for t in range(MT):
                pool.wait_ge(fin_ready, t + 1)
                pool.indirect_dma_start(out, bass.IndirectOffsetOnAxis(ap=sidx[:, t:t + 1], axis=0), fin[:, t, :], None,
                                        bounds_check=N - 1, oob_is_err=False).then_inc(scattered, 16)
            pool.wait_ge(scattered, 16 * MT)


def kernel(**inputs):
    import numpy as np
    import concourse.bacc as bacc
    from concourse.bass_utils import run_bass_kernel_spmd as run

    a = {k.replace("L0_xattn_", "").replace("L0_ffn_", ""): np.asarray(v) for k, v in inputs.items()}
    f32 = np.float32
    NB, S, D = a["x"].shape
    HD, FD = a["Wf"].shape
    E, H = a["eb1"].shape
    M = a["index_b"].shape[0]
    wf = np.zeros((P, 8 * FD), f32)
    for h in range(8):
        wf[HD * h:HD * h + HD, FD * h:FD * h + FD] = a["Wf"]
    rows = np.concatenate([a["bv"], np.tile(a["bf"], 8), a["bo"], a["sb1"], a["sb2"], a["sb3"], a["eg_b"], a["sg_b"],
                           a["exp_bias"], a["g_xattn"], a["g_ffn"]])[None, :]
    cols = np.stack([a["bq"][:P], a["bq"][P:], a["bk"][:P], a["bk"][P:], np.tile(a["bf"], 2), a["s_ln_g"],
                     a["s_ln_b"], a["sel_ln_g"], a["sel_ln_b"]], axis=1)
    ew12 = np.concatenate([a["ew1"], a["ew2"]], axis=1)
    ew12 = ew12.transpose(2, 0, 1).reshape(2, P, E, 2 * H).transpose(1, 2, 0, 3)
    arrays = {
        "x": a["x"].reshape(NB * S, D),
        "ctx_t": a["ctx_1024"].reshape(NB * S, D).T,
        "w_q": a["Wq"], "w_k": a["Wk"], "w_v": a["Wv"], "w_o": a["Wo"], "w_f_diag": wf, "rows": rows, "cols": cols,
        "sw12": np.concatenate([a["sw1"].T, a["sw2"].T], axis=1),
        "sw3": a["sw3"].T,
        "w_gate": np.concatenate([a["eg_w"], a["sg_w"]], axis=0).T,
        "ew12": ew12,
        "ew3": a["ew3"].transpose(2, 0, 1),
        "eb12": np.concatenate([a["eb1"], a["eb2"]], axis=1),
        "eb3": a["eb3"],
        "index": np.stack([a["index_b"].reshape(M // P, P).T, a["index_t"].reshape(M // P, P).T], axis=1),
        "ident": np.eye(P, dtype=f32),
    }
    arrays = {f"in_{k}": np.ascontiguousarray(v) for k, v in arrays.items()}
    nc = bacc.Bacc("TRN2", target_bir_lowering=False, num_devices=1)
    args = [nc.dram_tensor(k, v.shape, mybir.dt.from_np(v.dtype), kind="ExternalInput").ap() for k, v in arrays.items()]
    out = nc.dram_tensor("out", (NB * S, D), F32, kind="ExternalOutput").ap()
    flamingo_block(nc, *args, out)
    r = run(nc, [arrays], core_ids=[0])
    return r.results[0]["out"].reshape(NB, S, D)
```

```python
from contextlib import ExitStack

import concourse.bass as bass
from concourse import mybir

P = 128
F32 = mybir.dt.float32
F32R = mybir.dt.float32r
BF16 = mybir.dt.bfloat16
I32 = mybir.dt.int32
U32 = mybir.dt.uint32
ALU = mybir.AluOpType
ACT = mybir.ActivationFunctionType
AX_X = mybir.AxisListType.X
LN_EPS = 1e-5
ATT_EPS = 1e-8


def flamingo_block(nc, x, ctx_t, w_q, w_k, w_v, w_o, w_f_diag, rows_a, rows_b, cols, sw12, sw3, w_gate, ew, eb, index,
                   ident, part_mask, out):
    NB, S, D = 4, 512, x.shape[1]
    N = NB * S
    T = S // P
    KD = D // P
    HD, FD = 16, w_f_diag.shape[1] // 8
    PAIRS = D // (2 * HD)
    PG = PAIRS // KD
    H = sw3.shape[0]
    E = w_gate.shape[1] - 1
    EP = E // 2
    MT = index.shape[2]
    M = MT * P
    EC = ew.shape[1]
    ECB = EC // NB
    assert 2 * FD == P and H == P and PG == 4 and T == 4 and MT == 4 and KD == 2 and ECB * NB == EC

    R_BV, R_BF, R_BO, R_GX = 0, D, D + FD, 2 * D + FD
    R_SB, R_GB, R_XB = 0, 2 * H + D, 2 * H + D + E + 1
    C_BQ, C_BK, C_BF, C_SG, C_SB, C_EG, C_EB = 0, 2, 4, 5, 6, 7, 8

    scratch_x1 = nc.dram_tensor("scratch_x1", (N, D), F32).ap()
    scratch_sh = nc.dram_tensor("scratch_sh", (N, D), F32).ap()

    def by_tile(a):
        return a.rearrange("(g p) d -> p g d", p=P)

    def by_k(a):
        return a.rearrange("(k p) n -> p k n", p=P)

    with ExitStack() as ctx:
        def sb(name, shape, dt=F32):
            return ctx.enter_context(nc.sbuf_tensor(name, shape, dt))

        def sb_split(name, shape):
            return sb(name + "_hi", shape, F32R), sb(name + "_lo", shape, F32R)

        def sem(name):
            return ctx.enter_context(nc.semaphore(name))

        wq2, wk2, wv2, wo2 = (sb_split(n, [P, KD, D]) for n in ("wq", "wk", "wv", "wo"))
        wf2 = sb_split("wf", [P, 8 * FD])
        sw12_2 = sb_split("sw12s", [P, KD, 2 * H])
        sw3_2 = sb_split("sw3s", [P, D])
        ew2 = sb_split("ews", [P, EC, 512])
        rows_sb = sb("rows_sb", [P, rows_a.shape[1]])
        rows2_sb = sb("rows2_sb", [P, rows_b.shape[1]])
        cols_sb = sb("cols_sb", [P, cols.shape[1]])
        pm_sb = sb("pm_sb", [P, part_mask.shape[1]])
        wg_sb = sb("wg_sb", [P, KD, E + 1])
        ident_sb = sb("ident_sb", [P, P])
        ident_bf = sb("ident_bf", [P, P], BF16)
        ones_sb = sb("ones_sb", [P, 2 * HD])
        ones3 = sb("ones3", [P, P], BF16)
        bias3 = sb("bias3", [P, 2 * H + D], BF16)
        eb3p = sb("eb3p", [3 * E, 512], BF16)
        eb_st = sb("eb_st", [3 * E, 512])
        neg_half = sb("neg_half", [P, 16])
        att_eps = sb("att_eps", [P, 1])
        tanh_g = sb("tanh_g", [P, 2])
        tbo = sb("tbo", [P, D])
        xs = sb("xs", [P, NB * T, D])
        x1 = xs
        ctx_sb = sb("ctx_sb", [P, KD, S])
        ctx2 = sb_split("ctx", [P, KD, S])
        kT2 = sb_split("kT", [P, KD, S])
        vv = sb("vv", [P, T, D])
        x_cur = sb("x_cur", [P, T, D])
        nm_cur = sb("nm_cur", [P, T])
        rs_cur = sb("rs_cur", [P, T])
        xn = sb("xn", [P, T, D])
        xnT2 = sb_split("xnT", [P, KD, S])
        qT2 = sb_split("qT", [P, KD, S])
        full = sb("full", [P, KD, S])
        kf = sb("kf", [P, T, PAIRS * P])
        kf_sum = sb("kf_sum", [P, PAIRS * P])
        qf = sb("qf", [P, PAIRS, S])
        kvs = sb("kvs", [P, 2 * KD, P])
        kvd = sb("kvd", [P, 2 * KD, PG, 2 * HD])
        at = sb("at", [P, KD, S])
        aT2 = ctx2
        ew_st = sb("ew_st", [P, ECB, 512])
        st1 = sb("st1", [P, NB * T, 6])
        mv1 = sb("mv1", [P, NB * T, 2])
        ve1 = sb("ve1", [P, NB * T])
        nm1 = sb("nm1", [P, NB * T])
        st2 = sb("st2", [P, T, 6])
        mv2 = sb("mv2", [P, T, 2])
        ve2 = sb("ve2", [P, NB * T])
        nm2 = sb("nm2", [P, NB * T])
        stage = qf[:]
        sg, hu, hz, zn = (kf[:, 0, 512 * 0:512 * 1], kf[:, 0, 512:1024], kf[:, 1, 0:512], kf[:, 1, 512:1024])
        sg, hu, hz, zn = (a.rearrange("p (t h) -> p t h", t=T) for a in (sg, hu, hz, zn))
        sh, yo = (kf[:, n, :].rearrange("p (t d) -> p t d", t=T) for n in (2, 3))
        xn2, xn2T2 = xn, xnT2
        z_full = kf_sum[:, 0:S]
        zT2 = tuple(a[:, 0, :] for a in aT2)
        st3 = sb("st3", [P, T, 6])
        mv3 = sb("mv3", [P, T, 2])
        ve3 = sb("ve3", [P, T])
        nm3 = sb("nm3", [P, T])
        rs3 = sb("rs3", [P, T])
        xg, shg = (qf[:, 2 * n:2 * n + 2, :].rearrange("p a n -> p (a n)").rearrange("p (t d) -> p t d", t=MT)
                   for n in range(2))
        ebs = qf[:, 4:8, :]
        xgn, base, fin = xs[:, 0:4, :], xs[:, 4:8, :], xs[:, 8:12, :]
        acc = xs[:, 12:16, :]
        acc_y = ctx_sb[:].rearrange("p k (n d) -> p (k n) d", d=D)
        xgT2 = kT2
        sgm, hum, hzm, znm = (vv[:, n, :].rearrange("p (i h) -> p i h", i=2) for n in range(4))
        zfm = kf_sum[:, S:S + 2 * P].rearrange("p (i q) -> p i q", i=2)
        zTm2 = tuple(a[:, 1, :].rearrange("p (i q) -> p i q", q=P) for a in aT2)
        idx_i = sb("idx_i", [P, 2, MT], I32)
        idf = sb("idf", [P, 8, MT])
        gidx = sb("gidx", [P, MT], U32)
        sidx = sb("sidx", [P, MT], U32)
        stg = sb("stg", [P, MT, 6])
        mvg = sb("mvg", [P, MT, 2])
        veg = sb("veg", [P, MT])
        nmg = sb("nmg", [P, MT])
        rsg = sb("rsg", [P, MT])
        lg = sb("lg", [P, MT, E + 1])
        sc = sb("sc", [P, MT, E + 1])
        sx = sb("sx", [P, MT, E])
        rank_w = sb("rank_w", [P, MT, E])
        eq = sb("eq", [P, MT, E])
        mx = sb("mx", [P, MT])
        m2 = sb("m2", [P, MT])
        oh = sb("oh", [P, MT, E])
        ohc = sb("ohc", [P, MT, E])
        oh3 = sb("oh3", [P, MT, 3, E], BF16)
        top = sb("top", [P, MT])
        dif = sb("dif", [P, MT])
        swt = sb("swt", [P, 2, MT])
        cw = sb("cw", [P, 2, MT])
        ohT = sb("ohT", [3 * E, MT, P], BF16)
        stm = sb("stm", [P, MT, 6])
        mvm = sb("mvm", [P, MT, 2])
        vem = sb("vem", [P, MT])
        nmm = sb("nmm", [P, MT])
        rsm = sb("rsm", [P, MT])

        bank = [ctx.enter_context(nc.psum_tensor(f"bank{i}", [P, 512], F32)) for i in range(8)]

        def halves(b):
            return b[:].rearrange("p (t d) -> p t d", t=2)

        def quarters(b):
            return b[:].rearrange("p (t d) -> p t d", t=4)

        in_wk, in_ctx, in_wv, in_x0, in_x, in_cols, in_rows, in_id, in_wq, in_wf, in_wo, in_ffn, in_moe, in_idx, in_ew = (
            sem(n) for n in ("in_wk", "in_ctx", "in_wv", "in_x0", "in_x", "in_cols", "in_rows", "in_id", "in_wq",
                             "in_wf", "in_wo", "in_ffn", "in_moe", "in_idx", "in_ew"))
        x1_stored, sh_stored, out_stored, xg_in, shg_in, scattered = (
            sem(n) for n in ("x1_stored", "sh_stored", "out_stored", "xg_in", "shg_in", "scattered"))
        consts_ready, tanh_ready, tbo_ready, bf_consts, parts = (
            sem(n) for n in ("consts_ready", "tanh_ready", "tbo_ready", "bf_consts", "parts"))
        st1_ready, mv1_ready, ve1_ready = (sem(n) for n in ("st1_ready", "mv1_ready", "ve1_ready"))
        x_cur_in, cur_ready, held, pool_held, act_held = (
            sem(n) for n in ("x_cur_in", "cur_ready", "held", "pool_held", "act_held"))
        (w_hi, w_lo, ctx0_hi, ctx_hi, ctx_ready, ew_hi, ew_lo, kT_hi, kT_ready, xnT_hi, xnT_ready, qT_hi, qT_ready,
         aT_hi, aT_ready) = (
            sem(n) for n in ("w_hi", "w_lo", "ctx0_hi", "ctx_hi", "ctx_ready", "ew_hi", "ew_lo", "kT_hi", "kT_ready",
                             "xnT_hi", "xnT_ready", "qT_hi", "qT_ready", "aT_hi", "aT_ready"))
        pe_k, pe_v, pe_xt, pe_q, pe_kf, pe_qf, pe_kv, pe_kvt, pe_nd, pe_wo = (
            sem(n) for n in ("pe_k", "pe_v", "pe_xt", "pe_q", "pe_kf", "pe_qf", "pe_kv", "pe_kvt", "pe_nd", "pe_wo"))
        (xn_ready, xb_ready, v_ready, kf_added, kf_ready, kfs_part, kfs_ready, qf_ready, kvs_ready, kvd_zero, kvd_ready,
         den_ready, rden_ready, at_ready, x1_ready) = (
            sem(n) for n in ("xn_ready", "xb_ready", "v_ready", "kf_added", "kf_ready", "kfs_part", "kfs_ready",
                             "qf_ready", "kvs_ready", "kvd_zero", "kvd_ready", "den_ready", "rden_ready", "at_ready",
                             "x1_ready"))
        st2_ready, mv2_ready, ve2_ready = (sem(n) for n in ("st2_ready", "mv2_ready", "ve2_ready"))
        pe_x2t, pe_h, pe_zt, pe_y = (sem(n) for n in ("pe_x2t", "pe_h", "pe_zt", "pe_y"))
        (xn2_ready, xn2T_hi, xn2T_ready, sg_ready, hu_ready, hz_ready, st3_ready, mv3_ready, ve3_ready, rs3_ready,
         zn_ready, z_hi, zT_ready, sh_ready, yo_ready) = (
            sem(n) for n in ("xn2_ready", "xn2T_hi", "xn2T_ready", "sg_ready", "hu_ready", "hz_ready", "st3_ready",
                             "mv3_ready", "ve3_ready", "rs3_ready", "zn_ready", "z_hi", "zT_ready", "sh_ready",
                             "yo_ready"))
        idx_step, idx_ready, dve_g, rsg_ready, xgn_ready, pe_xgt, xgT_hi, xgT_ready, pe_gate, gate_added, sc_ready = (
            sem(n) for n in ("idx_step", "idx_ready", "dve_g", "rsg_ready", "xgn_ready", "pe_xgt", "xgT_hi", "xgT_ready",
                             "pe_gate", "gate_added", "sc_ready"))
        rank_ready, route_step, dif_ready, swt_ready, oh_ready, oh3_ready, pe_oht, ohT_ready, pe_eb, ebs_ready, ohc_ready = (
            sem(n) for n in ("rank_ready", "route_step", "dif_ready", "swt_ready", "oh_ready", "oh3_ready", "pe_oht",
                             "ohT_ready", "pe_eb", "ebs_ready", "ohc_ready"))
        cw_ready, base_step = sem("cw_ready"), sem("base_step")
        (pe_hm, h_part, hs_ready, sgm_ready, dve_m, ve_m_ready, rsm_ready, znm_ready, pe_ztm, zm_hi, zTm_ready,
         pe_ym, y_part, base_ready, fin_ready) = (
            sem(n) for n in ("pe_hm", "h_part", "hs_ready", "sgm_ready", "dve_m", "ve_m_ready", "rsm_ready", "znm_ready",
                             "pe_ztm", "zm_hi", "zTm_ready", "pe_ym", "y_part", "base_ready", "fin_ready"))

        block = ctx.enter_context(nc.Block())

        def row(a, n):
            return rows_sb[:, a:a + n]

        def row2(a, n):
            return rows2_sb[:, a:a + n]

        def col(a):
            return cols_sb[:, a:a + 1]

        def bc(a, n):
            return a.unsqueeze(1).to_broadcast([P, n, a.shape[1]])

        def bcl(a, n):
            return a.unsqueeze(2).to_broadcast([P, a.shape[1], n])

        def staged(n, like):
            a = stage[:, n, :]
            return a.rearrange("p (k n) -> p k n", k=like.shape[1]) if len(like.shape) == 3 else a[:, 0:like.shape[1]]

        SPLITS = [(staged(n, w[0]), w, s_, v) for n, (w, s_, v) in enumerate(
            ((wk2, in_wk, 16), (wv2, in_wv, 16), (wq2, in_wq, 16), (wf2, in_wf, 16), (wo2, in_wo, 16),
             (sw12_2, in_ffn, 32), (sw3_2, in_ffn, 32)))]
        W_K, W_V, W_Q, W_F, W_O, W_SW12, W_SW3 = (n + 1 for n in range(7))

        @block.sync
        def _(sp):
            ctx_v = by_k(ctx_t)
            xv = by_tile(x)
            sp.dma_start(SPLITS[0][0], by_k(w_k)).then_inc(in_wk, 16)
            sp.dma_start(ctx_sb[:], ctx_v[:, :, 0:S]).then_inc(in_ctx, 16)
            sp.dma_start(x_cur[:], xv[:, 0:T, :]).then_inc(x_cur_in, 16)
            sp.dma_start(SPLITS[1][0], by_k(w_v)).then_inc(in_wv, 16)
            sp.dma_start(SPLITS[2][0], by_k(w_q)).then_inc(in_wq, 16)
            sp.dma_start(SPLITS[3][0], w_f_diag).then_inc(in_wf, 16)
            sp.dma_start(SPLITS[4][0], by_k(w_o)).then_inc(in_wo, 16)
            sp.dma_start(xs[:, T:NB * T, :], xv[:, T:NB * T, :]).then_inc(in_x, 16)
            sp.dma_start(SPLITS[5][0], by_k(sw12)).then_inc(in_ffn, 16)
            sp.dma_start(SPLITS[6][0], sw3).then_inc(in_ffn, 16)
            sp.dma_start(rows2_sb[:], rows_b.partition_broadcast(P)).then_inc(in_moe, 16)
            for n in range(3):
                sp.dma_start(eb_st[n * E:n * E + E, :], eb).then_inc(in_moe, 16)
            sp.dma_start(wg_sb[:], by_k(w_gate)).then_inc(in_moe, 16)
            sp.dma_start(idx_i[:], index).then_inc(in_idx, 16)
            sp.dma_start(ew_st[:], ew[:, 0:ECB, :]).then_inc(in_ew, 16)
            sp.wait_ge(in_x, 16)
            with sp.Fori(1, NB) as b:
                sp.wait_ge(ctx_ready, b)
                sp.dma_start(ctx_sb[:], ctx_v[:, :, bass.ds(b * S, S)]).then_inc(in_ctx, 16)
                sp.wait_ge(xn_ready, 4 * b)
                sp.dma_start(x_cur[:], xs[:, bass.ds(b * T, T), :]).then_inc(x_cur_in, 16)
                sp.wait_ge(ew_lo, ECB * b)
                sp.dma_start(ew_st[:], ew[:, bass.ds(b * ECB, ECB), :]).then_inc(in_ew, 16)
            s1, s2, o = by_tile(scratch_x1), by_tile(scratch_sh), by_tile(out)


            def store_x1(b):
                sp.wait_ge(x1_ready, 2 * b + 2)
                sp.dma_start(s1[:, bass.ds(b * T, T), :], x1[:, bass.ds(b * T, T), :]).then_inc(x1_stored, 16)

            def load_x1(b):
                sp.dma_start(x_cur[:], x1[:, bass.ds(b * T, T), :]).then_inc(x_cur_in, 16)

            with sp.Fori(0, NB - 1) as b:
                store_x1(b)
            sp.wait_ge(xn_ready, 4 * NB)
            load_x1(0)
            with sp.Fori(1, NB - 1) as b:
                sp.wait_ge(xn2_ready, 4 * b)
                load_x1(b)
            store_x1(NB - 1)
            sp.wait_ge(xn2_ready, 4 * NB - 4)
            load_x1(NB - 1)
            with sp.Fori(0, NB) as b:
                sp.wait_ge(sh_ready, 2 * b + 4)
                sp.dma_start(s2[:, bass.ds(b * T, T), :], sh).then_inc(sh_stored, 16)
                sp.wait_ge(yo_ready, 2 * b + 4)
                sp.dma_start(o[:, bass.ds(b * T, T), :], yo).then_inc(out_stored, 16)
            sp.wait_ge(scattered, 16 * MT)

        @block.tensor
        def _(pe):
            def mm3(dst, lhs, rhs, start, stop):
                pe.matmul(dst, lhs[0], rhs[0], start=start, stop=False)
                pe.matmul(dst, lhs[1], rhs[0], start=False, stop=False)
                return pe.matmul(dst, lhs[0], rhs[1], start=False, stop=stop)

            def cut(pair, *at):
                return tuple(a[at] for a in pair)

            ALL = slice(None)

            def tok(t):
                return slice(t * P, (t + 1) * P)

            def transposes(src, dst, k, done):
                for t in range(T):
                    last = pe.transpose(dst[:, t * P:(t + 1) * P], src[:, t, k * P:(k + 1) * P], ident_sb[:])
                last.then_inc(done, 1)

            def out_proj(b, dsts):
                pe.wait_ge(aT_ready, 2 * b + 2)
                for n, dst in enumerate(dsts):
                    for t in (2 * n, 2 * n + 1):
                        for k in range(KD):
                            last = mm3(halves(dst)[:, t % 2, :], cut(aT2, ALL, k, tok(t)), cut(wo2, ALL, k),
                                       k == 0, k == KD - 1)
                    last.then_inc(pe_wo, 1)

            def query_features(b, p):
                if p < 4:
                    pe.wait_ge(kf_added, 8 * b + p + 5)
                else:
                    pe.wait_ge(qf_ready, 8 * b + p - 3)
                mm3(bank[2 + p % 4][:], cut(wf2, ALL, slice((p % PG) * P, (p % PG + 1) * P)), cut(qT2, ALL, p // PG),
                    True, True).then_inc(pe_qf, 1)

            def attention(b, first):
                if first:
                    pe.wait_ge(w_lo, W_K)
                else:
                    pe.wait_ge(xn_ready, 4 * b + 4)
                    for k in range(KD):
                        transposes(xn, bank[k], k, pe_xt)
                pe.wait_ge(ctx_ready, b + 1)
                for m in range(KD):
                    for k in range(KD):
                        last = mm3(bank[6 + m][:], cut(wk2, ALL, k, tok(m)), cut(ctx2, ALL, k), k == 0, k == KD - 1)
                    last.then_inc(pe_k, 1)
                if first:
                    pe.wait_ge(in_id, 16)
                    pe.wait_ge(xn_ready, 4)
                    for k in range(KD):
                        transposes(xn, bank[k], k, pe_xt)
                    pe.wait_ge(w_lo, W_V)
                for n in range(2):
                    pe.wait_ge(xnT_hi, 2 * b + 1 + n)
                    for t in (2 * n, 2 * n + 1):
                        for k in range(KD):
                            last = mm3(halves(bank[n])[:, t % 2, :], cut(ctx2, ALL, k, tok(t)), cut(wv2, ALL, k),
                                       k == 0, k == KD - 1)
                    last.then_inc(pe_v, 1)
                if first:
                    pe.wait_ge(w_lo, W_Q)
                pe.wait_ge(xnT_ready, 2 * b + 2)
                for m in range(KD):
                    pe.wait_ge(kT_hi, 2 * b + 1 + m)
                    for k in range(KD):
                        last = mm3(bank[6 + m][:], cut(wq2, ALL, k, tok(m)), cut(xnT2, ALL, k), k == 0, k == KD - 1)
                    last.then_inc(pe_q, 1)
                if first:
                    pe.wait_ge(w_lo, W_F)
                else:
                    pe.wait_ge(v_ready, 2 * b + 2)
                    out_proj(b - 1, (bank[0], bank[1]))
                pe.wait_ge(kT_ready, 2 * b + 2)
                for j in range(2 * T):
                    if j >= 4:
                        pe.wait_ge(kf_added, 8 * b + j - 3)
                    elif not first and j % 2 == 0:
                        pe.wait_ge(at_ready, 2 * b - 1 + j // 2)
                    t, c = j // 2, j % 2
                    mm3(bank[2 + j % 4][:], cut(kT2, ALL, c, tok(t)), cut(wf2, ALL), True, True).then_inc(pe_kf, 1)
                pe.wait_ge(qT_ready, 2 * b + 2)
                query_features(b, 0)
                query_features(b, 1)
                pe.wait_ge(kf_ready, 8 * b + 8)
                pe.wait_ge(v_ready, 2 * b + 2)
                if first:
                    pe.wait_ge(consts_ready, 2)
                for c in range(KD):
                    for t in range(T):
                        for g in range(PG):
                            p = PG * c + g
                            pe.matmul(quarters(bank[6])[32 * g:32 * g + 32, c, :], vv[:, t, 32 * p:32 * p + 32],
                                      kf[:, t, P * p:P * (p + 1)], start=(t == 0), stop=(t == T - 1))
                query_features(b, 2)
                query_features(b, 3)
                pe.wait_ge(kfs_ready, b + 1)
                for c in range(KD):
                    for g in range(PG):
                        p = PG * c + g
                        last = pe.matmul(quarters(bank[6])[32 * g:32 * g + 32, KD + c, :], ones_sb[:],
                                         kf_sum[:, P * p:P * (p + 1)], start=True, stop=True)
                last.then_inc(pe_kv, 1)
                query_features(b, 4)
                query_features(b, 5)
                pe.wait_ge(kvs_ready, b + 1)
                for n in range(2 * KD):
                    last = pe.transpose(quarters(bank[6])[:, n, :], kvs[:, n, :], ident_sb[:])
                last.then_inc(pe_kvt, 1)
                query_features(b, 6)
                query_features(b, 7)
                if not first:
                    pe.wait_ge(x1_ready, 2 * b)
                pe.wait_ge(kvd_ready, 2 * b + 2)
                for c in range(KD):
                    pe.wait_ge(qf_ready, 8 * b + 6 + 2 * c)
                    for n in range(2):
                        for g in range(PG):
                            last = pe.matmul(bank[2 + 2 * c + n][32 * g:32 * g + 32, :], kvd[:, KD * n + c, g, :],
                                             qf[:, PG * c + g, :], start=True, stop=True)
                    last.then_inc(pe_nd, 1)

            attention(0, True)
            pe.wait_ge(w_lo, W_O)
            with pe.Fori(1, NB) as b:
                attention(b, False)

            def bias(dst, at_):
                pe.matmul(dst, ones3[:], bias3[:, at_:at_ + 256], start=True, stop=False)

            def rows_t(b, first):
                pe.wait_ge(xn2_ready, 4 * b + 4)
                for k in range(KD):
                    if not first:
                        pe.wait_ge(xn2T_hi, 2 * b - 1 + k)
                    transposes(xn2, bank[k], k, pe_x2t)

            def ffn_up(b, n):
                for t in (2 * n, 2 * n + 1):
                    dst = halves(bank[2 + n])[:, t % 2, :]
                    bias(dst, R_SB)
                    for k in range(KD):
                        last = mm3(dst, cut(xn2T2, ALL, k, tok(t)), cut(sw12_2, ALL, k), False, k == KD - 1)
                last.then_inc(pe_h, 1)

            def z_t(b):
                pe.wait_ge(zn_ready, 4 * b + 4)
                for t in range(T):
                    last = pe.transpose(bank[4][:, t * P:(t + 1) * P], zn[:, t, :], ident_sb[:])
                last.then_inc(pe_zt, 1)

            def ffn_down(b):
                pe.wait_ge(zT_ready, b + 1)
                pe.wait_ge(x1_ready, 2 * NB)
                for n in range(2):
                    pe.wait_ge(sh_ready, 2 * b + 1 + n)
                    pe.wait_ge(yo_ready, 2 * b + 1 + n)
                    for t in (2 * n, 2 * n + 1):
                        dst = halves(bank[5 + n])[:, t % 2, :]
                        bias(dst, R_SB + 2 * H)
                        last = mm3(dst, cut(zT2, ALL, tok(t)), cut(sw3_2, ALL), False, True)
                    last.then_inc(pe_y, 1)

            pe.wait_ge(w_lo, W_SW3)
            pe.wait_ge(bf_consts, 3)
            pe.wait_ge(parts, 5)
            rows_t(0, True)
            pe.wait_ge(at_ready, 2 * NB - 1)
            pe.wait_ge(xn2T_ready, 2)
            ffn_up(0, 0)
            ffn_up(0, 1)
            rows_t(1, False)
            out_proj(NB - 1, (bank[5], bank[6]))
            with pe.Fori(1, NB - 1) as b:
                pe.wait_ge(xn2T_ready, 2 * b + 2)
                pe.wait_ge(hz_ready, 2 * b)
                ffn_up(b, 0)
                z_t(b - 1)
                ffn_up(b, 1)
                rows_t(b + 1, False)
                ffn_down(b - 1)
            pe.wait_ge(xn2T_ready, 2 * NB)
            pe.wait_ge(hz_ready, 2 * NB - 2)
            ffn_up(NB - 1, 0)
            z_t(NB - 2)
            ffn_up(NB - 1, 1)
            ffn_down(NB - 2)
            pe.wait_ge(xgn_ready, 1)
            pe.wait_ge(xn2T_hi, 2 * NB)
            for k in range(KD):
                transposes(xgn, bank[k], k, pe_xgt)
            z_t(NB - 1)
            pe.wait_ge(xgT_hi, KD)
            pe.wait_ge(in_moe, 80)
            for t in range(MT):
                for k in range(KD):
                    last = pe.matmul(bank[7][:, t * (E + 1):(t + 1) * (E + 1)], full[:, k, t * P:(t + 1) * P],
                                     wg_sb[:, k, :], start=(k == 0), stop=(k == KD - 1))
            last.then_inc(pe_gate, 1)
            ffn_down(NB - 1)

            def expert_up(t):
                for j in range(EP):
                    if t:
                        pe.wait_ge(h_part, 8 * (t - 1) + 2 * j + 2)
                    for k in range(KD):
                        last = mm3(bank[j][:], cut(xgT2, ALL, k, tok(t)), cut(ew2, ALL, k * EP + j), k == 0, k == KD - 1)
                    last.then_inc(pe_hm, 1)

            def z_expert_t(t):
                pe.wait_ge(znm_ready, t + 1)
                if t:
                    pe.wait_ge(zm_hi, t)
                else:
                    pe.wait_ge(z_hi, NB)
                pe.transpose(bank[4][:, 0:P], znm[:, t % 2, :], ident_sb[:]).then_inc(pe_ztm, 1)

            def expert_down(t):
                pe.wait_ge(zTm_ready, t + 1)
                for j in range(EP):
                    u = EP * t + j
                    if u >= 3:
                        pe.wait_ge(y_part, 2 * (u - 2))
                    mm3(bank[5 + u % 3][:], cut(zTm2, ALL, t % 2), cut(ew2, ALL, KD * EP + j), True, True)\
                        .then_inc(pe_ym, 1)

            pe.wait_ge(xgT_ready, KD)
            pe.wait_ge(ew_lo, EC)
            pe.wait_ge(hz_ready, 2 * NB)
            expert_up(0)
            pe.wait_ge(oh3_ready, 1)
            bank7_bf = bank[7][:].bitcast(BF16)
            for t in range(MT):
                last = pe.transpose(bank7_bf[0:3 * E, t * P:(t + 1) * P], oh3[:, t, :, :].rearrange("p r e -> p (r e)"),
                                    ident_bf[:])
            last.then_inc(pe_oht, 1)
            pe.wait_ge(ohT_ready, 1)
            pe.wait_ge(parts, 10)
            for t in range(MT):
                if t:
                    pe.wait_ge(ebs_ready, t)
                pe.matmul(bank[7][:], ohT[:, t, :], eb3p[:], start=True, stop=True).then_inc(pe_eb, 1)
            expert_up(1)
            pe.wait_ge(ebs_ready, MT)
            pe.wait_ge(yo_ready, 2 * NB + 2)
            pe.wait_ge(sh_ready, 2 * NB + 2)
            for t in range(MT):
                z_expert_t(t)
                if t + 2 < MT:
                    expert_up(t + 2)
                expert_down(t)

        @block.scalar
        def _(act):
            act.dma_start(xs[:, 0:T, :], by_tile(x)[:, 0:T, :]).then_inc(in_x0, 16)
            act.dma_start(cols_sb[:], cols).then_inc(in_cols, 16)
            act.dma_start(ident_sb[:], ident).then_inc(in_id, 16)
            act.dma_start(rows_sb[:], rows_a.partition_broadcast(P)).then_inc(in_rows, 16)
            act.dma_start(pm_sb[:], part_mask).then_inc(in_cols, 16)
            act.sem_inc(sh_ready, 2)
            act.sem_inc(sh_stored, 16)

            def weight_hi(n):
                st, w, s_, v = SPLITS[n]
                act.wait_ge(s_, v)
                act.activation(w[0][:], st, ACT.Copy).then_inc(w_hi, 1)

            def split_evac(dst, m, src, hi_sem, b=None):
                kw = {} if b is None else {"bias": b}
                f = ACT.Copy if b is None else ACT.Identity
                act.activation(dst[0][:, m, :], src[:], f, **kw)
                act.activation(full[:, m, :], src[:], f, **kw).then_inc(hi_sem, 1)

            weight_hi(0)
            act.wait_ge(in_ctx, 16)
            act.activation(ctx2[0][:], ctx_sb[:], ACT.Copy).then_inc(ctx0_hi, 1)
            weight_hi(1)

            def rows_evac(b, first):
                for k in range(KD):
                    act.wait_ge(pe_xt, 2 * b + 1 + k)
                    if not first:
                        act.wait_ge(qT_ready, 2 * b - 1 + k)
                    elif k == 0:
                        act.wait_ge(kT_ready, 2)
                    split_evac(xnT2, k, bank[k], xnT_hi)

            def keys_evac(b, first):
                for m in range(KD):
                    act.wait_ge(pe_k, 2 * b + 1 + m)
                    if not first:
                        act.wait_ge(xnT_ready, 2 * b + 1 + m)
                    split_evac(kT2, m, bank[6 + m], kT_hi, col(C_BK + m))

            def output_hi(b, v_total):
                act.wait_ge(pe_v, v_total)
                act.sem_inc(act_held, 1)
                for c in range(KD):
                    act.wait_ge(at_ready, 2 * b + 1 + c)
                    act.activation(aT2[0][:, c, :], at[:, c, :], ACT.Copy).then_inc(aT_hi, 1)

            def attention(b, first):
                if first:
                    act.wait_ge(in_cols, 32)
                    keys_evac(b, first)
                    rows_evac(b, first)
                    for n in range(2, 7):
                        weight_hi(n)
                    act.wait_ge(in_rows, 16)
                    act.activation(tanh_g[:], row(R_GX, 2), ACT.Tanh).then_inc(tanh_ready, 1)
                else:
                    rows_evac(b, first)
                    keys_evac(b, first)
                    output_hi(b - 1, 2 * b + 2)
                for m in range(KD):
                    act.wait_ge(pe_q, 2 * b + 1 + m)
                    if first:
                        act.wait_ge(xnT_ready, 1 + m)
                    else:
                        act.wait_ge(kT_ready, 2 * b + 1 + m)
                    split_evac(qT2, m, bank[6 + m], qT_hi, col(C_BQ + m))
                for j in range(2 * T):
                    act.wait_ge(kf_added, 8 * b + j + 1)
                    part = kf[:, j // 2, (j % 2) * 512:(j % 2) * 512 + 512]
                    act.activation(part, part, ACT.Relu).then_inc(kf_ready, 1)
                for p in range(PAIRS):
                    if p == 4:
                        act.wait_ge(pe_kv, b + 1)
                        act.activation(kvs[:], quarters(bank[6]), ACT.Copy).then_inc(kvs_ready, 1)
                    act.wait_ge(pe_qf, 8 * b + p + 1)
                    if first and p == 0:
                        act.wait_ge(w_lo, W_SW3)
                    act.activation(qf[:, p, :], bank[2 + p % 4][:], ACT.Relu, bias=col(C_BF)).then_inc(qf_ready, 1)
                act.wait_ge(in_ew, 16 * b + 16)
                act.sem_inc(act_held, 1)
                for n in range(ECB):
                    act.activation(ew2[0][:, b * ECB + n, :], ew_st[:, n, :], ACT.Copy).then_inc(ew_hi, 1)
                for c in range(KD):
                    act.wait_ge(pe_nd, 2 * b + c + 1)
                    if first and c == 0:
                        act.wait_ge(bf_consts, 1)
                    act.activation(at[:, c, :], bank[3 + 2 * c][:], ACT.Identity, bias=att_eps[:]).then_inc(den_ready, 1)

            attention(0, True)
            with act.Fori(1, NB) as b:
                attention(b, False)

            def rows2_evac(b, whole):
                for k in range(KD):
                    act.wait_ge(pe_x2t, 2 * b + 1 + k)
                    if whole:
                        act.activation(full[:, k, :], bank[k][:], ACT.Copy)
                    act.activation(xn2T2[0][:, k, :], bank[k][:], ACT.Copy).then_inc(xn2T_hi, 1)

            def gate_sigmoid(b, n, first=False):
                act.wait_ge(pe_h, 2 * b + 1 + n)
                if not first:
                    act.wait_ge(hz_ready, 2 * b)
                act.activation(sg[:, 2 * n:2 * n + 2, :], halves(bank[2 + n])[:, :, 0:H], ACT.Sigmoid).then_inc(sg_ready, 1)

            def z_evac(b):
                act.wait_ge(pe_zt, b + 1)
                act.activation(z_full, bank[4][:], ACT.Identity, bias=col(C_SB), scale=col(C_SG))
                act.activation(zT2[0], bank[4][:], ACT.Identity, bias=col(C_SB), scale=col(C_SG)).then_inc(z_hi, 1)

            def shared_evac(b):
                for n in range(2):
                    act.wait_ge(pe_y, 2 * b + 1 + n)
                    act.wait_ge(sh_stored, 16 * b + 16)
                    act.activation(sh[:, 2 * n:2 * n + 2, :], halves(bank[5 + n]), ACT.Copy).then_inc(sh_ready, 1)

            act.wait_ge(qT_ready, 2 * NB)
            rows2_evac(0, True)
            output_hi(NB - 1, 2 * NB)
            gate_sigmoid(0, 0, True)
            gate_sigmoid(0, 1, True)
            act.wait_ge(xn2T_ready, 2)
            rows2_evac(1, True)
            with act.Fori(1, NB - 1) as b:
                gate_sigmoid(b, 0)
                z_evac(b - 1)
                gate_sigmoid(b, 1)
                rows2_evac(b + 1, False)
                shared_evac(b - 1)
            gate_sigmoid(NB - 1, 0)
            z_evac(NB - 2)
            gate_sigmoid(NB - 1, 1)
            shared_evac(NB - 2)
            for k in range(KD):
                act.wait_ge(pe_xgt, k + 1)
                act.activation(full[:, k, :], bank[k][:], ACT.Copy)
                act.activation(xgT2[0][:, k, :], bank[k][:], ACT.Copy).then_inc(xgT_hi, 1)
            z_evac(NB - 1)
            act.wait_ge(gate_added, 1)
            act.activation(sc[:], lg[:], ACT.Sigmoid).then_inc(sc_ready, 1)
            shared_evac(NB - 1)
            act.wait_ge(dif_ready, 1)
            act.activation(swt[:, 0, :], dif[:], ACT.Sigmoid).then_inc(swt_ready, 1)
            act.activation(swt[:, 1, :], dif[:], ACT.Sigmoid, scale=-1.0).then_inc(swt_ready, 1)

            act.wait_ge(pe_oht, 1)
            act.activation(ohT[:], bank[7][:].bitcast(BF16)[0:3 * E, 0:MT * P].rearrange("p (t q) -> p t q", t=MT),
                           ACT.Copy).then_inc(ohT_ready, 1)
            for t in range(MT):
                act.wait_ge(pe_eb, t + 1)
                act.activation(ebs[:, t, :], bank[7][:], ACT.Copy).then_inc(ebs_ready, 1)
            for t in range(MT):
                act.wait_ge(hs_ready, t + 1)
                act.activation(sgm[:, t % 2, :], acc[:, 2 * (t % 2), 0:H], ACT.Sigmoid).then_inc(sgm_ready, 1)
                act.wait_ge(pe_ztm, t + 1)
                if t >= 2:
                    act.wait_ge(zTm_ready, t - 1)
                    act.wait_ge(pe_ym, EP * (t - 1))
                act.activation(zfm[:, t % 2, :], bank[4][:, 0:P], ACT.Identity, bias=col(C_EB), scale=col(C_EG))
                act.activation(zTm2[0][:, t % 2, :], bank[4][:, 0:P], ACT.Identity, bias=col(C_EB), scale=col(C_EG))\
                   .then_inc(zm_hi, 1)

        @block.vector
        def _(dve):
            def low(dst, whole, hi, done):
                return dve.tensor_tensor(dst, whole, hi.bitcast(F32), ALU.subtract).then_inc(done, 1)

            def stats(src, st, mv, n, st_sem, mv_sem, total, by_register):
                for t in range(n):
                    last = dve.bn_stats(st[:, t, :], src(t))
                last.then_inc(st_sem, 1)
                aggregate(st, mv, n, st_sem, mv_sem, total, total, by_register)

            def aggregate(st, mv, n, st_sem, mv_sem, st_total, mv_total, by_register):
                dve.wait_ge(st_sem, st_total)
                if by_register:
                    dve.sem_inc(held, 1)
                for t in range(n):
                    last = dve.bn_aggr(mv[:, t, :], st[:, t, :])
                last.then_inc(mv_sem, 1)
                dve.wait_ge(mv_sem, mv_total)

            def weight_lo(n):
                st, w, s_, v = SPLITS[n]
                dve.wait_ge(w_hi, n + 1)
                low(w[1][:], st, w[0][:], w_lo)

            def x_stats(b):
                stats(lambda t: xs[:, T * b + t, :], st1[:, T * b:T * b + T, :], mv1[:, T * b:T * b + T, :], T,
                      st1_ready, mv1_ready, b + 1, False)
                dve.tensor_scalar(ve1[:, T * b:T * b + T], mv1[:, T * b:T * b + T, 1], LN_EPS, None, ALU.add)\
                   .then_inc(ve1_ready, 1)
                dve.tensor_scalar(nm1[:, T * b:T * b + T], mv1[:, T * b:T * b + T, 0], -1.0, None, ALU.mult)\
                   .then_inc(ve1_ready, 1)

            def bf16_parts(whole, dst, m1, m2, count):
                for n, m in enumerate((m1, m2)):
                    dve.tensor_copy(dst, whole).then_inc(parts, 1)
                    dve.wait_ge(parts, count + 2 * n + 1)
                    dve.scalar_tensor_tensor(whole, dst, m, whole, ALU.mult, ALU.add).then_inc(parts, 1)
                    dve.wait_ge(parts, count + 2 * n + 2)
                dve.tensor_copy(dst, whole).then_inc(parts, 1)

            dve.sem_inc(yo_ready, 2)
            dve.sem_inc(out_stored, 16)
            dve.memset(neg_half[:], -0.5).then_inc(consts_ready, 1)
            dve.memset(ones_sb[:], 1.0).then_inc(consts_ready, 1)
            dve.memset(kvd[:], 0.0).then_inc(kvd_zero, 1)
            dve.memset(att_eps[:], ATT_EPS).then_inc(bf_consts, 1)
            weight_lo(0)
            dve.wait_ge(ctx0_hi, 1)
            low(ctx2[1][:], ctx_sb[:], ctx2[0][:], ctx_ready)
            dve.wait_ge(in_x0, 16)
            x_stats(0)
            for n in range(1, 4):
                weight_lo(n)
            dve.wait_ge(in_rows, 16)
            dve.wait_ge(kvd_zero, 1)

            def output_lo(b):
                for c in range(KD):
                    dve.wait_ge(aT_hi, 2 * b + c + 1)
                    low(aT2[1][:, c, :], at[:, c, :], aT2[0][:, c, :], aT_ready)

            def residual(b, srcs):
                for n, src in enumerate(srcs):
                    dve.wait_ge(xb_ready, b + 1)
                    dve.wait_ge(pe_wo, 2 * b + 1 + n)
                    rows = bass.ds(b * T + 2 * n, 2)
                    dve.scalar_tensor_tensor(x1[:, rows, :], halves(src), tanh_g[:, 0:1], xs[:, rows, :], ALU.mult, ALU.add)\
                       .then_inc(x1_ready, 1)

            def x1_stats(b):
                dve.wait_ge(x1_ready, 2 * b + 2)
                dve.sem_inc(held, 1)
                stats(lambda t: x1[:, b * T + t, :], st2, mv2, T, st2_ready, mv2_ready, b + 1, True)
                dve.tensor_scalar(ve2[:, bass.ds(b * T, T)], mv2[:, :, 1], LN_EPS, None, ALU.add).then_inc(ve2_ready, 1)
                dve.tensor_scalar(nm2[:, bass.ds(b * T, T)], mv2[:, :, 0], -1.0, None, ALU.mult).then_inc(ve2_ready, 1)
                dve.wait_ge(ve2_ready, 2 * b + 2)

            def attention(b, first):
                for n in range(2):
                    dve.wait_ge(pe_v, 2 * b + 1 + n)
                    dve.tensor_tensor(vv[:, 2 * n:2 * n + 2, :], halves(bank[n]), bc(row(R_BV, D), 2), ALU.add)\
                       .then_inc(v_ready, 1)
                if not first:
                    output_lo(b - 1)
                    residual(b - 1, (bank[0], bank[1]))
                for j in range(2 * T):
                    dve.wait_ge(pe_kf, 8 * b + j + 1)
                    dve.tensor_tensor(kf[:, j // 2, (j % 2) * 512:(j % 2) * 512 + 512].rearrange("p (h f) -> p h f", f=FD),
                                      bank[2 + j % 4][:].rearrange("p (h f) -> p h f", f=FD), bc(row(R_BF, FD), 8),
                                      ALU.add).then_inc(kf_added, 1)
                    if first and j == 0:
                        for n in range(4, 7):
                            weight_lo(n)
                if first:
                    dve.wait_ge(tanh_ready, 1)
                    dve.tensor_scalar(tbo[:], row(R_BO, D), tanh_g[:, 0:1], None, ALU.mult).then_inc(tbo_ready, 1)
                    dve.wait_ge(in_x, 16)
                    for n in range(1, NB):
                        x_stats(n)
                    dve.wait_ge(in_id, 16)
                    dve.tensor_copy(ident_bf[:], ident_sb[:]).then_inc(bf_consts, 1)
                    dve.wait_ge(in_cols, 32)
                    dve.tensor_copy(ones3[:], pm_sb[:, 0:1].to_broadcast([P, P])).then_inc(bf_consts, 1)
                    dve.wait_ge(in_moe, 80)
                    bf16_parts(row2(R_SB, 2 * H + D), bias3[:], pm_sb[:, 1:2], pm_sb[:, 2:3], 0)
                    bf16_parts(eb_st[:], eb3p[:], pm_sb[0:3 * E, 3:4], pm_sb[0:3 * E, 4:5], 5)
                else:
                    x1_stats(b - 1)
                for n in range(ECB):
                    dve.wait_ge(ew_hi, b * ECB + n + 1)
                    low(ew2[1][:, b * ECB + n, :], ew_st[:, n, :], ew2[0][:, b * ECB + n, :], ew_lo)
                dve.wait_ge(pe_kvt, b + 1)
                src = bank[6][:].rearrange("p (n g d) -> p (n g) d", n=2 * KD, g=PG)
                dst = kvd[:].rearrange("p n g d -> p (n g) d")
                for a in range(2):
                    dve.tensor_copy(dst[64 * a:64 * a + 64, :, HD * a:HD * a + HD],
                                    src[64 * a:64 * a + 64, :, HD * a:HD * a + HD]).then_inc(kvd_ready, 1)
                for c in range(KD):
                    dve.wait_ge(den_ready, 2 * b + c + 1)
                    dve.reciprocal(at[:, c, :], at[:, c, :]).then_inc(rden_ready, 1)
                    dve.wait_ge(rden_ready, 2 * b + c + 1)
                    dve.tensor_tensor(at[:, c, :], bank[2 + 2 * c][:], at[:, c, :], ALU.mult).then_inc(at_ready, 1)

            attention(0, True)
            with dve.Fori(1, NB) as b:
                attention(b, False)
            output_lo(NB - 1)

            def swiglu(b, n):
                dve.wait_ge(sg_ready, 2 * b + 1 + n)
                two = slice(2 * n, 2 * n + 2)
                dve.tensor_tensor(hu[:, two, :], halves(bank[2 + n])[:, :, 0:H], sg[:, two, :], ALU.mult).then_inc(hu_ready, 1)
                dve.wait_ge(hu_ready, 2 * b + 1 + n)
                dve.tensor_tensor(hz[:, two, :], halves(bank[2 + n])[:, :, H:2 * H], hu[:, two, :], ALU.mult)\
                   .then_inc(hz_ready, 1)

            def swiglu_stats(b, n):
                dve.wait_ge(hz_ready, 2 * b + 1 + n)
                dve.sem_inc(held, 1)
                for t in (2 * n, 2 * n + 1):
                    last = dve.bn_stats(st3[:, t, :], hz[:, t, :])
                last.then_inc(st3_ready, 1)

            def swiglu_norm(b, first, between=lambda: None):
                aggregate(st3, mv3, T, st3_ready, mv3_ready, 2 * b + 2, b + 1, True)
                dve.tensor_scalar(ve3[:], mv3[:, :, 1], LN_EPS, None, ALU.add).then_inc(ve3_ready, 1)
                dve.tensor_scalar(nm3[:], mv3[:, :, 0], -1.0, None, ALU.mult).then_inc(ve3_ready, 1)
                between()
                dve.wait_ge(rs3_ready, b + 1)
                dve.wait_ge(ve3_ready, 2 * b + 2)
                if not first:
                    dve.wait_ge(pe_zt, b)
                for t in range(T):
                    dve.tensor_scalar(zn[:, t, :], hz[:, t, :], nm3[:, t:t + 1], rs3[:, t:t + 1], ALU.add, ALU.mult)\
                       .then_inc(zn_ready, 1)

            def rows2_lo(b):
                for k in range(KD):
                    dve.wait_ge(xn2T_hi, 2 * b + 1 + k)
                    low(xn2T2[1][:, k, :], bank[k][:], xn2T2[0][:, k, :], xn2T_ready)

            def shared_out(b):
                for n in range(2):
                    dve.wait_ge(sh_ready, 2 * b + 3 + n)
                    dve.wait_ge(out_stored, 16 * b + 16)
                    dve.scalar_tensor_tensor(yo[:, 2 * n:2 * n + 2, :], halves(bank[5 + n]), tanh_g[:, 1:2],
                                             x1[:, bass.ds(b * T + 2 * n, 2), :], ALU.mult, ALU.add).then_inc(yo_ready, 1)

            step = [0]

            def link(sem_, ins):
                step[0] += 1
                ins.then_inc(sem_, 1)
                dve.wait_ge(sem_, step[0])

            for n in range(2):
                swiglu(0, n)
                swiglu_stats(0, n)
            swiglu_norm(0, True)
            residual(NB - 1, (bank[5], bank[6]))
            x1_stats(NB - 1)

            dve.wait_ge(in_idx, 16)
            for n, size in ((0, NB), (1, S)):
                v, neg = idf[:, n, :], idf[:, 2 + n, :]
                link(idx_step, dve.tensor_copy(v, idx_i[:, n, :]))
                link(idx_step, dve.tensor_scalar(neg, v, 0.0, float(size), ALU.is_lt, ALU.mult))
                link(idx_step, dve.tensor_tensor(v, v, neg, ALU.add))
                link(idx_step, dve.tensor_scalar(neg, v, 0.0, None, ALU.is_ge))
                link(idx_step, dve.scalar_tensor_tensor(idf[:, 4 + n, :], v, float(size - 1), neg, ALU.is_le, ALU.mult))
                link(idx_step, dve.tensor_scalar(v, v, 0.0, float(size - 1), ALU.max, ALU.min))
            link(idx_step, dve.scalar_tensor_tensor(idf[:, 6, :], idf[:, 0, :], float(S), idf[:, 1, :], ALU.mult, ALU.add))
            link(idx_step, dve.tensor_copy(gidx[:], idf[:, 6, :]))
            link(idx_step, dve.tensor_tensor(idf[:, 7, :], idf[:, 4, :], idf[:, 5, :], ALU.mult))
            link(idx_step, dve.tensor_scalar(idf[:, 7, :], idf[:, 7, :], -float(N), float(N), ALU.mult, ALU.add))
            link(idx_step, dve.tensor_tensor(idf[:, 6, :], idf[:, 6, :], idf[:, 7, :], ALU.add))
            dve.tensor_copy(sidx[:], idf[:, 6, :]).then_inc(idx_ready, 1)
            for e in range(E):
                dve.memset(rank_w[:, :, e], float(E - e)).then_inc(rank_ready, 1)

            with dve.Fori(1, NB - 1) as b:
                swiglu(b, 0)
                swiglu_stats(b, 0)
                swiglu(b, 1)
                rows2_lo(b + 1)
                swiglu_stats(b, 1)
                swiglu_norm(b, False, lambda: shared_out(b - 1))
            swiglu(NB - 1, 0)
            swiglu_stats(NB - 1, 0)
            swiglu(NB - 1, 1)
            swiglu_stats(NB - 1, 1)
            step[0] = 0
            dve.wait_ge(xg_in, 16 * MT)
            for t in range(MT):
                last = dve.bn_stats(stg[:, t, :], xg[:, t, :])
            link(dve_g, last)
            for t in range(MT):
                last = dve.bn_aggr(mvg[:, t, :], stg[:, t, :])
            link(dve_g, last)
            link(dve_g, dve.tensor_scalar(veg[:], mvg[:, :, 1], LN_EPS, None, ALU.add))
            link(dve_g, dve.tensor_scalar(nmg[:], mvg[:, :, 0], -1.0, None, ALU.mult))
            swiglu_norm(NB - 1, False, lambda: shared_out(NB - 2))
            dve.wait_ge(rsg_ready, 1)
            for t in range(MT):
                last = dve.tensor_scalar(xgn[:, t, :], xg[:, t, :], nmg[:, t:t + 1], rsg[:, t:t + 1], ALU.add, ALU.mult)
            last.then_inc(xgn_ready, 1)
            for k in range(KD):
                dve.wait_ge(xgT_hi, k + 1)
                low(xgT2[1][:, k, :], full[:, k, :], xgT2[0][:, k, :], xgT_ready)
            dve.wait_ge(pe_gate, 1)
            dve.tensor_tensor(lg[:], bank[7][:, 0:MT * (E + 1)].rearrange("p (t e) -> p t e", t=MT),
                              bc(row2(R_GB, E + 1), MT), ALU.add).then_inc(gate_added, 1)
            step[0] = 0
            dve.wait_ge(sc_ready, 1)
            dve.wait_ge(rank_ready, E)
            link(route_step, dve.tensor_tensor(sx[:], sc[:, :, 0:E], bc(row2(R_XB, E), MT), ALU.add))
            link(route_step, dve.reduce_max(mx[:], sx[:], AX_X))
            link(route_step, dve.tensor_tensor(eq[:], sx[:], bcl(mx[:], E), ALU.is_equal))
            link(route_step, dve.tensor_tensor(eq[:], eq[:], rank_w[:], ALU.mult))
            link(route_step, dve.reduce_max(m2[:], eq[:], AX_X))
            dve.tensor_tensor(oh[:], eq[:], bcl(m2[:], E), ALU.is_equal).then_inc(oh_ready, 1)
            dve.wait_ge(oh_ready, 1)
            for r in range(3):
                last = dve.tensor_copy(oh3[:, :, r, :], oh[:])
            last.then_inc(oh3_ready, 1)
            link(route_step, dve.tensor_tensor(sx[:], sc[:, :, 0:E], oh[:], ALU.mult))
            link(route_step, dve.reduce_sum(top[:], sx[:], AX_X))
            dve.tensor_tensor(dif[:], top[:], sc[:, :, E], ALU.subtract).then_inc(dif_ready, 1)
            shared_out(NB - 1)
            dve.wait_ge(swt_ready, 2)
            dve.tensor_scalar(cw[:], swt[:], tanh_g[:, 1:2], None, ALU.mult).then_inc(cw_ready, 1)
            dve.wait_ge(cw_ready, 1)
            dve.tensor_tensor(ohc[:], oh[:], bcl(cw[:, 0, :], E), ALU.mult).then_inc(ohc_ready, 1)
            dve.wait_ge(ohc_ready, 1)

            def select(t, banks, made, start, pick, sums, done):
                for j in range(EP):
                    dve.wait_ge(made, EP * t + j + 1)
                    for par in range(2):
                        src, slot = halves(banks(j))[:, par, :], sums[:, 2 * (t % 2) + par, :]
                        w = pick[:, t, 2 * j + par:2 * j + par + 1]
                        if j:
                            dve.wait_ge(done, 8 * t + 2 * j + par - 1)
                            ins = dve.scalar_tensor_tensor(slot, src, w, slot, ALU.mult, ALU.add)
                        elif par:
                            ins = dve.tensor_scalar(slot, src, w, None, ALU.mult)
                        else:
                            ins = dve.scalar_tensor_tensor(slot, src, w, start, ALU.mult, ALU.add)
                        ins.then_inc(done, 1)
                dve.wait_ge(done, 8 * t + 8)

            step[0] = 0

            def expert_hidden(t):
                i, even, odd = t % 2, acc[:, 2 * (t % 2), :], acc[:, 2 * (t % 2) + 1, :]
                dve.wait_ge(ebs_ready, t + 1)
                select(t, lambda j: bank[j], pe_hm, ebs[:, t, 0:2 * H], oh, acc, h_part)
                dve.tensor_tensor(even, even, odd, ALU.add).then_inc(hs_ready, 1)
                dve.wait_ge(hs_ready, t + 1)
                dve.wait_ge(sgm_ready, t + 1)
                link(dve_m, dve.tensor_tensor(hum[:, i, :], even[:, 0:H], sgm[:, i, :], ALU.mult))
                link(dve_m, dve.tensor_tensor(hzm[:, i, :], even[:, H:2 * H], hum[:, i, :], ALU.mult))
                link(dve_m, dve.bn_stats(stm[:, t, :], hzm[:, i, :]))
                link(dve_m, dve.bn_aggr(mvm[:, t, :], stm[:, t, :]))
                dve.tensor_scalar(vem[:, t:t + 1], mvm[:, t, 1:2], LN_EPS, None, ALU.add).then_inc(ve_m_ready, 1)
                link(dve_m, dve.tensor_scalar(nmm[:, t:t + 1], mvm[:, t, 0:1], -1.0, None, ALU.mult))

            def expert_norm(t):
                i = t % 2
                dve.wait_ge(rsm_ready, t + 1)
                if t >= 2:
                    dve.wait_ge(pe_ztm, t - 1)
                dve.tensor_scalar(znm[:, i, :], hzm[:, i, :], nmm[:, t:t + 1], rsm[:, t:t + 1], ALU.add, ALU.mult)\
                   .then_inc(znm_ready, 1)

            def combine(t):
                dve.wait_ge(base_ready, t + 1)
                select(t, lambda j: bank[5 + (EP * t + j) % 3], pe_ym, base[:, t, :], ohc, acc_y, y_part)
                dve.tensor_tensor(fin[:, t, :], acc_y[:, 2 * (t % 2), :], acc_y[:, 2 * (t % 2) + 1, :], ALU.add)\
                   .then_inc(fin_ready, 1)

            for t in range(MT):
                expert_hidden(t)
                expert_norm(t)
                if t:
                    combine(t - 1)
            combine(MT - 1)

        @block.gpsimd
        def _(pool):
            def norm_rows(b, ve, nm, ve_sem, dst, done, loads, free, free_total):
                pool.wait_ge(ve_sem, 2 * b + 2)
                pool.sem_inc(pool_held, 1)
                rows = bass.ds(b * T, T)
                pool.tensor_tensor(rs_cur[:], ve[:, rows], neg_half[:, 0:T], ALU.pow).then_inc(cur_ready, 1)
                pool.tensor_tensor(nm_cur[:], nm[:, rows], ones_sb[:, 0:T], ALU.mult).then_inc(cur_ready, 1)
                pool.wait_ge(x_cur_in, 16 * loads)
                pool.wait_ge(cur_ready, 2 * loads)
                if free is not None:
                    pool.wait_ge(free, free_total)
                pool.sem_inc(pool_held, 1)
                for t in range(T):
                    pool.tensor_scalar(dst[:, t, :], x_cur[:, t, :], nm_cur[:, t:t + 1], rs_cur[:, t:t + 1],
                                       ALU.add, ALU.mult).then_inc(done, 1)
                pool.wait_ge(done, 4 * b + 4)
                pool.sem_inc(pool_held, 1)

            def low(pair, m, b, hi_sem, done):
                pool.wait_ge(hi_sem, 2 * b + 1 + m)
                pool.tensor_tensor(pair[1][:, m, :], full[:, m, :], pair[0][:, m, :].bitcast(F32), ALU.subtract)\
                    .then_inc(done, 1)

            def attention(b, first):
                if first:
                    pool.wait_ge(consts_ready, 2)
                else:
                    pool.wait_ge(in_ctx, 16 * b + 16)
                    pool.wait_ge(pe_kf, 8 * b - 7)
                    pool.sem_inc(pool_held, 1)
                    pool.tensor_scalar(ctx2[0][:], ctx_sb[:], 1.0, 0.0, ALU.mult, ALU.add).then_inc(ctx_hi, 1)
                    pool.wait_ge(ctx_hi, b)
                    pool.tensor_tensor(ctx2[1][:], ctx_sb[:], ctx2[0][:].bitcast(F32), ALU.subtract).then_inc(ctx_ready, 1)
                norm_rows(b, ve1, nm1, ve1_ready, xn, xn_ready, b + 1, None if first else pe_xt, 2 * b)
                order = ((kT2, kT_hi, kT_ready), (xnT2, xnT_hi, xnT_ready))
                for pair, hi_sem, done in (*(order if first else order[::-1]), (qT2, qT_hi, qT_ready)):
                    for m in range(KD):
                        low(pair, m, b, hi_sem, done)
                if first:
                    pool.wait_ge(tbo_ready, 1)
                rows = bass.ds(b * T, T)
                pool.tensor_tensor(xs[:, rows, :], xs[:, rows, :], bc(tbo[:], T), ALU.add).then_inc(xb_ready, 1)
                pool.wait_ge(kf_ready, 8 * b + 4)
                pool.tensor_tensor(kf_sum[:], kf[:, 0, :], kf[:, 1, :], ALU.add).then_inc(kfs_part, 1)
                for t in (2, 3):
                    pool.wait_ge(kfs_part, 2 * b + t - 1)
                    pool.wait_ge(kf_ready, 8 * b + 2 * t + 2)
                    pool.tensor_tensor(kf_sum[:], kf_sum[:], kf[:, t, :], ALU.add)\
                        .then_inc(kfs_part if t == 2 else kfs_ready, 1)

            attention(0, True)
            with pool.Fori(1, NB) as b:
                attention(b, False)

            def norm2(b):
                norm_rows(b, ve2, nm2, ve2_ready, xn2, xn2_ready, NB + b + 1, pe_x2t if b else pe_xt, 2 * b if b else 2 * NB)

            def rs3_pow(b):
                pool.wait_ge(ve3_ready, 2 * b + 2)
                pool.tensor_tensor(rs3[:], ve3[:], neg_half[:, 0:T], ALU.pow).then_inc(rs3_ready, 1)

            def z_low(b):
                pool.wait_ge(z_hi, b + 1)
                pool.tensor_tensor(zT2[1], z_full, zT2[0].bitcast(F32), ALU.subtract).then_inc(zT_ready, 1)

            norm2(0)
            for m in range(KD):
                low(xn2T2, m, 0, xn2T_hi, xn2T_ready)
            norm2(1)
            for m in range(KD):
                low(xn2T2, m, 1, xn2T_hi, xn2T_ready)
            rs3_pow(0)
            norm2(2)
            z_low(0)
            pool.wait_ge(idx_ready, 1)
            pool.wait_ge(x1_stored, 16 * NB)
            for t in range(MT):
                pool.indirect_dma_start(xg[:, t, :], None, scratch_x1, bass.IndirectOffsetOnAxis(ap=gidx[:, t:t + 1], axis=0))\
                    .then_inc(xg_in, 16)
            rs3_pow(1)
            norm2(3)
            z_low(1)
            rs3_pow(2)
            z_low(2)
            pool.wait_ge(dve_g, 3)
            pool.tensor_tensor(rsg[:], veg[:], neg_half[:, 0:MT], ALU.pow).then_inc(rsg_ready, 1)
            rs3_pow(3)
            z_low(3)

            def expert_scale(t):
                pool.wait_ge(ve_m_ready, t + 1)
                pool.tensor_tensor(rsm[:, t:t + 1], vem[:, t:t + 1], neg_half[:, 0:1], ALU.pow).then_inc(rsm_ready, 1)

            def z_expert_low(t):
                pool.wait_ge(zm_hi, t + 1)
                pool.tensor_tensor(zTm2[1][:, t % 2, :], zfm[:, t % 2, :], zTm2[0][:, t % 2, :].bitcast(F32),
                                   ALU.subtract).then_inc(zTm_ready, 1)

            def base_rows(t):
                pool.tensor_scalar(base[:, t, :], shg[:, t, :], cw[:, 1, t:t + 1], 0.0, ALU.mult, ALU.add)\
                    .then_inc(base_step, 1)
                pool.wait_ge(ebs_ready, t + 1)
                pool.tensor_scalar(ebs[:, t, 2 * H:2 * H + D], ebs[:, t, 2 * H:2 * H + D], cw[:, 0, t:t + 1], 0.0,
                                   ALU.mult, ALU.add).then_inc(base_step, 1)
                pool.wait_ge(base_step, 3 * t + 2)
                pool.tensor_tensor(base[:, t, :], base[:, t, :], xg[:, t, :], ALU.add).then_inc(base_step, 1)
                pool.wait_ge(base_step, 3 * t + 3)
                pool.tensor_tensor(base[:, t, :], base[:, t, :], ebs[:, t, 2 * H:2 * H + D], ALU.add)\
                    .then_inc(base_ready, 1)

            pool.wait_ge(sh_stored, 16 * NB + 16)
            for t in range(MT):
                pool.indirect_dma_start(shg[:, t, :], None, scratch_sh, bass.IndirectOffsetOnAxis(ap=gidx[:, t:t + 1], axis=0))\
                    .then_inc(shg_in, 16)
            expert_scale(0)
            z_expert_low(0)
            pool.wait_ge(cw_ready, 1)
            pool.wait_ge(shg_in, 16 * MT)
            base_rows(0)
            for t in range(1, MT):
                expert_scale(t)
                base_rows(t)
                z_expert_low(t)
            pool.wait_ge(out_stored, 16 * NB + 16)
            for t in range(MT):
                pool.wait_ge(fin_ready, t + 1)
                pool.indirect_dma_start(out, bass.IndirectOffsetOnAxis(ap=sidx[:, t:t + 1], axis=0), fin[:, t, :], None,
                                        bounds_check=N - 1, oob_is_err=False).then_inc(scattered, 16)
            pool.wait_ge(scattered, 16 * MT)


def kernel(**inputs):
    import numpy as np
    import concourse.bacc as bacc
    from concourse.bass_utils import run_bass_kernel_spmd as run

    a = {k.replace("L0_xattn_", "").replace("L0_ffn_", ""): np.asarray(v) for k, v in inputs.items()}
    f32 = np.float32
    NB, S, D = a["x"].shape
    HD, FD = a["Wf"].shape
    E, H = a["eb1"].shape
    M = a["index_b"].shape[0]
    wf = np.zeros((P, 8 * FD), f32)
    for h in range(8):
        wf[HD * h:HD * h + HD, FD * h:FD * h + FD] = a["Wf"]
    rows_a = np.concatenate([a["bv"], a["bf"], a["bo"], a["g_xattn"], a["g_ffn"]])[None, :]
    rows_b = np.concatenate([a["sb1"], a["sb2"], a["sb3"], a["eg_b"], a["sg_b"], a["exp_bias"]])[None, :]
    cols = np.stack([a["bq"][:P], a["bq"][P:], a["bk"][:P], a["bk"][P:], np.tile(a["bf"], 2), a["s_ln_g"],
                     a["s_ln_b"], a["sel_ln_g"], a["sel_ln_b"]], axis=1)
    up = np.concatenate([a["ew1"], a["ew2"]], axis=1).transpose(2, 0, 1).reshape(2, P, E // 2, 4 * H)
    up = up.transpose(1, 0, 2, 3).reshape(P, E, 4 * H)
    down = a["ew3"].transpose(2, 0, 1).reshape(P, E // 2, 2 * D)
    part = np.arange(P)
    part_mask = np.stack([part < 3, -1 * (part >= 1), -1 * (part >= 2), -1 * (part >= E), -1 * (part >= 2 * E)],
                         axis=1).astype(f32)
    arrays = {
        "x": a["x"].reshape(NB * S, D),
        "ctx_t": a["ctx_1024"].reshape(NB * S, D).T,
        "w_q": a["Wq"], "w_k": a["Wk"], "w_v": a["Wv"], "w_o": a["Wo"], "w_f_diag": wf, "rows_a": rows_a, "rows_b": rows_b,
        "cols": cols,
        "sw12": np.concatenate([a["sw1"].T, a["sw2"].T], axis=1),
        "sw3": a["sw3"].T,
        "w_gate": np.concatenate([a["eg_w"], a["sg_w"]], axis=0).T,
        "ew": np.concatenate([up, down], axis=1),
        "eb": np.concatenate([a["eb1"], a["eb2"], a["eb3"]], axis=1),
        "index": np.stack([a["index_b"].reshape(M // P, P).T, a["index_t"].reshape(M // P, P).T], axis=1),
        "ident": np.eye(P, dtype=f32),
        "part_mask": part_mask,
    }
    arrays = {f"in_{k}": np.ascontiguousarray(v) for k, v in arrays.items()}
    nc = bacc.Bacc("TRN2", target_bir_lowering=False, num_devices=1)
    args = [nc.dram_tensor(k, v.shape, mybir.dt.from_np(v.dtype), kind="ExternalInput").ap() for k, v in arrays.items()]
    out = nc.dram_tensor("out", (NB * S, D), F32, kind="ExternalOutput").ap()
    flamingo_block(nc, *args, out)
    r = run(nc, [arrays], core_ids=[0])
    return r.results[0]["out"].reshape(NB, S, D)
```

```python
from contextlib import ExitStack

import concourse.bass as bass
from concourse import mybir

P = 128
F32 = mybir.dt.float32
F32R = mybir.dt.float32r
BF16 = mybir.dt.bfloat16
I32 = mybir.dt.int32
U32 = mybir.dt.uint32
ALU = mybir.AluOpType
ACT = mybir.ActivationFunctionType
AX_X = mybir.AxisListType.X
LN_EPS = 1e-5
ATT_EPS = 1e-8


def flamingo_block(nc, x, ctx_t, w_q, w_k, w_v, w_o, w_f_diag, rows_a, rows_b, cols, sw12, sw3, w_gate, ew, eb, index,
                   ident, part_mask, out):
    NB, S, D = 4, 512, x.shape[1]
    N = NB * S
    T = S // P
    KD = D // P
    HD, FD = 16, w_f_diag.shape[1] // 8
    PAIRS = D // (2 * HD)
    PG = PAIRS // KD
    H = sw3.shape[0]
    E = w_gate.shape[1] - 1
    EP = E // 2
    MT = index.shape[2]
    M = MT * P
    EC = ew.shape[1]
    ECB = EC // NB
    assert 2 * FD == P and H == P and PG == 4 and T == 4 and MT == 4 and KD == 2 and ECB * NB == EC

    R_BV, R_BF, R_BO, R_GX = 0, D, D + FD, 2 * D + FD
    R_SB, R_GB, R_XB = 0, 2 * H + D, 2 * H + D + E + 1
    C_BQ, C_BK, C_BF, C_SG, C_SB, C_EG, C_EB = 0, 2, 4, 5, 6, 7, 8

    scratch_x1 = nc.dram_tensor("scratch_x1", (N, D), F32).ap()
    scratch_sh = nc.dram_tensor("scratch_sh", (N, D), F32).ap()

    def by_tile(a):
        return a.rearrange("(g p) d -> p g d", p=P)

    def by_k(a):
        return a.rearrange("(k p) n -> p k n", p=P)

    with ExitStack() as ctx:
        def sb(name, shape, dt=F32):
            return ctx.enter_context(nc.sbuf_tensor(name, shape, dt))

        def sb_split(name, shape):
            return sb(name + "_hi", shape, F32R), sb(name + "_lo", shape, F32R)

        def sem(name):
            return ctx.enter_context(nc.semaphore(name))

        wq2, wk2, wv2, wo2 = (sb_split(n, [P, KD, D]) for n in ("wq", "wk", "wv", "wo"))
        wf2 = sb_split("wf", [P, 8 * FD])
        sw12_2 = sb_split("sw12s", [P, KD, 2 * H])
        sw3_2 = sb_split("sw3s", [P, D])
        ew2 = sb_split("ews", [P, EC, 512])
        rows_sb = sb("rows_sb", [P, rows_a.shape[1]])
        rows2_sb = sb("rows2_sb", [P, rows_b.shape[1]])
        cols_sb = sb("cols_sb", [P, cols.shape[1]])
        pm_sb = sb("pm_sb", [P, part_mask.shape[1]])
        wg_sb = sb("wg_sb", [P, KD, E + 1])
        ident_sb = sb("ident_sb", [P, P])
        ident_bf = sb("ident_bf", [P, P], BF16)
        ones_sb = sb("ones_sb", [P, 2 * HD])
        ones3 = sb("ones3", [P, P], BF16)
        bias3 = sb("bias3", [P, 2 * H + D], BF16)
        eb3p = sb("eb3p", [3 * E, 512], BF16)
        eb_st = sb("eb_st", [3 * E, 512])
        neg_half = sb("neg_half", [P, 16])
        att_eps = sb("att_eps", [P, 1])
        tanh_g = sb("tanh_g", [P, 2])
        table = sb("table", [P, 1])
        tbo = sb("tbo", [P, D])
        xs = sb("xs", [P, NB * T, D])
        x1 = xs
        ctx_sb = sb("ctx_sb", [P, KD, S])
        ctx2 = sb_split("ctx", [P, KD, S])
        kT2 = sb_split("kT", [P, KD, S])
        vv = sb("vv", [P, T, D])
        x_cur = sb("x_cur", [P, T, D])
        nm_cur = sb("nm_cur", [P, T])
        rs_cur = sb("rs_cur", [P, T])
        xn = sb("xn", [P, T, D])
        xnT2 = sb_split("xnT", [P, KD, S])
        qT2 = sb_split("qT", [P, KD, S])
        full = sb("full", [P, KD, S])
        kf = sb("kf", [P, T, PAIRS * P])
        kf_sum = sb("kf_sum", [P, PAIRS * P])
        qf = sb("qf", [P, PAIRS, S])
        kvs = sb("kvs", [P, 2 * KD, P])
        kvd = sb("kvd", [P, 2 * KD, PG, 2 * HD])
        at = sb("at", [P, KD, S])
        aT2 = ctx2
        ew_st = sb("ew_st", [P, ECB, 512])
        st1 = sb("st1", [P, NB * T, 6])
        mv1 = sb("mv1", [P, NB * T, 2])
        ve = sb("ve", [P, 2 * NB * T])
        nm = sb("nm", [P, 2 * NB * T])
        st2 = sb("st2", [P, T, 6])
        mv2 = sb("mv2", [P, T, 2])
        stage = qf[:]
        sg, hu, hz, zn = (kf[:, 0, 512 * 0:512 * 1], kf[:, 0, 512:1024], kf[:, 1, 0:512], kf[:, 1, 512:1024])
        sg, hu, hz, zn = (a.rearrange("p (t h) -> p t h", t=T) for a in (sg, hu, hz, zn))
        sh, yo = (kf[:, n, :].rearrange("p (t d) -> p t d", t=T) for n in (2, 3))
        z_full = (kf_sum[:, 0:S], kf_sum[:, S:2 * S])
        zT2 = tuple(tuple(a[:, n, :] for a in aT2) for n in range(2))
        st3 = sb("st3", [P, T, 6])
        mv3 = sb("mv3", [P, T, 2])
        ve3 = sb("ve3", [P, T])
        nm3 = sb("nm3", [P, T])
        rs3 = sb("rs3", [P, T])
        xg, shg = (qf[:, 2 * n:2 * n + 2, :].rearrange("p a n -> p (a n)").rearrange("p (t d) -> p t d", t=MT)
                   for n in range(2))
        ebs = qf[:, 4:8, :]
        xgn, base, fin = xs[:, 0:4, :], xs[:, 4:8, :], xs[:, 8:12, :]
        acc_h, acc_y = xs[:, 12:16, :], ctx_sb[:].rearrange("p k (n d) -> p (k n) d", d=D)
        part_h = (x_cur[:], at[:].rearrange("p k (n d) -> p (k n) d", d=D))
        part_y = (xn[:], ew_st[:, 0:2, :].rearrange("p k (n d) -> p (k n) d", d=D))
        ffn_rows2 = (xnT2, kT2, xnT2, kT2)
        xgT2 = kT2
        sgm, hum, hzm, znm = (vv[:, n, :].rearrange("p (i h) -> p i h", i=2) for n in range(4))
        zfm = kf_sum[:, S:S + 2 * P].rearrange("p (i q) -> p i q", i=2)
        zTm2 = tuple(a[:, 1, :].rearrange("p (i q) -> p i q", q=P) for a in aT2)
        idx_i = sb("idx_i", [P, 2, MT], I32)
        idf = sb("idf", [P, 8, MT])
        gidx = sb("gidx", [P, MT], U32)
        sidx = sb("sidx", [P, MT], U32)
        stg = sb("stg", [P, MT, 6])
        mvg = sb("mvg", [P, MT, 2])
        veg = sb("veg", [P, MT])
        nmg = sb("nmg", [P, MT])
        rsg = sb("rsg", [P, MT])
        lg = sb("lg", [P, MT, E + 1])
        sc = sb("sc", [P, MT, E + 1])
        sx = sb("sx", [P, MT, E])
        rank_w = sb("rank_w", [P, MT, E])
        eq = sb("eq", [P, MT, E])
        mx = sb("mx", [P, MT])
        m2 = sb("m2", [P, MT])
        oh = sb("oh", [P, MT, E])
        oh3 = sb("oh3", [P, MT, 3, E], BF16)
        top = sb("top", [P, MT])
        dif = sb("dif", [P, MT])
        swt = sb("swt", [P, 2, MT])
        cw = sb("cw", [P, 2, MT])
        ohT = sb("ohT", [3 * E, MT, P], BF16)
        stm = sb("stm", [P, MT, 6])
        mvm = sb("mvm", [P, MT, 2])
        vem = sb("vem", [P, MT])
        nmm = sb("nmm", [P, MT])
        rsm = sb("rsm", [P, MT])

        bank = [ctx.enter_context(nc.psum_tensor(f"bank{i}", [P, 512], F32)) for i in range(8)]

        down_bank = [bank[n] for n in (5, 6, 7, 5, 6, 7, 5, 6, 0, 1, 2, 3, 5, 6, 7, 0)]
        down_before = [max((v for v in range(u) if down_bank[v] is down_bank[u]), default=None) for u in range(16)]

        def halves(b):
            return b[:].rearrange("p (t d) -> p t d", t=2)

        def quarters(b):
            return b[:].rearrange("p (t d) -> p t d", t=4)

        in_wk, in_ctx_a, in_ctx_b, in_ctx, in_pm, in_wv, in_x0, in_x, in_cols, in_rows, in_id, in_wq, in_wf, in_wo, in_ffn, in_moe, in_wg, in_idx, in_ew = (
            sem(n) for n in ("in_wk", "in_ctx_a", "in_ctx_b", "in_ctx", "in_pm", "in_wv", "in_x0", "in_x", "in_cols", "in_rows", "in_id", "in_wq",
                             "in_wf", "in_wo", "in_ffn", "in_moe", "in_wg", "in_idx", "in_ew"))
        x1_stored, sh_stored, out_stored, xg_in, shg_in, scattered = (
            sem(n) for n in ("x1_stored", "sh_stored", "out_stored", "xg_in", "shg_in", "scattered"))
        consts_ready, tanh_ready, tbo_ready, bf_consts, parts = (
            sem(n) for n in ("consts_ready", "tanh_ready", "tbo_ready", "bf_consts", "parts"))
        st1_ready, mv1_ready, ve_ready = (sem(n) for n in ("st1_ready", "mv1_ready", "ve_ready"))
        x_cur_in, cur_ready, held, pool_held, act_held = (
            sem(n) for n in ("x_cur_in", "cur_ready", "held", "pool_held", "act_held"))
        (w_hi, w_lo, ctx0_hi, ctx_hi, ctx_ready, ew_hi, ew_lo, kT_hi, kT_ready, xnT_hi, xnT_ready, qT_hi, qT_ready,
         aT_hi, aT_ready) = (
            sem(n) for n in ("w_hi", "w_lo", "ctx0_hi", "ctx_hi", "ctx_ready", "ew_hi", "ew_lo", "kT_hi", "kT_ready",
                             "xnT_hi", "xnT_ready", "qT_hi", "qT_ready", "aT_hi", "aT_ready"))
        pe_k, pe_v, pe_xt, pe_q, pe_kf, pe_qf, pe_kv, pe_kvt, pe_den, pe_num, pe_wo = (
            sem(n) for n in ("pe_k", "pe_v", "pe_xt", "pe_q", "pe_kf", "pe_qf", "pe_kv", "pe_kvt", "pe_den", "pe_num", "pe_wo"))
        (xn_ready, xb_ready, v_ready, kf_added, kf_ready, kfs_part, kfs_ready, qf_ready, kvs_ready, kvd_zero, kvd_ready,
         den_ready, rden_ready, at_ready, x1_ready) = (
            sem(n) for n in ("xn_ready", "xb_ready", "v_ready", "kf_added", "kf_ready", "kfs_part", "kfs_ready",
                             "qf_ready", "kvs_ready", "kvd_zero", "kvd_ready", "den_ready", "rden_ready", "at_ready",
                             "x1_ready"))
        st2_ready, mv2_ready = (sem(n) for n in ("st2_ready", "mv2_ready"))
        pe_h, pe_zt, pe_y, rows_lo_ready = (sem(n) for n in ("pe_h", "pe_zt", "pe_y", "rows_lo_ready"))
        last_xn_ready = sem("last_xn_ready")
        (sg_ready, hu_ready, hz_ready, st3_ready, mv3_ready, ve3_ready, rs3_ready,
         zn_ready, z_hi, zT_ready, sh_ready, yo_ready) = (
            sem(n) for n in ("sg_ready", "hu_ready", "hz_ready", "st3_ready",
                             "mv3_ready", "ve3_ready", "rs3_ready", "zn_ready", "z_hi", "zT_ready", "sh_ready",
                             "yo_ready"))
        idx_step, idx_ready, dve_g, rsg_ready, xgn_ready, pe_xgt, xgT_hi, xgT_ready, pe_gate, gate_added, sc_ready = (
            sem(n) for n in ("idx_step", "idx_ready", "dve_g", "rsg_ready", "xgn_ready", "pe_xgt", "xgT_hi", "xgT_ready",
                             "pe_gate", "gate_added", "sc_ready"))
        rank_ready, route_step, dif_ready, swt_ready, oh_ready, oh3_ready, pe_oht, ohT_ready, pe_eb, ebs_ready = (
            sem(n) for n in ("rank_ready", "route_step", "dif_ready", "swt_ready", "oh_ready", "oh3_ready", "pe_oht",
                             "ohT_ready", "pe_eb", "ebs_ready"))
        cw_ready, base_step = sem("cw_ready"), sem("base_step")
        (h_pick, h_two, h_half, y_pick, y_two, y_half, f_step) = (
            sem(n) for n in ("h_pick", "h_two", "h_half", "y_pick", "y_two", "y_half", "f_step"))
        h_sum, y_sum, xg_full = sem("h_sum"), sem("y_sum"), sem("xg_full")
        (pe_hm, h_part, hs_ready, sgm_ready, dve_m, ve_m_ready, rsm_ready, znm_ready, pe_ztm, zm_hi, zTm_ready,
         pe_ym, y_part, base_ready, fin_ready) = (
            sem(n) for n in ("pe_hm", "h_part", "hs_ready", "sgm_ready", "dve_m", "ve_m_ready", "rsm_ready", "znm_ready",
                             "pe_ztm", "zm_hi", "zTm_ready", "pe_ym", "y_part", "base_ready", "fin_ready"))

        block = ctx.enter_context(nc.Block())

        def row(a, n):
            return rows_sb[:, a:a + n]

        def row2(a, n):
            return rows2_sb[:, a:a + n]

        def col(a):
            return cols_sb[:, a:a + 1]

        def bc(a, n):
            return a.unsqueeze(1).to_broadcast([P, n, a.shape[1]])

        def bcl(a, n):
            return a.unsqueeze(2).to_broadcast([P, a.shape[1], n])

        def staged(n, like):
            a = stage[:, n, :]
            return a.rearrange("p (k n) -> p k n", k=like.shape[1]) if len(like.shape) == 3 else a[:, 0:like.shape[1]]

        SPLITS = [(staged(n, w[0]), w, s_, v) for n, (w, s_, v) in enumerate(
            ((wk2, in_wk, 16), (wv2, in_wv, 16), (wq2, in_wq, 16), (wf2, in_wf, 16), (wo2, in_wo, 16),
             (sw12_2, in_ffn, 32), (sw3_2, in_ffn, 32)))]
        W_K, W_V, W_Q, W_F, W_O, W_SW12, W_SW3 = (n + 1 for n in range(7))

        @block.sync
        def _(sp):
            ctx_v = by_k(ctx_t)
            xv = by_tile(x)
            sp.dma_start(SPLITS[0][0], by_k(w_k)).then_inc(in_wk, 16)
            for k in range(KD):
                sp.dma_start(ctx_sb[:, k, :], ctx_v[:, k, 0:S]).then_inc((in_ctx_a, in_ctx_b)[k], 16)
            sp.dma_start(xs[:, 0:T, :], xv[:, 0:T, :]).then_inc(in_x0, 16)
            for n in range(1, 4):
                src = (w_v, w_q, w_f_diag)[n - 1]
                sp.dma_start(SPLITS[n][0], src if n == 3 else by_k(src)).then_inc(SPLITS[n][2], 16)
            sp.dma_start(rows_sb[:], rows_a.partition_broadcast(P)).then_inc(in_rows, 16)
            sp.dma_start(rows2_sb[:], rows_b.partition_broadcast(P)).then_inc(in_moe, 16)
            sp.dma_start(SPLITS[4][0], by_k(w_o)).then_inc(in_wo, 16)
            sp.dma_start(SPLITS[5][0], by_k(sw12)).then_inc(in_ffn, 16)
            sp.dma_start(SPLITS[6][0], sw3).then_inc(in_ffn, 16)
            for n in range(3):
                sp.dma_start(eb_st[n * E:n * E + E, :], eb).then_inc(in_moe, 16)
            sp.dma_start(xs[:, T:NB * T, :], xv[:, T:NB * T, :]).then_inc(in_x, 16)
            sp.dma_start(ew_st[:], ew[:, 0:ECB, :]).then_inc(in_ew, 16)
            sp.dma_start(wg_sb[:], by_k(w_gate)).then_inc(in_wg, 16)
            s1, s2, o = by_tile(scratch_x1), by_tile(scratch_sh), by_tile(out)

            def load_cur(b):
                sp.dma_start(x_cur[:], xs[:, bass.ds(b * T, T), :]).then_inc(x_cur_in, 16)

            def load_batch(b):
                sp.wait_ge(ctx_ready, b + 1)
                sp.dma_start(ctx_sb[:], ctx_v[:, :, bass.ds(b * S, S)]).then_inc(in_ctx, 16)
                sp.wait_ge(ew_lo, ECB * b)
                sp.dma_start(ew_st[:], ew[:, bass.ds(b * ECB, ECB), :]).then_inc(in_ew, 16)

            def store_x1(b):
                sp.wait_ge(x1_ready, 2 * b + 2)
                sp.dma_start(s1[:, bass.ds(b * T, T), :], x1[:, bass.ds(b * T, T), :]).then_inc(x1_stored, 16)

            sp.wait_ge(in_x, 16)
            load_cur(1)
            with sp.Fori(1, NB - 1) as b:
                load_batch(b)
                sp.wait_ge(xn_ready, 4 * b + 4)
                load_cur(b + 1)
            load_batch(NB - 1)
            store_x1(0)
            sp.wait_ge(xn_ready, 4 * NB)
            load_cur(0)
            with sp.Fori(1, NB) as b:
                store_x1(b)
            with sp.Fori(0, NB) as b:
                sp.wait_ge(sh_ready, 2 * b + 4)
                sp.dma_start(s2[:, bass.ds(b * T, T), :], sh).then_inc(sh_stored, 16)
                sp.wait_ge(yo_ready, 2 * b + 4)
                sp.dma_start(o[:, bass.ds(b * T, T), :], yo).then_inc(out_stored, 16)
            sp.wait_ge(scattered, 16 * MT)

        @block.tensor
        def _(pe):
            def mm3(dst, lhs, rhs, start, stop):
                pe.matmul(dst, lhs[0], rhs[0], start=start, stop=False)
                pe.matmul(dst, lhs[1], rhs[0], start=False, stop=False)
                return pe.matmul(dst, lhs[0], rhs[1], start=False, stop=stop)

            def cut(pair, *at):
                return tuple(a[at] for a in pair)

            ALL = slice(None)

            def tok(t):
                return slice(t * P, (t + 1) * P)

            def transposes(src, dst, k, done):
                for t in range(T):
                    last = pe.transpose(dst[:, t * P:(t + 1) * P], src[:, t, k * P:(k + 1) * P], ident_sb[:])
                last.then_inc(done, 1)

            def rows_t(n, waits, into=(bank[0], bank[1]), last_batch=False):
                if last_batch:
                    pe.wait_ge(last_xn_ready, T)
                else:
                    pe.wait_ge(xn_ready, 4 * n + 4)
                for k in range(KD):
                    if waits:
                        pe.wait_ge(xnT_hi, 2 * n - 1 + k)
                    transposes(xn, into[k], k, pe_xt)

            def out_proj(b, dsts):
                pe.wait_ge(aT_ready, 2 * b + 2)
                for n, dst in enumerate(dsts):
                    for t in (2 * n, 2 * n + 1):
                        for k in range(KD):
                            last = mm3(halves(dst)[:, t % 2, :], cut(aT2, ALL, k, tok(t)), cut(wo2, ALL, k),
                                       k == 0, k == KD - 1)
                    last.then_inc(pe_wo, 1)

            def key_features(b, j):
                t, c = j // 2, j % 2
                mm3(bank[2 + j % 4][:], cut(kT2, ALL, c, tok(t)), cut(wf2, ALL), True, True).then_inc(pe_kf, 1)

            def query_features(b, p):
                if p < 4:
                    pe.wait_ge(kf_added, 8 * b + p + 5)
                else:
                    pe.wait_ge(qf_ready, 8 * b + p - 3)
                mm3(bank[2 + p % 4][:], cut(wf2, ALL, slice((p % PG) * P, (p % PG + 1) * P)), cut(qT2, ALL, p // PG),
                    True, True).then_inc(pe_qf, 1)

            def attention(b, first):
                if first:
                    pe.wait_ge(w_lo, W_K)
                if not first:
                    pe.wait_ge(ctx_ready, b + 2)
                for k in range(KD):
                    if first:
                        pe.wait_ge(ctx_ready, k + 1)
                    for m in range(KD):
                        last = mm3(bank[6 + m][:], cut(wk2, ALL, k, tok(m)), cut(ctx2, ALL, k), k == 0, k == KD - 1)
                        if k == KD - 1:
                            last.then_inc(pe_k, 1)
                if first:
                    pe.wait_ge(w_lo, W_V)
                for n in range(2):
                    if not first:
                        pe.wait_ge(xnT_hi, 2 * b + 1 + n)
                    for t in (2 * n, 2 * n + 1):
                        for k in range(KD):
                            last = mm3(halves(bank[n])[:, t % 2, :], cut(ctx2, ALL, k, tok(t)), cut(wv2, ALL, k),
                                       k == 0, k == KD - 1)
                    last.then_inc(pe_v, 1)
                if first:
                    pe.wait_ge(in_id, 16)
                    rows_t(0, False, (bank[4], bank[5]))
                    pe.wait_ge(w_lo, W_F)
                    pe.wait_ge(kT_ready, 2)
                    key_features(b, 0)
                    key_features(b, 1)
                if first:
                    pe.wait_ge(w_lo, W_Q)
                pe.wait_ge(xnT_ready, 2 * b + 2)
                for m in range(KD):
                    pe.wait_ge(kT_hi, 2 * b + 1 + m)
                    for k in range(KD):
                        last = mm3(bank[6 + m][:], cut(wq2, ALL, k, tok(m)), cut(xnT2, ALL, k), k == 0, k == KD - 1)
                    last.then_inc(pe_q, 1)
                if not first:
                    pe.wait_ge(kT_ready, 2 * b + 2)
                    for j in range(2):
                        pe.wait_ge(at_ready, 2 * b - 1)
                        key_features(b, j)
                    pe.wait_ge(v_ready, 2 * b + 2)
                    out_proj(b - 1, (bank[0], bank[1]))
                    pe.wait_ge(at_ready, 2 * b)
                for j in range(2, 2 * T):
                    if j >= 4:
                        pe.wait_ge(kf_added, 8 * b + j - 3)
                    key_features(b, j)
                pe.wait_ge(qT_ready, 2 * b + 2)
                query_features(b, 0)
                query_features(b, 1)
                pe.wait_ge(kf_ready, 8 * b + 8)
                pe.wait_ge(v_ready, 2 * b + 2)
                if first:
                    pe.wait_ge(consts_ready, 2)
                for c in range(KD):
                    for t in range(T):
                        for g in range(PG):
                            p = PG * c + g
                            pe.matmul(quarters(bank[6])[32 * g:32 * g + 32, c, :], vv[:, t, 32 * p:32 * p + 32],
                                      kf[:, t, P * p:P * (p + 1)], start=(t == 0), stop=(t == T - 1))
                for p in range(2, 6):
                    query_features(b, p)
                pe.wait_ge(kfs_ready, b + 1)
                for c in range(KD):
                    for g in range(PG):
                        p = PG * c + g
                        last = pe.matmul(quarters(bank[6])[32 * g:32 * g + 32, KD + c, :], ones_sb[:],
                                         kf_sum[:, P * p:P * (p + 1)], start=True, stop=True)
                last.then_inc(pe_kv, 1)
                query_features(b, 6)
                pe.wait_ge(kvs_ready, b + 1)
                for n in range(2 * KD):
                    last = pe.transpose(quarters(bank[6])[:, n, :], kvs[:, n, :], ident_sb[:])
                last.then_inc(pe_kvt, 1)
                query_features(b, 7)
                if not first:
                    pe.wait_ge(x1_ready, 2 * b)
                rows_t(b + 1, False)
                pe.wait_ge(kvd_ready, 2 * b + 2)
                for n in (1, 0):
                    for c in range(KD):
                        if n:
                            pe.wait_ge(qf_ready, 8 * b + 6 + 2 * c)
                        for g in range(PG):
                            last = pe.matmul(bank[2 + 2 * c + n][32 * g:32 * g + 32, :], kvd[:, KD * n + c, g, :],
                                             qf[:, PG * c + g, :], start=True, stop=True)
                        last.then_inc(pe_den if n else pe_num, 1)

            attention(0, True)
            pe.wait_ge(w_lo, W_O)
            with pe.Fori(1, NB) as b:
                attention(b, False)

            def bias(dst, at_):
                pe.matmul(dst, ones3[:], bias3[:, at_:at_ + 256], start=True, stop=False)

            def ffn_up(b, n):
                for t in (2 * n, 2 * n + 1):
                    dst = halves(bank[6 + n])[:, t % 2, :]
                    bias(dst, R_SB)
                    for k in range(KD):
                        last = mm3(dst, cut(ffn_rows2[b], ALL, k, tok(t)), cut(sw12_2, ALL, k), False, k == KD - 1)
                last.then_inc(pe_h, 1)

            def up_again(b):
                if b < NB - 1:
                    pe.wait_ge(xnT_ready, 2 * NB + 2 * b + 2)
                else:
                    pe.wait_ge(rows_lo_ready, KD)
                for n in range(2):
                    pe.wait_ge(hz_ready, 2 * b - 1 + n)
                    ffn_up(b, n)

            def z_t(b):
                if b:
                    pe.wait_ge(z_hi, b)
                pe.wait_ge(zn_ready, 4 * b + 4)
                for t in range(T):
                    last = pe.transpose(bank[4][:, t * P:(t + 1) * P], zn[:, t, :], ident_sb[:])
                last.then_inc(pe_zt, 1)

            def ffn_down(b, pairs=(0, 1)):
                pe.wait_ge(zT_ready, b + 1)
                pe.wait_ge(x1_ready, 2 * NB)
                for n in pairs:
                    pe.wait_ge(sh_ready, 2 * b + 1 + n)
                    pe.wait_ge(yo_ready, 2 * b + 1 + n)
                    for t in (2 * n, 2 * n + 1):
                        dst = halves(bank[2 + n])[:, t % 2, :]
                        bias(dst, R_SB + 2 * H)
                        last = mm3(dst, cut(zT2[b % 2], ALL, tok(t)), cut(sw3_2, ALL), False, True)
                    last.then_inc(pe_y, 1)

            pe.wait_ge(w_lo, W_SW3)
            pe.wait_ge(bf_consts, 3)
            pe.wait_ge(parts, 5)
            pe.wait_ge(xnT_ready, 2 * NB + 2)
            ffn_up(0, 0)
            ffn_up(0, 1)
            rows_t(NB + 1, True)
            rows_t(NB + 2, True)
            out_proj(NB - 1, (bank[2], bank[3]))
            up_again(1)
            z_t(0)
            up_again(2)
            ffn_down(0)
            rows_t(NB + 3, True, last_batch=True)
            z_t(1)
            up_again(3)
            ffn_down(1, (0,))
            z_t(2)
            ffn_down(1, (1,))
            ffn_down(2)
            pe.wait_ge(xgn_ready, 1)
            for k in range(KD):
                transposes(xgn, bank[k], k, pe_xgt)
            pe.wait_ge(xg_full, KD)
            pe.wait_ge(in_wg, 16)
            pe.wait_ge(hz_ready, 2 * NB)
            for t in range(MT):
                for k in range(KD):
                    last = pe.matmul(bank[7][:, t * (E + 1):(t + 1) * (E + 1)], full[:, k, t * P:(t + 1) * P],
                                     wg_sb[:, k, :], start=(k == 0), stop=(k == KD - 1))
            last.then_inc(pe_gate, 1)
            z_t(NB - 1)

            def expert_up(t, j):
                if t and j < 2:
                    pe.wait_ge(h_pick, 4 * (t - 1) + 2 * j + 2)
                elif t:
                    pe.wait_ge(h_part, 4 * (t - 1) + 2 * j - 2)
                for k in range(KD):
                    last = mm3(bank[j][:], cut(xgT2, ALL, k, tok(t)), cut(ew2, ALL, k * EP + j), k == 0, k == KD - 1)
                last.then_inc(pe_hm, 1)

            def expert_bias(t):
                if t:
                    pe.wait_ge(ebs_ready, t)
                pe.matmul(bank[7][:], ohT[:, t, :], eb3p[:], start=True, stop=True).then_inc(pe_eb, 1)

            def z_expert_t(t):
                pe.wait_ge(znm_ready, t + 1)
                if t:
                    pe.wait_ge(zm_hi, t)
                else:
                    pe.wait_ge(z_hi, NB)
                pe.transpose(bank[4][:, 0:P], znm[:, t % 2, :], ident_sb[:]).then_inc(pe_ztm, 1)

            def expert_down(t):
                pe.wait_ge(zTm_ready, t + 1)
                for j in range(EP):
                    u = EP * t + j
                    if down_before[u] is not None:
                        before, jb = down_before[u] // EP, down_before[u] % EP
                        if jb < 2:
                            pe.wait_ge(y_pick, 4 * before + 2 * jb + 2)
                        else:
                            pe.wait_ge(y_part, 4 * before + 2 * jb - 2)
                    elif t and j == 0:
                        pe.wait_ge(h_pick, 4 * MT)
                        pe.wait_ge(h_part, 4 * MT)
                    mm3(down_bank[u][:], cut(zTm2, ALL, t % 2), cut(ew2, ALL, KD * EP + j), True, True)\
                        .then_inc(pe_ym, 1)
                    if j == 1 and t + 1 < MT:
                        z_expert_t(t + 1)

            pe.wait_ge(xgT_ready, KD)
            pe.wait_ge(ew_lo, EC)
            for j in range(2):
                expert_up(0, j)
            pe.wait_ge(oh3_ready, 1)
            bank7_bf = bank[7][:].bitcast(BF16)
            for t in range(MT):
                last = pe.transpose(bank7_bf[0:3 * E, t * P:(t + 1) * P], oh3[:, t, :, :].rearrange("p r e -> p (r e)"),
                                    ident_bf[:])
            last.then_inc(pe_oht, 1)
            ffn_down(NB - 1)
            pe.wait_ge(parts, 10)
            pe.wait_ge(ohT_ready, 1)
            expert_bias(0)
            for j in range(2, EP):
                pe.wait_ge(yo_ready, 2 * NB + 1 + j - 2)
                expert_up(0, j)
                expert_bias(j - 1)
            expert_up(1, 0)
            expert_bias(MT - 1)
            for j in range(1, EP):
                expert_up(1, j)
            pe.wait_ge(ebs_ready, MT)
            z_expert_t(0)
            for t in range(MT):
                if t + 2 < MT:
                    for j in range(EP):
                        expert_up(t + 2, j)
                expert_down(t)

        @block.scalar
        def _(act):
            act.sem_inc(sh_ready, 2)
            act.sem_inc(sh_stored, 16)

            def weight_hi(n):
                st, w, s_, v = SPLITS[n]
                act.wait_ge(s_, v)
                act.activation(w[0][:], st, ACT.Copy).then_inc(w_hi, 1)

            def split_evac(dst, m, src, hi_sem, b=None):
                kw = {} if b is None else {"bias": b}
                f = ACT.Copy if b is None else ACT.Identity
                act.activation(dst[0][:, m, :], src[:], f, **kw)
                act.activation(full[:, m, :], src[:], f, **kw).then_inc(hi_sem, 1)

            weight_hi(0)
            for k in range(KD):
                act.wait_ge((in_ctx_a, in_ctx_b)[k], 16)
                act.activation(ctx2[0][:, k, :], ctx_sb[:, k, :], ACT.Copy).then_inc(ctx0_hi, 1)
            for n in range(1, 4):
                weight_hi(n)

            def rows_evac(n, low_taken, total, src=(bank[0], bank[1]), dst=xnT2):
                for k in range(KD):
                    act.wait_ge(pe_xt, 2 * n + 1 + k)
                    act.wait_ge(low_taken, total + k)
                    split_evac(dst, k, src[k], xnT_hi)

            def keys_evac(b, first):
                for m in range(KD):
                    act.wait_ge(pe_k, 2 * b + 1 + m)
                    if not first:
                        act.wait_ge(xnT_ready, 2 * b + 1 + m)
                    split_evac(kT2, m, bank[6 + m], kT_hi, col(C_BK + m))

            def output_hi(b, v_total, between=None):
                act.wait_ge(pe_v, v_total)
                act.sem_inc(act_held, 1)
                for c in range(KD):
                    if c and between is not None:
                        between()
                    act.wait_ge(at_ready, 2 * b + 1 + c)
                    act.activation(aT2[0][:, c, :], at[:, c, :], ACT.Copy).then_inc(aT_hi, 1)

            def expert_hi(b):
                act.wait_ge(in_ew, 16 * b + 16)
                act.sem_inc(act_held, 1)
                for n in range(ECB):
                    act.activation(ew2[0][:, b * ECB + n, :], ew_st[:, n, :], ACT.Copy).then_inc(ew_hi, 1)

            def attention(b, first):
                if first:
                    act.wait_ge(in_rows, 16)
                    act.activation(tanh_g[:], row(R_GX, 2), ACT.Tanh).then_inc(tanh_ready, 1)
                    act.wait_ge(tanh_ready, 1)
                    act.wait_ge(in_cols, 16)
                    keys_evac(b, first)
                    rows_evac(0, kT_ready, 1, (bank[4], bank[5]))
                    for n in range(4, 7):
                        weight_hi(n)
                    act.activation(table[:], tanh_g[:, 0:1], ACT.Sigmoid)
                else:
                    keys_evac(b, first)
                    output_hi(b - 1, 2 * b + 2)
                for m in range(KD):
                    act.wait_ge(pe_q, 2 * b + 1 + m)
                    if first:
                        act.wait_ge(xnT_ready, 1 + m)
                    else:
                        act.wait_ge(kT_ready, 2 * b + 1 + m)
                    split_evac(qT2, m, bank[6 + m], qT_hi, col(C_BQ + m))
                for j in range(2 * T):
                    act.wait_ge(kf_added, 8 * b + j + 1)
                    part = kf[:, j // 2, (j % 2) * 512:(j % 2) * 512 + 512]
                    act.activation(part, part, ACT.Relu).then_inc(kf_ready, 1)
                for p in range(PAIRS):
                    if p == 2:
                        expert_hi(b)
                    if p == 6:
                        act.wait_ge(pe_kv, b + 1)
                        act.activation(kvs[:], quarters(bank[6]), ACT.Copy).then_inc(kvs_ready, 1)
                    act.wait_ge(pe_qf, 8 * b + p + 1)
                    if first and p == 0:
                        act.wait_ge(w_lo, W_SW3)
                    act.activation(qf[:, p, :], bank[2 + p % 4][:], ACT.Relu, bias=col(C_BF)).then_inc(qf_ready, 1)
                rows_evac(b + 1, qT_ready, 2 * b + 1)
                for c in range(KD):
                    act.wait_ge(pe_den, 2 * b + c + 1)
                    if first and c == 0:
                        act.wait_ge(bf_consts, 1)
                    act.activation(at[:, c, :], bank[3 + 2 * c][:], ACT.Identity, bias=att_eps[:]).then_inc(den_ready, 1)

            attention(0, True)
            with act.Fori(1, NB) as b:
                attention(b, False)

            def rows_hi(n):
                for k in range(KD):
                    act.wait_ge(pe_xt, 2 * n + 1 + k)
                    act.activation(ffn_rows2[n - NB][0][:, k, :], bank[k][:], ACT.Copy).then_inc(xnT_hi, 1)

            def gate_sigmoid(b, n, first=False):
                act.wait_ge(pe_h, 2 * b + 1 + n)
                if not first:
                    act.wait_ge(hz_ready, 2 * b)
                act.activation(sg[:, 2 * n:2 * n + 2, :], halves(bank[6 + n])[:, :, 0:H], ACT.Sigmoid).then_inc(sg_ready, 1)

            def z_evac(b):
                act.wait_ge(pe_zt, b + 1)
                act.activation(z_full[b % 2], bank[4][:], ACT.Identity, bias=col(C_SB), scale=col(C_SG))
                act.activation(zT2[b % 2][0], bank[4][:], ACT.Identity, bias=col(C_SB), scale=col(C_SG)).then_inc(z_hi, 1)

            def shared_evac(b, pairs=(0, 1)):
                for n in pairs:
                    act.wait_ge(pe_y, 2 * b + 1 + n)
                    act.wait_ge(sh_stored, 16 * b + 16)
                    act.activation(sh[:, 2 * n:2 * n + 2, :], halves(bank[2 + n]), ACT.Copy).then_inc(sh_ready, 1)

            def first_gates():
                gate_sigmoid(0, 0, True)
                gate_sigmoid(0, 1, True)
                rows_evac(NB + 1, xnT_ready, 2 * NB + 1, dst=kT2)

            output_hi(NB - 1, 2 * NB, first_gates)
            rows_evac(NB + 2, xnT_ready, 2 * NB + 3)
            gate_sigmoid(1, 0)
            gate_sigmoid(1, 1)
            z_evac(0)
            gate_sigmoid(2, 0)
            gate_sigmoid(2, 1)
            rows_hi(NB + 3)
            shared_evac(0)
            z_evac(1)
            gate_sigmoid(3, 0)
            gate_sigmoid(3, 1)
            shared_evac(1, (0,))
            z_evac(2)
            shared_evac(1, (1,))
            shared_evac(NB - 2)
            for k in range(KD):
                act.wait_ge(pe_xgt, k + 1)
                act.activation(full[:, k, :], bank[k][:], ACT.Copy).then_inc(xg_full, 1)
            for k in range(KD):
                act.activation(xgT2[0][:, k, :], bank[k][:], ACT.Copy).then_inc(xgT_hi, 1)
            act.wait_ge(gate_added, 1)
            act.activation(sc[:], lg[:], ACT.Sigmoid).then_inc(sc_ready, 1)
            z_evac(NB - 1)
            act.wait_ge(pe_oht, 1)
            act.activation(ohT[:], bank[7][:].bitcast(BF16)[0:3 * E, 0:MT * P].rearrange("p (t q) -> p t q", t=MT),
                           ACT.Copy).then_inc(ohT_ready, 1)
            act.wait_ge(dif_ready, 1)
            act.activation(swt[:, 0, :], dif[:], ACT.Sigmoid).then_inc(swt_ready, 1)
            act.activation(swt[:, 1, :], dif[:], ACT.Sigmoid, scale=-1.0).then_inc(swt_ready, 1)
            shared_evac(NB - 1)

            def pick(t, banks, made, dst, free, done):
                if t >= 2:
                    act.wait_ge(free, t - 1)
                for j in range(2):
                    act.wait_ge(made, EP * t + j + 1)
                    for par in range(2):
                        act.activation(dst[t % 2][:, 2 * j + par, :], halves(banks(j))[:, par, :], ACT.Copy,
                                       scale=oh[:, t, 2 * j + par:2 * j + par + 1]).then_inc(done, 1)

            def pick_hidden(t):
                pick(t, lambda j: bank[j], pe_hm, part_h, hs_ready, h_pick)

            def pick_down(t):
                pick(t, lambda j: down_bank[EP * t + j], pe_ym, part_y, fin_ready, y_pick)

            def expert_bias(t):
                act.wait_ge(pe_eb, t + 1)
                act.activation(ebs[:, t, :], bank[7][:], ACT.Copy).then_inc(ebs_ready, 1)

            def expert_gate(t):
                act.wait_ge(hs_ready, t + 1)
                act.activation(sgm[:, t % 2, :], acc_h[:, 2 * (t % 2), 0:H], ACT.Sigmoid).then_inc(sgm_ready, 1)

            def expert_z(t):
                act.wait_ge(pe_ztm, t + 1)
                if t >= 2:
                    act.wait_ge(zTm_ready, t - 1)
                    act.wait_ge(pe_ym, EP * (t - 1))
                act.activation(zfm[:, t % 2, :], bank[4][:, 0:P], ACT.Identity, bias=col(C_EB), scale=col(C_EG))
                act.activation(zTm2[0][:, t % 2, :], bank[4][:, 0:P], ACT.Identity, bias=col(C_EB), scale=col(C_EG))\
                   .then_inc(zm_hi, 1)

            expert_bias(0)
            act.wait_ge(oh_ready, 1)
            pick_hidden(0)
            for t in range(1, MT):
                expert_bias(t)
            expert_gate(0)
            pick_hidden(1)
            expert_z(0)
            for t in range(1, MT):
                expert_gate(t)
                if t + 1 < MT:
                    pick_hidden(t + 1)
                pick_down(t - 1)
                expert_z(t)
            pick_down(MT - 1)

        @block.vector
        def _(dve):
            def low(dst, whole, hi, done):
                return dve.tensor_tensor(dst, whole, hi.bitcast(F32), ALU.subtract).then_inc(done, 1)

            def stats(src, st, mv, n, st_sem, mv_sem, total, by_register):
                for t in range(n):
                    last = dve.bn_stats(st[:, t, :], src(t))
                last.then_inc(st_sem, 1)
                aggregate(st, mv, n, st_sem, mv_sem, total, total, by_register)

            def aggregate(st, mv, n, st_sem, mv_sem, st_total, mv_total, by_register):
                dve.wait_ge(st_sem, st_total)
                if by_register:
                    dve.sem_inc(held, 1)
                for t in range(n):
                    last = dve.bn_aggr(mv[:, t, :], st[:, t, :])
                last.then_inc(mv_sem, 1)
                dve.wait_ge(mv_sem, mv_total)

            def weight_lo(n):
                st, w, s_, v = SPLITS[n]
                dve.wait_ge(w_hi, n + 1)
                low(w[1][:], st, w[0][:], w_lo)

            def x_stats(b):
                stats(lambda t: xs[:, T * b + t, :], st1[:, T * b:T * b + T, :], mv1[:, T * b:T * b + T, :], T,
                      st1_ready, mv1_ready, b + 1, False)
                dve.tensor_scalar(ve[:, T * b:T * b + T], mv1[:, T * b:T * b + T, 1], LN_EPS, None, ALU.add)\
                   .then_inc(ve_ready, 1)
                dve.tensor_scalar(nm[:, T * b:T * b + T], mv1[:, T * b:T * b + T, 0], -1.0, None, ALU.mult)\
                   .then_inc(ve_ready, 1)

            def bf16_parts(whole, dst, m1, m2, count):
                for n, m in enumerate((m1, m2)):
                    dve.tensor_copy(dst, whole).then_inc(parts, 1)
                    dve.wait_ge(parts, count + 2 * n + 1)
                    dve.scalar_tensor_tensor(whole, dst, m, whole, ALU.mult, ALU.add).then_inc(parts, 1)
                    dve.wait_ge(parts, count + 2 * n + 2)
                dve.tensor_copy(dst, whole).then_inc(parts, 1)

            dve.sem_inc(yo_ready, 2)
            dve.sem_inc(out_stored, 16)
            dve.memset(neg_half[:], -0.5).then_inc(consts_ready, 1)
            dve.memset(ones_sb[:], 1.0).then_inc(consts_ready, 1)
            dve.memset(kvd[:], 0.0).then_inc(kvd_zero, 1)
            dve.memset(att_eps[:], ATT_EPS).then_inc(bf_consts, 1)

            step = [0]

            def link(sem_, ins):
                step[0] += 1
                ins.then_inc(sem_, 1)
                dve.wait_ge(sem_, step[0])

            weight_lo(0)
            for k in range(KD):
                dve.wait_ge(ctx0_hi, k + 1)
                low(ctx2[1][:, k, :], ctx_sb[:, k, :], ctx2[0][:, k, :], ctx_ready)
            dve.wait_ge(in_x0, 16)
            x_stats(0)
            for n in range(1, 4):
                weight_lo(n)
            dve.wait_ge(in_id, 16)
            dve.tensor_copy(ident_bf[:], ident_sb[:]).then_inc(bf_consts, 1)
            dve.wait_ge(in_pm, 16)
            dve.tensor_copy(ones3[:], pm_sb[:, 0:1].to_broadcast([P, P])).then_inc(bf_consts, 1)
            dve.wait_ge(in_moe, 64)
            bf16_parts(row2(R_SB, 2 * H + D), bias3[:], pm_sb[:, 1:2], pm_sb[:, 2:3], 0)

            for n in range(4, 7):
                weight_lo(n)
            bf16_parts(eb_st[:], eb3p[:], pm_sb[0:3 * E, 3:4], pm_sb[0:3 * E, 4:5], 5)
            dve.wait_ge(tanh_ready, 1)
            dve.tensor_scalar(tbo[:], row(R_BO, D), tanh_g[:, 0:1], None, ALU.mult).then_inc(tbo_ready, 1)
            dve.wait_ge(in_rows, 16)
            dve.wait_ge(kvd_zero, 1)

            def output_lo(b):
                for c in range(KD):
                    dve.wait_ge(aT_hi, 2 * b + c + 1)
                    low(aT2[1][:, c, :], at[:, c, :], aT2[0][:, c, :], aT_ready)

            def residual(b, srcs):
                for n, src in enumerate(srcs):
                    dve.wait_ge(xb_ready, b + 1)
                    dve.wait_ge(pe_wo, 2 * b + 1 + n)
                    rows = bass.ds(b * T + 2 * n, 2)
                    dve.scalar_tensor_tensor(x1[:, rows, :], halves(src), tanh_g[:, 0:1], xs[:, rows, :], ALU.mult, ALU.add)\
                       .then_inc(x1_ready, 1)

            def x1_stats(b):
                dve.wait_ge(x1_ready, 2 * b + 2)
                dve.sem_inc(held, 1)
                stats(lambda t: x1[:, b * T + t, :], st2, mv2, T, st2_ready, mv2_ready, b + 1, True)
                rows = bass.ds(b * T + NB * T, T)
                dve.tensor_scalar(ve[:, rows], mv2[:, :, 1], LN_EPS, None, ALU.add).then_inc(ve_ready, 1)
                dve.tensor_scalar(nm[:, rows], mv2[:, :, 0], -1.0, None, ALU.mult).then_inc(ve_ready, 1)
                dve.wait_ge(ve_ready, 2 * b + 2 * NB + 2)

            def index_rows():
                dve.wait_ge(in_idx, 16)
                for n, size in ((0, NB), (1, S)):
                    v, neg = idf[:, n, :], idf[:, 2 + n, :]
                    link(idx_step, dve.tensor_copy(v, idx_i[:, n, :]))
                    link(idx_step, dve.tensor_scalar(neg, v, 0.0, float(size), ALU.is_lt, ALU.mult))
                    link(idx_step, dve.tensor_tensor(v, v, neg, ALU.add))
                    link(idx_step, dve.tensor_scalar(neg, v, 0.0, None, ALU.is_ge))
                    link(idx_step, dve.scalar_tensor_tensor(idf[:, 4 + n, :], v, float(size - 1), neg, ALU.is_le, ALU.mult))
                    link(idx_step, dve.tensor_scalar(v, v, 0.0, float(size - 1), ALU.max, ALU.min))
                link(idx_step, dve.scalar_tensor_tensor(idf[:, 6, :], idf[:, 0, :], float(S), idf[:, 1, :], ALU.mult, ALU.add))
                link(idx_step, dve.tensor_copy(gidx[:], idf[:, 6, :]))
                link(idx_step, dve.tensor_tensor(idf[:, 7, :], idf[:, 4, :], idf[:, 5, :], ALU.mult))
                link(idx_step, dve.tensor_scalar(idf[:, 7, :], idf[:, 7, :], -float(N), float(N), ALU.mult, ALU.add))
                link(idx_step, dve.tensor_tensor(idf[:, 6, :], idf[:, 6, :], idf[:, 7, :], ALU.add))
                dve.tensor_copy(sidx[:], idf[:, 6, :]).then_inc(idx_ready, 1)
                for e in range(E):
                    dve.memset(rank_w[:, :, e], float(E - e)).then_inc(rank_ready, 1)

            def attention(b, first):
                for n in range(2):
                    dve.wait_ge(pe_v, 2 * b + 1 + n)
                    dve.tensor_tensor(vv[:, 2 * n:2 * n + 2, :], halves(bank[n]), bc(row(R_BV, D), 2), ALU.add)\
                       .then_inc(v_ready, 1)
                if not first:
                    output_lo(b - 1)
                for j in range(2 * T):
                    if not first and j == 2:
                        residual(b - 1, (bank[0], bank[1]))
                    dve.wait_ge(pe_kf, 8 * b + j + 1)
                    dve.tensor_tensor(kf[:, j // 2, (j % 2) * 512:(j % 2) * 512 + 512].rearrange("p (h f) -> p h f", f=FD),
                                      bank[2 + j % 4][:].rearrange("p (h f) -> p h f", f=FD), bc(row(R_BF, FD), 8),
                                      ALU.add).then_inc(kf_added, 1)
                if first:
                    dve.wait_ge(in_x, 16)
                    for n in range(1, NB):
                        x_stats(n)
                else:
                    x1_stats(b - 1)
                for n in range(ECB):
                    dve.wait_ge(ew_hi, b * ECB + n + 1)
                    low(ew2[1][:, b * ECB + n, :], ew_st[:, n, :], ew2[0][:, b * ECB + n, :], ew_lo)
                dve.wait_ge(pe_kvt, b + 1)
                src = bank[6][:].rearrange("p (n g d) -> p (n g) d", n=2 * KD, g=PG)
                dst = kvd[:].rearrange("p n g d -> p (n g) d")
                for a in range(2):
                    dve.tensor_copy(dst[64 * a:64 * a + 64, :, HD * a:HD * a + HD],
                                    src[64 * a:64 * a + 64, :, HD * a:HD * a + HD]).then_inc(kvd_ready, 1)
                if first:
                    index_rows()
                for c in range(KD):
                    dve.wait_ge(den_ready, 2 * b + c + 1)
                    dve.reciprocal(at[:, c, :], at[:, c, :]).then_inc(rden_ready, 1)
                    dve.wait_ge(rden_ready, 2 * b + c + 1)
                    dve.wait_ge(pe_num, 2 * b + c + 1)
                    dve.tensor_tensor(at[:, c, :], bank[2 + 2 * c][:], at[:, c, :], ALU.mult).then_inc(at_ready, 1)

            attention(0, True)
            with dve.Fori(1, NB) as b:
                attention(b, False)
            output_lo(NB - 1)

            def swiglu(b):
                for n in range(2):
                    two = slice(2 * n, 2 * n + 2)
                    dve.wait_ge(sg_ready, 2 * b + 1 + n)
                    dve.tensor_tensor(hu[:, two, :], halves(bank[6 + n])[:, :, 0:H], sg[:, two, :], ALU.mult)\
                       .then_inc(hu_ready, 1)
                    dve.wait_ge(hu_ready, 2 * b + 1 + n)
                    dve.tensor_tensor(hz[:, two, :], halves(bank[6 + n])[:, :, H:2 * H], hu[:, two, :], ALU.mult)\
                       .then_inc(hz_ready, 1)

            def swiglu_stats(b):
                dve.wait_ge(hz_ready, 2 * b + 2)
                dve.sem_inc(held, 1)
                stats(lambda t: hz[:, t, :], st3, mv3, T, st3_ready, mv3_ready, b + 1, True)
                dve.tensor_scalar(ve3[:], mv3[:, :, 1], LN_EPS, None, ALU.add).then_inc(ve3_ready, 1)
                dve.tensor_scalar(nm3[:], mv3[:, :, 0], -1.0, None, ALU.mult).then_inc(ve3_ready, 1)

            def swiglu_norm(b, first):
                dve.wait_ge(rs3_ready, b + 1)
                dve.wait_ge(ve3_ready, 2 * b + 2)
                if not first:
                    dve.wait_ge(pe_zt, b)
                for t in range(T):
                    dve.tensor_scalar(zn[:, t, :], hz[:, t, :], nm3[:, t:t + 1], rs3[:, t:t + 1], ALU.add, ALU.mult)\
                       .then_inc(zn_ready, 1)

            def last_rows():
                dve.wait_ge(cur_ready, 4 * NB)
                dve.wait_ge(pe_xt, 4 * NB - 2)
                for t in range(T):
                    dve.tensor_scalar(xn[:, t, :], x1[:, (NB - 1) * T + t, :], nm_cur[:, t:t + 1], rs_cur[:, t:t + 1],
                                      ALU.add, ALU.mult).then_inc(last_xn_ready, 1)

            def rows_lo(n):
                for k in range(KD):
                    dve.wait_ge(xnT_hi, 2 * n + 1 + k)
                    rows2 = ffn_rows2[n - NB]
                    low(rows2[1][:, k, :], bank[k][:], rows2[0][:, k, :], rows_lo_ready)

            def shared_out(b, pairs=(0, 1)):
                for n in pairs:
                    dve.wait_ge(sh_ready, 2 * b + 3 + n)
                    dve.wait_ge(out_stored, 16 * b + 16)
                    dve.scalar_tensor_tensor(yo[:, 2 * n:2 * n + 2, :], halves(bank[2 + n]), tanh_g[:, 1:2],
                                             x1[:, bass.ds(b * T + 2 * n, 2), :], ALU.mult, ALU.add).then_inc(yo_ready, 1)

            swiglu(0)
            swiglu_stats(0)
            residual(NB - 1, (bank[2], bank[3]))
            swiglu_norm(0, True)
            swiglu(1)
            x1_stats(NB - 1)
            swiglu_stats(1)
            last_rows()
            swiglu_norm(1, False)
            rows_lo(NB + 3)
            swiglu(2)
            shared_out(0)
            swiglu_stats(2)
            swiglu_norm(2, False)
            swiglu(3)
            shared_out(1, (0,))
            step[0] = 0
            dve.wait_ge(xg_in, 16 * MT)
            for t in range(MT):
                last = dve.bn_stats(stg[:, t, :], xg[:, t, :])
            link(dve_g, last)
            for t in range(MT):
                last = dve.bn_aggr(mvg[:, t, :], stg[:, t, :])
            link(dve_g, last)
            link(dve_g, dve.tensor_scalar(veg[:], mvg[:, :, 1], LN_EPS, None, ALU.add))
            link(dve_g, dve.tensor_scalar(nmg[:], mvg[:, :, 0], -1.0, None, ALU.mult))
            shared_out(1, (1,))
            dve.wait_ge(rsg_ready, 1)
            for t in range(MT):
                last = dve.tensor_scalar(xgn[:, t, :], xg[:, t, :], nmg[:, t:t + 1], rsg[:, t:t + 1], ALU.add, ALU.mult)
            last.then_inc(xgn_ready, 1)
            swiglu_stats(NB - 1)
            for k in range(KD):
                dve.wait_ge(xg_full, k + 1)
                dve.wait_ge(xgT_hi, k + 1)
                low(xgT2[1][:, k, :], full[:, k, :], xgT2[0][:, k, :], xgT_ready)
            swiglu_norm(NB - 1, False)
            dve.wait_ge(pe_gate, 1)
            dve.tensor_tensor(lg[:], bank[7][:, 0:MT * (E + 1)].rearrange("p (t e) -> p t e", t=MT),
                              bc(row2(R_GB, E + 1), MT), ALU.add).then_inc(gate_added, 1)
            shared_out(NB - 2, (0,))
            step[0] = 0
            dve.wait_ge(sc_ready, 1)
            dve.wait_ge(rank_ready, E)
            link(route_step, dve.tensor_tensor(sx[:], sc[:, :, 0:E], bc(row2(R_XB, E), MT), ALU.add))
            link(route_step, dve.reduce_max(mx[:], sx[:], AX_X))
            link(route_step, dve.tensor_tensor(eq[:], sx[:], bcl(mx[:], E), ALU.is_equal))
            link(route_step, dve.tensor_tensor(eq[:], eq[:], rank_w[:], ALU.mult))
            link(route_step, dve.reduce_max(m2[:], eq[:], AX_X))
            dve.tensor_tensor(oh[:], eq[:], bcl(m2[:], E), ALU.is_equal).then_inc(oh_ready, 1)
            dve.wait_ge(oh_ready, 1)
            for r in range(3):
                last = dve.tensor_copy(oh3[:, :, r, :], oh[:])
            last.then_inc(oh3_ready, 1)
            link(route_step, dve.tensor_tensor(sx[:], sc[:, :, 0:E], oh[:], ALU.mult))
            link(route_step, dve.reduce_sum(top[:], sx[:], AX_X))
            dve.tensor_tensor(dif[:], top[:], sc[:, :, E], ALU.subtract).then_inc(dif_ready, 1)
            shared_out(NB - 2, (1,))
            shared_out(NB - 1)
            dve.wait_ge(swt_ready, 2)
            dve.tensor_scalar(cw[:], swt[:], tanh_g[:, 1:2], None, ALU.mult).then_inc(cw_ready, 1)

            def select(t, banks, made, start, acc, done, rest, rest_half, total_sem):
                for j in (2, 3):
                    dve.wait_ge(made, EP * t + j + 1)
                    for par in range(2):
                        src, slot = halves(banks(j))[:, par, :], acc[:, 2 * (t % 2) + par, :]
                        w = oh[:, t, 2 * j + par:2 * j + par + 1]
                        if j == 3:
                            dve.wait_ge(done, 4 * t + par + 1)
                            ins = dve.scalar_tensor_tensor(slot, src, w, slot, ALU.mult, ALU.add)
                        elif par:
                            ins = dve.tensor_scalar(slot, src, w, None, ALU.mult)
                        else:
                            ins = dve.scalar_tensor_tensor(slot, src, w, start, ALU.mult, ALU.add)
                        ins.then_inc(done, 1)
                dve.wait_ge(done, 4 * t + 4)
                even, odd = acc[:, 2 * (t % 2), :], acc[:, 2 * (t % 2) + 1, :]
                dve.tensor_tensor(odd, even, odd, ALU.add).then_inc(total_sem, 1)
                dve.wait_ge(total_sem, t + 1)
                dve.wait_ge(rest_half, t + 1)
                return dve.tensor_tensor(even, odd, rest[t % 2][:, 0, :], ALU.add)

            step[0] = 0

            def expert_hidden(t):
                i, even = t % 2, acc_h[:, 2 * (t % 2), :]
                dve.wait_ge(ebs_ready, t + 1)
                select(t, lambda j: bank[j], pe_hm, ebs[:, t, 0:2 * H], acc_h, h_part, part_h, h_half, h_sum)\
                    .then_inc(hs_ready, 1)
                dve.wait_ge(hs_ready, t + 1)
                dve.wait_ge(sgm_ready, t + 1)
                link(dve_m, dve.tensor_tensor(hum[:, i, :], even[:, 0:H], sgm[:, i, :], ALU.mult))
                link(dve_m, dve.tensor_tensor(hzm[:, i, :], even[:, H:2 * H], hum[:, i, :], ALU.mult))
                link(dve_m, dve.bn_stats(stm[:, t, :], hzm[:, i, :]))
                link(dve_m, dve.bn_aggr(mvm[:, t, :], stm[:, t, :]))
                dve.tensor_scalar(vem[:, t:t + 1], mvm[:, t, 1:2], LN_EPS, None, ALU.add).then_inc(ve_m_ready, 1)
                link(dve_m, dve.tensor_scalar(nmm[:, t:t + 1], mvm[:, t, 0:1], -1.0, None, ALU.mult))

            def expert_norm(t):
                i = t % 2
                dve.wait_ge(rsm_ready, t + 1)
                if t >= 2:
                    dve.wait_ge(pe_ztm, t - 1)
                dve.tensor_scalar(znm[:, i, :], hzm[:, i, :], nmm[:, t:t + 1], rsm[:, t:t + 1], ALU.add, ALU.mult)\
                   .then_inc(znm_ready, 1)

            def combine(t):
                select(t, lambda j: down_bank[EP * t + j], pe_ym, ebs[:, t, 2 * H:2 * H + D], acc_y, y_part,
                       part_y, y_half, y_sum).then_inc(f_step, 1)
                dve.wait_ge(f_step, t + 1)
                dve.wait_ge(base_ready, t + 1)
                dve.scalar_tensor_tensor(fin[:, t, :], acc_y[:, 2 * (t % 2), :], cw[:, 0, t:t + 1], base[:, t, :],
                                         ALU.mult, ALU.add).then_inc(fin_ready, 1)

            for t in range(MT):
                expert_hidden(t)
                if t == 2:
                    combine(0)
                expert_norm(t)
            combine(1)
            combine(MT - 2)
            combine(MT - 1)

        @block.gpsimd
        def _(pool):
            pool.dma_start(idx_i[:], index).then_inc(in_idx, 16)
            pool.dma_start(cols_sb[:], cols).then_inc(in_cols, 16)
            pool.dma_start(ident_sb[:], ident).then_inc(in_id, 16)
            pool.dma_start(pm_sb[:], part_mask).then_inc(in_pm, 16)

            def norm_prepare(n):
                pool.wait_ge(ve_ready, 2 * n + 2)
                pool.sem_inc(pool_held, 1)
                rows = bass.ds(n * T, T)
                pool.tensor_tensor(rs_cur[:], ve[:, rows], neg_half[:, 0:T], ALU.pow).then_inc(cur_ready, 1)
                pool.tensor_tensor(nm_cur[:], nm[:, rows], ones_sb[:, 0:T], ALU.mult).then_inc(cur_ready, 1)

            def norm_rows(n, src):
                pool.wait_ge(cur_ready, 2 * n + 2)
                if src is x_cur:
                    pool.wait_ge(x_cur_in, 16 * n)
                if src is not xs:
                    pool.wait_ge(pe_xt, 2 * n)
                pool.sem_inc(pool_held, 1)
                for t in range(T):
                    pool.tensor_scalar(xn[:, t, :], src[:, t, :], nm_cur[:, t:t + 1], rs_cur[:, t:t + 1],
                                       ALU.add, ALU.mult).then_inc(xn_ready, 1)
                pool.wait_ge(xn_ready, 4 * n + 4)
                pool.sem_inc(pool_held, 1)

            def low(pair, m, b, hi_sem, done):
                pool.wait_ge(hi_sem, 2 * b + 1 + m)
                pool.tensor_tensor(pair[1][:, m, :], full[:, m, :], pair[0][:, m, :].bitcast(F32), ALU.subtract)\
                    .then_inc(done, 1)

            def attention(b, first):
                if first:
                    pool.wait_ge(consts_ready, 2)
                    norm_prepare(0)
                    norm_rows(0, xs)
                else:
                    pool.wait_ge(in_ctx, 16 * b)
                    pool.wait_ge(pe_kf, 8 * b - 7)
                    pool.sem_inc(pool_held, 1)
                    pool.tensor_scalar(ctx2[0][:], ctx_sb[:], 1.0, 0.0, ALU.mult, ALU.add).then_inc(ctx_hi, 1)
                    pool.wait_ge(ctx_hi, b)
                    pool.tensor_tensor(ctx2[1][:], ctx_sb[:], ctx2[0][:].bitcast(F32), ALU.subtract).then_inc(ctx_ready, 1)
                order = ((kT2, kT_hi, kT_ready), (xnT2, xnT_hi, xnT_ready))
                rows = bass.ds(b * T, T)
                for pair, hi_sem, done in (*(order if first else order[::-1]), (qT2, qT_hi, qT_ready)):
                    if first and pair is qT2:
                        pool.wait_ge(tbo_ready, 1)
                        pool.tensor_tensor(xs[:, rows, :], xs[:, rows, :], bc(tbo[:], T), ALU.add).then_inc(xb_ready, 1)
                    for m in range(KD):
                        low(pair, m, b, hi_sem, done)
                if not first:
                    pool.tensor_tensor(xs[:, rows, :], xs[:, rows, :], bc(tbo[:], T), ALU.add).then_inc(xb_ready, 1)
                    norm_prepare(b + 1)
                pool.wait_ge(kf_ready, 8 * b + 4)
                pool.tensor_tensor(kf_sum[:], kf[:, 0, :], kf[:, 1, :], ALU.add).then_inc(kfs_part, 1)
                for t in (2, 3):
                    pool.wait_ge(kfs_part, 2 * b + t - 1)
                    pool.wait_ge(kf_ready, 8 * b + 2 * t + 2)
                    pool.tensor_tensor(kf_sum[:], kf_sum[:], kf[:, t, :], ALU.add)\
                        .then_inc(kfs_part if t == 2 else kfs_ready, 1)
                if first:
                    norm_prepare(1)
                norm_rows(b + 1, x_cur)

            attention(0, True)
            with pool.Fori(1, NB) as b:
                attention(b, False)

            def rs3_pow(b):
                pool.wait_ge(ve3_ready, 2 * b + 2)
                pool.tensor_tensor(rs3[:], ve3[:], neg_half[:, 0:T], ALU.pow).then_inc(rs3_ready, 1)

            def z_low(b):
                pool.wait_ge(z_hi, b + 1)
                pool.tensor_tensor(zT2[b % 2][1], z_full[b % 2], zT2[b % 2][0].bitcast(F32), ALU.subtract).then_inc(zT_ready, 1)

            def rows_low(n):
                for m in range(KD):
                    low(ffn_rows2[n - NB], m, n, xnT_hi, xnT_ready)

            def gather_x1(t):
                pool.indirect_dma_start(xg[:, t, :], None, scratch_x1, bass.IndirectOffsetOnAxis(ap=gidx[:, t:t + 1], axis=0))\
                    .then_inc(xg_in, 16)

            def norm_x1(n):
                norm_rows(n, x1[:, (n - NB) * T:(n - NB) * T + T, :])

            rows_low(NB)
            for n in (NB + 1, NB + 2):
                norm_prepare(n)
                norm_x1(n)
            rows_low(NB + 1)
            rows_low(NB + 2)
            rs3_pow(0)
            z_low(0)
            norm_prepare(NB + 3)
            rs3_pow(1)
            pool.wait_ge(x1_stored, 16 * NB)
            pool.wait_ge(idx_ready, 1)
            gather_x1(0)
            gather_x1(1)
            z_low(1)
            gather_x1(2)
            gather_x1(3)
            rs3_pow(2)
            z_low(2)
            pool.wait_ge(dve_g, 3)
            pool.tensor_tensor(rsg[:], veg[:], neg_half[:, 0:MT], ALU.pow).then_inc(rsg_ready, 1)
            rs3_pow(3)
            z_low(3)

            def expert_scale(t):
                pool.wait_ge(ve_m_ready, t + 1)
                pool.tensor_tensor(rsm[:, t:t + 1], vem[:, t:t + 1], neg_half[:, 0:1], ALU.pow).then_inc(rsm_ready, 1)

            def z_expert_low(t):
                pool.wait_ge(zm_hi, t + 1)
                pool.tensor_tensor(zTm2[1][:, t % 2, :], zfm[:, t % 2, :], zTm2[0][:, t % 2, :].bitcast(F32),
                                   ALU.subtract).then_inc(zTm_ready, 1)

            def half(t, part, picked, two, done):
                rows = part[t % 2]
                pool.wait_ge(picked, 4 * t + 4)
                pool.tensor_tensor(rows[:, 0:2, :], rows[:, 0:2, :], rows[:, 2:4, :], ALU.add).then_inc(two, 1)
                pool.wait_ge(two, t + 1)
                pool.tensor_tensor(rows[:, 0, :], rows[:, 0, :], rows[:, 1, :], ALU.add).then_inc(done, 1)

            def half_hidden(t):
                half(t, part_h, h_pick, h_two, h_half)

            def half_down(t):
                half(t, part_y, y_pick, y_two, y_half)

            def base_rows(t):
                if t == 0:
                    pool.wait_ge(cw_ready, 1)
                    pool.wait_ge(shg_in, 16 * MT)
                pool.tensor_scalar(base[:, t, :], shg[:, t, :], cw[:, 1, t:t + 1], 0.0, ALU.mult, ALU.add)\
                    .then_inc(base_step, 1)
                pool.wait_ge(base_step, t + 1)
                pool.tensor_tensor(base[:, t, :], base[:, t, :], xg[:, t, :], ALU.add).then_inc(base_ready, 1)

            def scatter(t):
                pool.wait_ge(fin_ready, t + 1)
                if t == 0:
                    pool.wait_ge(out_stored, 16 * NB + 16)
                pool.indirect_dma_start(out, bass.IndirectOffsetOnAxis(ap=sidx[:, t:t + 1], axis=0), fin[:, t, :], None,
                                        bounds_check=N - 1, oob_is_err=False).then_inc(scattered, 16)

            def gather_shared(t):
                pool.indirect_dma_start(shg[:, t, :], None, scratch_sh, bass.IndirectOffsetOnAxis(ap=gidx[:, t:t + 1], axis=0))\
                    .then_inc(shg_in, 16)

            half_hidden(0)
            pool.wait_ge(sh_stored, 16 * NB + 16)
            gather_shared(0)
            gather_shared(1)
            expert_scale(0)
            half_hidden(1)
            z_expert_low(0)
            gather_shared(2)
            gather_shared(3)
            expert_scale(1)
            half_hidden(2)
            base_rows(0)
            z_expert_low(1)
            half_down(0)
            expert_scale(2)
            half_hidden(3)
            base_rows(1)
            scatter(0)
            z_expert_low(2)
            base_rows(2)
            expert_scale(3)
            half_down(1)
            z_expert_low(3)
            half_down(2)
            base_rows(3)
            scatter(1)
            half_down(3)
            scatter(2)
            scatter(3)
            pool.wait_ge(scattered, 16 * MT)


def kernel(**inputs):
    import numpy as np
    import concourse.bacc as bacc
    from concourse.bass_utils import run_bass_kernel_spmd as run

    a = {k.replace("L0_xattn_", "").replace("L0_ffn_", ""): np.asarray(v) for k, v in inputs.items()}
    f32 = np.float32
    NB, S, D = a["x"].shape
    HD, FD = a["Wf"].shape
    E, H = a["eb1"].shape
    M = a["index_b"].shape[0]
    wf = np.zeros((P, 8 * FD), f32)
    for h in range(8):
        wf[HD * h:HD * h + HD, FD * h:FD * h + FD] = a["Wf"]
    rows_a = np.concatenate([a["bv"], a["bf"], a["bo"], a["g_xattn"], a["g_ffn"]])[None, :]
    rows_b = np.concatenate([a["sb1"], a["sb2"], a["sb3"], a["eg_b"], a["sg_b"], a["exp_bias"]])[None, :]
    cols = np.stack([a["bq"][:P], a["bq"][P:], a["bk"][:P], a["bk"][P:], np.tile(a["bf"], 2), a["s_ln_g"],
                     a["s_ln_b"], a["sel_ln_g"], a["sel_ln_b"]], axis=1)
    up = np.concatenate([a["ew1"], a["ew2"]], axis=1).transpose(2, 0, 1).reshape(2, P, E // 2, 4 * H)
    up = up.transpose(1, 0, 2, 3).reshape(P, E, 4 * H)
    down = a["ew3"].transpose(2, 0, 1).reshape(P, E // 2, 2 * D)
    part = np.arange(P)
    part_mask = np.stack([part < 3, -1 * (part >= 1), -1 * (part >= 2), -1 * (part >= E), -1 * (part >= 2 * E)],
                         axis=1).astype(f32)
    arrays = {
        "x": a["x"].reshape(NB * S, D),
        "ctx_t": a["ctx_1024"].reshape(NB * S, D).T,
        "w_q": a["Wq"], "w_k": a["Wk"], "w_v": a["Wv"], "w_o": a["Wo"], "w_f_diag": wf, "rows_a": rows_a, "rows_b": rows_b,
        "cols": cols,
        "sw12": np.concatenate([a["sw1"].T, a["sw2"].T], axis=1),
        "sw3": a["sw3"].T,
        "w_gate": np.concatenate([a["eg_w"], a["sg_w"]], axis=0).T,
        "ew": np.concatenate([up, down], axis=1),
        "eb": np.concatenate([a["eb1"], a["eb2"], a["eb3"]], axis=1),
        "index": np.stack([a["index_b"].reshape(M // P, P).T, a["index_t"].reshape(M // P, P).T], axis=1),
        "ident": np.eye(P, dtype=f32),
        "part_mask": part_mask,
    }
    arrays = {f"in_{k}": np.ascontiguousarray(v) for k, v in arrays.items()}
    nc = bacc.Bacc("TRN2", target_bir_lowering=False, num_devices=1)
    args = [nc.dram_tensor(k, v.shape, mybir.dt.from_np(v.dtype), kind="ExternalInput").ap() for k, v in arrays.items()]
    out = nc.dram_tensor("out", (NB * S, D), F32, kind="ExternalOutput").ap()
    flamingo_block(nc, *args, out)
    r = run(nc, [arrays], core_ids=[0])
    return r.results[0]["out"].reshape(NB, S, D)
```
